# Optimizing a Trainium2 kernel written in Bass

```python
import numpy as np
import jax
import jax.numpy as jnp

def _softmax(x, axis=-1):
    return jax.nn.softmax(x, axis=axis)

def _gelu(x):
    return jax.nn.gelu(x, approximate=True)

def _silu(x):
    return jax.nn.silu(x)

def _sigmoid(x):
    return jax.nn.sigmoid(x)

def _layernorm(x, axis=-1, eps=1e-05):
    m = jnp.mean(x, axis=axis, keepdims=True)
    v = jnp.var(x, axis=axis, keepdims=True)
    return (x - m) / jnp.sqrt(v + eps)

def _scatter_add(tgt, idx, src, axis=0):
    return tgt.at[idx].add(src)

def _segment_sum(src, seg, n):
    return jax.ops.segment_sum(src, seg, n)
kernel_name = 'mk_decoder_preln_d2_seqx_r8_762419'

def setup_inputs(seed: int=0):
    np.random.seed(seed)
    _w = jnp.asarray

    def _rec_inputs():
        import jax
        import jax.numpy as jnp
        _rk = jax.random.key(seed)
        x = 0.0002417 + 0.9998 * jax.random.normal(jax.random.fold_in(_rk, 1), (4, 512, 128), jnp.float32)
        _lenS = 512 - jax.random.randint(jax.random.fold_in(_rk, 7), (4,), 0, max(1, 512 // 4) + 1, jnp.int32)
        _lenS2 = 77 - jax.random.randint(jax.random.fold_in(_rk, 8), (4,), 0, max(1, 77 // 4) + 1, jnp.int32)
        _ctx_1024P = jax.random.normal(jax.random.fold_in(_rk, 11), (4, 16, 128), jnp.float32)
        _ctx_1024c = jax.random.dirichlet(jax.random.fold_in(_rk, 511), 0.3 * jnp.ones((16,), jnp.float32), (4, 77))
        _ctx_1024t = jnp.einsum('bsk,bkd->bsd', _ctx_1024c, _ctx_1024P)
        _ctx_1024t = _ctx_1024t * jax.lax.rsqrt(jnp.mean(jnp.square(_ctx_1024t)) + 1e-12) * 0.953939
        ctx_1024 = 7.22013e-05 + 1.00017 * (_ctx_1024t + 0.3 * jax.random.normal(jax.random.fold_in(_rk, 611), (4, 77, 128), jnp.float32))
        _validS = jnp.arange(512)[None, :] < _lenS[:, None]
        _validS2 = jnp.arange(77)[None, :] < _lenS2[:, None]
        _causal = jnp.tril(jnp.ones((512, 512), dtype=bool))
        mask_1x1xSxS2_ik0 = jnp.where(jnp.broadcast_to(_validS2[0:1, None, None, :], (1, 1, 512, 77)), 0, 1).astype(jnp.int32)
        return (x, ctx_1024, mask_1x1xSxS2_ik0)
    x, ctx_1024, mask_1x1xSxS2_ik0 = _rec_inputs()

    def _L0_attn_setup():
        import jax, jax.numpy as jnp
        import numpy as np
        D_MODEL = 128
        NUM_HEADS = 16
        D_K = D_MODEL // NUM_HEADS
        ROPE_BASE = 10000.0

        def _rope_cos_sin(seq_len, d_k):
            inv_freq = 1.0 / ROPE_BASE ** (jnp.arange(0, d_k, 2, dtype=jnp.float32) / d_k)
            t = jnp.arange(seq_len, dtype=jnp.float32)
            freqs = t[:, None] * inv_freq[None, :]
            emb = jnp.concatenate([freqs, freqs], axis=-1)
            return (jnp.cos(emb)[None, None], jnp.sin(emb)[None, None])

        def _apply_rope(q, k, cos, sin):
            q1, q2 = (q[..., ::2], q[..., 1::2])
            k1, k2 = (k[..., ::2], k[..., 1::2])
            q_rot = jnp.concatenate([-q2, q1], axis=-1)
            k_rot = jnp.concatenate([-k2, k1], axis=-1)
            return (q * cos + q_rot * sin, k * cos + k_rot * sin)
        key = jax.random.key(seed)
        ks = jax.random.split(key, 5)
        B, S = (2, 256)
        x = jax.random.normal(ks[0], (B, S, D_MODEL), dtype=jnp.float32)
        scale = 1.0 / np.sqrt(D_MODEL)
        Wq = jax.random.normal(ks[1], (D_MODEL, D_MODEL), dtype=jnp.float32) * scale
        Wk = jax.random.normal(ks[2], (D_MODEL, D_MODEL), dtype=jnp.float32) * scale
        Wv = jax.random.normal(ks[3], (D_MODEL, D_MODEL), dtype=jnp.float32) * scale
        Wo = jax.random.normal(ks[4], (D_MODEL, D_MODEL), dtype=jnp.float32) * scale
        return {'x': x, 'Wq': Wq, 'Wk': Wk, 'Wv': Wv, 'Wo': Wo}
    _L0_attn_all = _L0_attn_setup()
    _L0_attn_in = {k: v for k, v in _L0_attn_all.items() if k in ('Wq', 'Wk', 'Wv', 'Wo')}
    del _L0_attn_all

    def _L0_xattn_setup():
        import jax, jax.numpy as jnp
        import numpy as np
        NEG = -1e+20
        key = jax.random.key(seed)
        ks = jax.random.split(key, 9)
        N, S, E, H = (4, 256, 128, 16)
        s = 0.02
        values = jax.random.normal(ks[0], (N, S, E), jnp.float32)
        keys = jax.random.normal(ks[1], (N, S, E), jnp.float32)
        query = jax.random.normal(ks[2], (N, S, E), jnp.float32)
        mask = jnp.tril(jnp.ones((S, S), jnp.int32))[None, None]
        Wv = jax.random.normal(ks[3], (E, E), jnp.float32) * s
        Wk = jax.random.normal(ks[4], (E, E), jnp.float32) * s
        Wq = jax.random.normal(ks[5], (E, E), jnp.float32) * s
        Wo = jax.random.normal(ks[6], (E, E), jnp.float32) * s
        bo = jnp.zeros((E,), jnp.float32)
        return {'values': values, 'keys': keys, 'query': query, 'mask': mask, 'Wv': Wv, 'Wk': Wk, 'Wq': Wq, 'Wo': Wo, 'bo': bo}
    _L0_xattn_all = _L0_xattn_setup()
    _L0_xattn_in = {k: v for k, v in _L0_xattn_all.items() if k in ('Wv', 'Wk', 'Wq', 'Wo', 'bo')}
    del _L0_xattn_all

    def _L0_ffn_setup():
        import jax, jax.numpy as jnp
        import numpy as np
        B, SEQ, D, E, F = (4, 128, 128, 8, 512)
        CAPACITY = 2
        key = jax.random.key(seed)
        ks = jax.random.split(key, 8)
        x = jax.random.normal(ks[0], (B, SEQ, D), jnp.float32)
        gate_weight = jax.random.normal(ks[1], (E, D), jnp.float32) * 0.006
        W1 = jax.random.normal(ks[2], (E, D, F), jnp.float32) * (1.0 / np.sqrt(D))
        b1 = jnp.zeros((E, F), jnp.float32)
        W2 = jax.random.normal(ks[3], (E, F, D), jnp.float32) * (1.0 / np.sqrt(F))
        b2 = jnp.zeros((E, D), jnp.float32)
        Ws1 = jax.random.normal(ks[4], (D, F), jnp.float32) * (1.0 / np.sqrt(D))
        bs1 = jnp.zeros((F,), jnp.float32)
        Ws2 = jax.random.normal(ks[5], (F, D), jnp.float32) * (1.0 / np.sqrt(F))
        bs2 = jnp.zeros((D,), jnp.float32)
        return {'x': x, 'gate_weight': gate_weight, 'W1': W1, 'b1': b1, 'W2': W2, 'b2': b2, 'Ws1': Ws1, 'bs1': bs1, 'Ws2': Ws2, 'bs2': bs2}
    _L0_ffn_all = _L0_ffn_setup()
    _L0_ffn_in = {k: v for k, v in _L0_ffn_all.items() if k in ('gate_weight', 'W1', 'b1', 'W2', 'b2', 'Ws1', 'bs1', 'Ws2', 'bs2')}
    del _L0_ffn_all

    def _L1_attn_setup():
        import jax, jax.numpy as jnp
        import numpy as np
        N_HEADS = 16
        key = jax.random.key(seed)
        ks = jax.random.split(key, 5)
        B, S, D = (2, 256, 128)
        dk = D // N_HEADS
        std = float(np.sqrt(2.0 / (D + D)))
        x = jax.random.normal(ks[0], (B, S, D), dtype=jnp.float32)
        w_q = jax.random.normal(ks[1], (D, D), dtype=jnp.float32) * std
        w_k = jax.random.normal(ks[2], (dk, D), dtype=jnp.float32) * std
        w_v = jax.random.normal(ks[3], (dk, D), dtype=jnp.float32) * std
        w_out = jax.random.normal(ks[4], (D, D), dtype=jnp.float32) * std
        softmax_scale = jnp.ones((1,), dtype=jnp.float32) / jnp.sqrt(jnp.float32(dk))
        return {'x': x, 'w_q': w_q, 'w_k': w_k, 'w_v': w_v, 'w_out': w_out, 'softmax_scale': softmax_scale}
    _L1_attn_all = _L1_attn_setup()
    _L1_attn_in = {k: v for k, v in _L1_attn_all.items() if k in ('w_q', 'w_k', 'w_v', 'w_out', 'softmax_scale')}
    del _L1_attn_all

    def _L1_xattn_setup():
        import jax, jax.numpy as jnp
        import numpy as np
        HEADS = 8
        DIM_HEAD = 64
        DIM = 128
        CTX_DIM = 128
        HIDDEN = HEADS * DIM_HEAD
        key = jax.random.key(seed)
        ks = jax.random.split(key, 7)
        b, n, m = (2, 256, 256)
        x = jax.random.normal(ks[0], (b, n, DIM), dtype=jnp.float32)
        context = jax.random.normal(ks[1], (b, m, CTX_DIM), dtype=jnp.float32)
        Wq = jax.random.normal(ks[2], (DIM, HIDDEN), dtype=jnp.float32) * (1.0 / np.sqrt(DIM))
        Wk = jax.random.normal(ks[3], (CTX_DIM, HIDDEN), dtype=jnp.float32) * (1.0 / np.sqrt(CTX_DIM))
        Wv = jax.random.normal(ks[4], (CTX_DIM, HIDDEN), dtype=jnp.float32) * (1.0 / np.sqrt(CTX_DIM))
        Wo = jax.random.normal(ks[5], (HIDDEN, DIM), dtype=jnp.float32) * (1.0 / np.sqrt(HIDDEN))
        bo = jax.random.normal(ks[6], (DIM,), dtype=jnp.float32) * 0.01
        return {'x': x, 'context': context, 'Wq': Wq, 'Wk': Wk, 'Wv': Wv, 'Wo': Wo, 'bo': bo}
    _L1_xattn_all = _L1_xattn_setup()
    _L1_xattn_in = {k: v for k, v in _L1_xattn_all.items() if k in ('Wq', 'Wk', 'Wv', 'Wo', 'bo')}
    del _L1_xattn_all

    def _L1_ffn_setup():
        import jax, jax.numpy as jnp
        import numpy as np
        TOP_K = 2

        def _mlp(x, w1, b1, w2, b2):
            h = jax.nn.gelu(jnp.einsum('bsd,di->bsi', x, w1) + b1)
            return jnp.einsum('bsi,id->bsd', h, w2) + b2
        key = jax.random.key(seed)
        ks = jax.random.split(key, 8)
        B, S, D, I, E = (2, 256, 128, 512, 8)
        s_in = 1.0 / np.sqrt(D)
        s_mid = 1.0 / np.sqrt(I)
        return {'x': jax.random.normal(ks[0], (B, S, D), jnp.float32), 'gate_w': jax.random.normal(ks[1], (D, E), jnp.float32) * s_in, 'gate_b': jnp.zeros((E,), jnp.float32), 'sh_w1': jax.random.normal(ks[2], (D, I), jnp.float32) * s_in, 'sh_b1': jnp.zeros((I,), jnp.float32), 'sh_w2': jax.random.normal(ks[3], (I, D), jnp.float32) * s_mid, 'sh_b2': jnp.zeros((D,), jnp.float32), 'ew1': jax.random.normal(ks[4], (E, D, I), jnp.float32) * s_in, 'eb1': jnp.zeros((E, I), jnp.float32), 'ew2': jax.random.normal(ks[5], (E, I, D), jnp.float32) * s_mid, 'eb2': jnp.zeros((E, D), jnp.float32)}
    _L1_ffn_all = _L1_ffn_setup()
    _L1_ffn_in = {k: v for k, v in _L1_ffn_all.items() if k in ('gate_w', 'gate_b', 'sh_w1', 'sh_b1', 'sh_w2', 'sh_b2', 'ew1', 'eb1', 'ew2', 'eb2')}
    del _L1_ffn_all
    return {'x': x, 'ctx_1024': ctx_1024, 'mask_1x1xSxS2_ik0': mask_1x1xSxS2_ik0, 'L0_attn_Wq': _L0_attn_in['Wq'], 'L0_attn_Wk': _L0_attn_in['Wk'], 'L0_attn_Wv': _L0_attn_in['Wv'], 'L0_attn_Wo': _L0_attn_in['Wo'], 'L0_xattn_Wv': _L0_xattn_in['Wv'], 'L0_xattn_Wk': _L0_xattn_in['Wk'], 'L0_xattn_Wq': _L0_xattn_in['Wq'], 'L0_xattn_Wo': _L0_xattn_in['Wo'], 'L0_xattn_bo': _L0_xattn_in['bo'], 'L0_ffn_gate_weight': _L0_ffn_in['gate_weight'], 'L0_ffn_W1': _L0_ffn_in['W1'], 'L0_ffn_b1': _L0_ffn_in['b1'], 'L0_ffn_W2': _L0_ffn_in['W2'], 'L0_ffn_b2': _L0_ffn_in['b2'], 'L0_ffn_Ws1': _L0_ffn_in['Ws1'], 'L0_ffn_bs1': _L0_ffn_in['bs1'], 'L0_ffn_Ws2': _L0_ffn_in['Ws2'], 'L0_ffn_bs2': _L0_ffn_in['bs2'], 'L1_attn_w_q': _L1_attn_in['w_q'], 'L1_attn_w_k': _L1_attn_in['w_k'], 'L1_attn_w_v': _L1_attn_in['w_v'], 'L1_attn_w_out': _L1_attn_in['w_out'], 'L1_attn_softmax_scale': _L1_attn_in['softmax_scale'], 'L1_xattn_Wq': _L1_xattn_in['Wq'], 'L1_xattn_Wk': _L1_xattn_in['Wk'], 'L1_xattn_Wv': _L1_xattn_in['Wv'], 'L1_xattn_Wo': _L1_xattn_in['Wo'], 'L1_xattn_bo': _L1_xattn_in['bo'], 'L1_ffn_gate_w': _L1_ffn_in['gate_w'], 'L1_ffn_gate_b': _L1_ffn_in['gate_b'], 'L1_ffn_sh_w1': _L1_ffn_in['sh_w1'], 'L1_ffn_sh_b1': _L1_ffn_in['sh_b1'], 'L1_ffn_sh_w2': _L1_ffn_in['sh_w2'], 'L1_ffn_sh_b2': _L1_ffn_in['sh_b2'], 'L1_ffn_ew1': _L1_ffn_in['ew1'], 'L1_ffn_eb1': _L1_ffn_in['eb1'], 'L1_ffn_ew2': _L1_ffn_in['ew2'], 'L1_ffn_eb2': _L1_ffn_in['eb2']}

def reference(x, ctx_1024, mask_1x1xSxS2_ik0, L0_attn_Wq, L0_attn_Wk, L0_attn_Wv, L0_attn_Wo, L0_xattn_Wv, L0_xattn_Wk, L0_xattn_Wq, L0_xattn_Wo, L0_xattn_bo, L0_ffn_gate_weight, L0_ffn_W1, L0_ffn_b1, L0_ffn_W2, L0_ffn_b2, L0_ffn_Ws1, L0_ffn_bs1, L0_ffn_Ws2, L0_ffn_bs2, L1_attn_w_q, L1_attn_w_k, L1_attn_w_v, L1_attn_w_out, L1_attn_softmax_scale, L1_xattn_Wq, L1_xattn_Wk, L1_xattn_Wv, L1_xattn_Wo, L1_xattn_bo, L1_ffn_gate_w, L1_ffn_gate_b, L1_ffn_sh_w1, L1_ffn_sh_b1, L1_ffn_sh_w2, L1_ffn_sh_b2, L1_ffn_ew1, L1_ffn_eb1, L1_ffn_ew2, L1_ffn_eb2):
    import jax
    import jax.numpy as jnp

    def _L0_attn_ref(x, Wq, Wk, Wv, Wo):
        import jax, jax.numpy as jnp
        import numpy as np
        D_MODEL = 128
        NUM_HEADS = 16
        D_K = D_MODEL // NUM_HEADS
        ROPE_BASE = 10000.0

        def _rope_cos_sin(seq_len, d_k):
            inv_freq = 1.0 / ROPE_BASE ** (jnp.arange(0, d_k, 2, dtype=jnp.float32) / d_k)
            t = jnp.arange(seq_len, dtype=jnp.float32)
            freqs = t[:, None] * inv_freq[None, :]
            emb = jnp.concatenate([freqs, freqs], axis=-1)
            return (jnp.cos(emb)[None, None], jnp.sin(emb)[None, None])

        def _apply_rope(q, k, cos, sin):
            q1, q2 = (q[..., ::2], q[..., 1::2])
            k1, k2 = (k[..., ::2], k[..., 1::2])
            q_rot = jnp.concatenate([-q2, q1], axis=-1)
            k_rot = jnp.concatenate([-k2, k1], axis=-1)
            return (q * cos + q_rot * sin, k * cos + k_rot * sin)
        B, S, D = x.shape
        H, dk = (NUM_HEADS, D_K)

        def proj(W):
            return (x @ W.T).reshape(B, S, H, dk).transpose(0, 2, 1, 3)
        q, k, v = (proj(Wq), proj(Wk), proj(Wv))
        cos, sin = _rope_cos_sin(S, dk)
        q, k = _apply_rope(q, k, cos, sin)
        scores = jnp.einsum('bhqd,bhkd->bhqk', q, k) / jnp.sqrt(jnp.float32(dk))
        attn = jax.nn.softmax(scores, axis=-1)
        out = jnp.einsum('bhqk,bhkd->bhqd', attn, v)
        out = out.transpose(0, 2, 1, 3).reshape(B, S, D)
        return out @ Wo.T

    def _L0_xattn_ref(values, keys, query, mask, Wv, Wk, Wq, Wo, bo):
        import jax, jax.numpy as jnp
        import numpy as np
        NEG = -1e+20
        N, Sq, E = query.shape
        H = 16
        D = E // H
        v = (values @ Wv.T).reshape(N, -1, H, D)
        k = (keys @ Wk.T).reshape(N, -1, H, D)
        q = (query @ Wq.T).reshape(N, Sq, H, D)
        energy = jnp.einsum('nqhd,nkhd->hnqk', q, k)
        energy = jnp.where(mask == 0, NEG, energy)
        attn = jax.nn.softmax(energy / jnp.sqrt(jnp.float32(D)), axis=-1)
        out = jnp.einsum('hnqk,nkhd->nqhd', attn, v).reshape(N, Sq, E)
        return out @ Wo.T + bo

    def _L0_ffn_ref(x, gate_weight, W1, b1, W2, b2, Ws1, bs1, Ws2, bs2):
        import jax, jax.numpy as jnp
        import numpy as np
        B, SEQ, D, E, F = (4, 128, 128, 8, 512)
        CAPACITY = 2
        Bb, s, Dd = x.shape
        Ee = gate_weight.shape[0]
        xf = x.reshape(-1, Dd)
        S = xf.shape[0]
        logits = xf @ gate_weight.T
        scores = jax.nn.softmax(logits, axis=-1).T
        k = S * CAPACITY
        vals, idx = jax.lax.top_k(scores.reshape(-1), k)
        eidx = idx // S
        tidx = idx % S
        gate = jnp.zeros((Ee, S), x.dtype).at[eidx, tidx].add(vals)
        h = jax.nn.gelu(jnp.einsum('sd,edf->esf', xf, W1) + b1[:, None, :], approximate=True)
        y = jnp.einsum('esf,efd->esd', h, W2) + b2[:, None, :]
        out = jnp.einsum('es,esd->sd', gate, y)
        shared = jax.nn.gelu(xf @ Ws1 + bs1, approximate=True) @ Ws2 + bs2
        out = out + shared
        return out.reshape(Bb, s, Dd)

    def _L1_attn_ref(x, w_q, w_k, w_v, w_out, softmax_scale):
        import jax, jax.numpy as jnp
        import numpy as np
        N_HEADS = 16
        B, S, D = x.shape
        dk = D // N_HEADS
        q = (x @ w_q.T).reshape(B, S, N_HEADS, dk)
        k = x @ w_k.T
        v = x @ w_v.T
        scores = jnp.einsum('bshd,btd->bhst', q, k) * softmax_scale[0]
        attn = jax.nn.softmax(scores, axis=-1)
        out = jnp.einsum('bhst,btd->bshd', attn, v).reshape(B, S, D)
        return out @ w_out.T

    def _L1_xattn_ref(x, context, Wq, Wk, Wv, Wo, bo):
        import jax, jax.numpy as jnp
        import numpy as np
        HEADS = 8
        DIM_HEAD = 64
        DIM = 128
        CTX_DIM = 128
        HIDDEN = HEADS * DIM_HEAD
        b, n, _ = x.shape
        m = context.shape[1]
        scale = DIM_HEAD ** (-0.5)
        q = (x @ Wq).reshape(b, n, HEADS, DIM_HEAD).transpose(0, 2, 1, 3)
        k = (context @ Wk).reshape(b, m, HEADS, DIM_HEAD).transpose(0, 2, 1, 3)
        v = (context @ Wv).reshape(b, m, HEADS, DIM_HEAD).transpose(0, 2, 1, 3)
        scores = jnp.einsum('bhnd,bhmd->bhnm', q, k) * scale
        attn = jax.nn.softmax(scores, axis=-1)
        out = jnp.einsum('bhnm,bhmd->bhnd', attn, v)
        out = out.transpose(0, 2, 1, 3).reshape(b, n, HIDDEN)
        return out @ Wo + bo

    def _L1_ffn_ref(x, gate_w, gate_b, sh_w1, sh_b1, sh_w2, sh_b2, ew1, eb1, ew2, eb2):
        import jax, jax.numpy as jnp
        import numpy as np
        TOP_K = 2

        def _mlp(x, w1, b1, w2, b2):
            h = jax.nn.gelu(jnp.einsum('bsd,di->bsi', x, w1) + b1)
            return jnp.einsum('bsi,id->bsd', h, w2) + b2
        E = ew1.shape[0]
        router_probs = jax.nn.softmax(jnp.einsum('bsd,de->bse', x, gate_w) + gate_b, axis=-1)
        expert_values, expert_indices = jax.lax.top_k(router_probs, k=TOP_K)
        expert_values = expert_values / (jnp.sum(expert_values, axis=-1, keepdims=True) + 1e-09)
        h = jax.nn.gelu(jnp.einsum('bsd,edi->bsei', x, ew1) + eb1)
        all_outputs = jnp.einsum('bsei,eid->bsed', h, ew2) + eb2
        one_hot = jax.nn.one_hot(expert_indices, E, dtype=x.dtype)
        weights_E = (one_hot * expert_values[..., None]).sum(axis=2)
        moe_out = jnp.einsum('bse,bsed->bsd', weights_E, all_outputs)
        return x + _mlp(x, sh_w1, sh_b1, sh_w2, sh_b2) + moe_out
    x = x + _L0_attn_ref(_layernorm(x, axis=-1), L0_attn_Wq, L0_attn_Wk, L0_attn_Wv, L0_attn_Wo)
    x = x + _L0_xattn_ref(ctx_1024, ctx_1024, _layernorm(x, axis=-1), mask_1x1xSxS2_ik0, L0_xattn_Wv, L0_xattn_Wk, L0_xattn_Wq, L0_xattn_Wo, L0_xattn_bo)
    x = x + _L0_ffn_ref(_layernorm(x, axis=-1), L0_ffn_gate_weight, L0_ffn_W1, L0_ffn_b1, L0_ffn_W2, L0_ffn_b2, L0_ffn_Ws1, L0_ffn_bs1, L0_ffn_Ws2, L0_ffn_bs2)
    x = x + _L1_attn_ref(_layernorm(x, axis=-1), L1_attn_w_q, L1_attn_w_k, L1_attn_w_v, L1_attn_w_out, L1_attn_softmax_scale)
    x = x + _L1_xattn_ref(_layernorm(x, axis=-1), ctx_1024, L1_xattn_Wq, L1_xattn_Wk, L1_xattn_Wv, L1_xattn_Wo, L1_xattn_bo)
    x = x + _L1_ffn_ref(_layernorm(x, axis=-1), L1_ffn_gate_w, L1_ffn_gate_b, L1_ffn_sh_w1, L1_ffn_sh_b1, L1_ffn_sh_w2, L1_ffn_sh_b2, L1_ffn_ew1, L1_ffn_eb1, L1_ffn_ew2, L1_ffn_eb2)
    return x

_drawn_inputs = setup_inputs


def setup_inputs(seed=0):
    import zlib

    import numpy as np

    out = dict(_drawn_inputs(seed))
    spreads = {'L0_xattn_bo': (0.0, 0.1),
     'L0_ffn_b1': (0.0, 0.391),
     'L0_ffn_b2': (0.0, 0.326),
     'L0_ffn_bs1': (0.0, 0.1),
     'L0_ffn_bs2': (0.0, 0.1),
     'L1_ffn_gate_b': (0.0, 0.1),
     'L1_ffn_sh_b1': (0.0, 0.321),
     'L1_ffn_sh_b2': (0.0, 0.1),
     'L1_ffn_eb1': (0.0, 0.42),
     'L1_ffn_eb2': (0.0, 0.268)}
    factors = {'L0_xattn_Wk': 8.0, 'L0_xattn_Wq': 8.0, 'L1_xattn_bo': 3.291}
    for name, (base, spread) in spreads.items():
        noise = np.random.default_rng([zlib.crc32(name.encode()), seed]).standard_normal(out[name].shape)
        drawn = base * np.exp(spread * noise) if base else spread * noise
        out[name] = jnp.asarray(drawn.astype(out[name].dtype))
    for name, factor in factors.items():
        out[name] = (out[name] * factor).astype(out[name].dtype)
    return out
```

```python
from contextlib import ExitStack

import concourse.bass as bass
from concourse import mybir

ALU = mybir.AluOpType
ACT = mybir.ActivationFunctionType
AX = mybir.AxisListType
F32 = mybir.dt.float32
F16 = mybir.dt.float16
BF16 = mybir.dt.bfloat16
I32 = mybir.dt.int32

P = 128
B = 4
S = 512
D = 128
QT = S // P
NT = B * QT
H = 16
DK = D // H
G = 4
J = H // G
C = 77
H1 = 8
DH = 64
HP = H1 // 2
E = 8
F = 512
FT = F // P
TOPK = B * S * 2
EPS = 1e-5
NEG = -1e20
MROW = 24

NST, NMX, NMI, NPT, NQS = 3, 2, 2, 8, 3

SELF0, CROSS0, FFN0, SELF1, CROSS1, FFN1 = range(6)

PACKS = [
    [("wq0", D), ("wqp0", D), ("wk0", D), ("wkp0", D), ("wv0", D)],
    [("xwq0", D), ("xwk0", D), ("xwv0", D), ("ctx", B * C), ("gate0", E)],
    [("wq1", D), ("wk1", D), ("wv1", D), ("gate1", E),
     ("ywq", 2 * H1 * DH), ("ywk", 2 * H1 * DH), ("ywv", H1 * DH)],
]
CONSTS = [("ident", P), ("cos", S), ("sin", S), ("selb", P), ("onerow", 1), ("headmask", J), ("tri", P), ("pick", E)]
CONSTS16 = [("id16", P), ("selqh", G * P), ("selql", G * P), ("selkh", G * P), ("selkl", G * P),
            ("irep", J * C), ("selm0", J * C), ("selm1", H1 * C)]


def offsets(cols):
    out, at = {}, 0
    for name, n in cols:
        out[name] = (at, n)
        at += n
    return out, at


CO, NCONST = offsets(CONSTS)
CH, NCONST16 = offsets(CONSTS16)
PO = [offsets(p) for p in PACKS]


def plan():
    steps = []
    helper = [0]

    def put(kind, *a, h=0):
        steps.append((kind, a, helper[0]))
        helper[0] += h

    def interleave(a, b, extra):
        n = max(len(a), len(b), 1)
        for i in range(n):
            for lst in (a, b):
                for x in lst[len(lst) * i // n:len(lst) * (i + 1) // n]:
                    put(*x)
            for x in extra[len(extra) * i // n:len(extra) * (i + 1) // n]:
                put(*x[0], h=x[1])

    def norm(ph, b):
        return [(("ln", ph, b), 0), (("xT", ph, b), 1)]

    def self_attention(ph):
        def project(b):
            rope = ph == SELF0
            return [(("proj", ph, b, "q"), 1 + rope), (("proj", ph, b, "k"), 1 + rope), (("v", ph, b), 1)]

        def stacks(n):
            return [(("ks", ph, n), 1), (("qs", ph, n), 1)]

        N = B * G
        for x in norm(ph, 0) + project(0) + stacks(0) + stacks(1):
            put(*x[0], h=x[1])
        for qt in range(QT):
            for j in range(J):
                put("max", ph, 0, qt, j)
        for n in range(N):
            b, g = divmod(n, G)
            put("mT", ph, n, h=1)
            extra = []
            if n:
                put("ou", ph, n - 1)
                extra += [(("sb", ph, n - 1), 1)]
            if g == 0 and b:
                extra += [(("out", ph, b - 1), 1)]
            if g in (0, 1) and n + 2 < N:
                extra += stacks(n + 2)
            if b + 1 < B:
                if g == 0:
                    extra += norm(ph, b + 1)
                if g == 1:
                    extra += project(b + 1)
                if g in (2, 3):
                    extra += stacks(n + 2)
            maxs = [("max", ph, n + 1, qt, j) for qt in range(QT) for j in range(J)] if n + 1 < N else []
            scores = []
            for kt in range(QT):
                scores += [("sc", ph, n, kt, j) for j in range(J)]
                if kt:
                    scores.insert(len(scores) - 2, ("pv", ph, n, kt - 1))
            scores.append(("pv", ph, n, QT - 1))
            interleave(maxs, scores, extra)
        for x in [(("ou", ph, N - 1), 0), (("sb", ph, N - 1), 1), (("out", ph, B - 1), 1)]:
            put(*x[0], h=x[1])

    def cross0():
        ph = CROSS0
        N = B * G
        put("proj", ph, 0, "k", h=1)
        for g in range(G):
            put("ks0", g, h=1)
        for b in range(B):
            put("v0", b, h=1)
        prep = lambda b: norm(ph, b) + [(("proj", ph, b, "q"), 1)]
        for x in prep(0) + [(("qs", ph, 0), 1), (("qs", ph, 1), 1)]:
            put(*x[0], h=x[1])
        for qt in range(QT):
            put("max", ph, 0, qt, 0)
        for n in range(N):
            b, g = divmod(n, G)
            put("mT", ph, n, h=1)
            extra = []
            if n:
                put("ou", ph, n - 1)
                extra += [(("sb", ph, n - 1), 1)]
            if g == 0 and b:
                extra += [(("out", ph, b - 1), 1)]
            if g in (0, 1) and n + 2 < N:
                extra += [(("qs", ph, n + 2), 1)]
            if b + 1 < B:
                if g == 0:
                    extra += norm(ph, b + 1)
                if g == 1:
                    extra += [(("proj", ph, b + 1, "q"), 1)]
                if g in (2, 3):
                    extra += [(("qs", ph, n + 2), 1)]
            maxs = [("max", ph, n + 1, qt, 0) for qt in range(QT)] if n + 1 < N else []
            interleave(maxs, [("sc", ph, n, 0, j) for j in range(J)], extra)
            put("pv", ph, n, 0)
        for x in [(("ou", ph, N - 1), 0), (("sb", ph, N - 1), 1), (("out", ph, B - 1), 1)]:
            put(*x[0], h=x[1])

    def cross1():
        ph = CROSS1
        for h in range(H1):
            put("yk", h, h=1)
        for b in range(B):
            put("yv", b, h=1)

        def prep(b):
            return norm(ph, b) + [x for h in range(H1) for x in ((("yq", b, h), 1), (("ymax", b, h), 0))]
        for x in prep(0):
            put(*x[0], h=x[1])
        for b in range(B):
            put("ymT", b, h=1)
            units = []
            for hp in range(HP):
                units += [("ysc", b, 2 * hp), ("ysc", b, 2 * hp + 1), ("ypv", b, hp)]
            nxt = prep(b + 1) if b + 1 < B else []
            for i, u in enumerate(units):
                if u[0] == "ypv":
                    put(*u, h=1)
                else:
                    put(*u)
                for x in nxt[len(nxt) * i // len(units):len(nxt) * (i + 1) // len(units)]:
                    put(*x[0], h=x[1])
            put("out", ph, b, h=1)

    def ffn(ph):
        for b in range(B):
            for x in norm(ph, b):
                put(*x[0], h=x[1])
        put("logits", ph, h=1)
        put("soft", ph)
        route = [(("bit", 29 - i), 1) for i in range(30)] + [(("choose",), 1)] if ph == FFN0 else [(("top2",), 0)]
        units = [(e, tb) for e in range(E + 1) for tb in range(B)]
        put("up", ph, 0, 0)
        for i, (e, tb) in enumerate(units):
            if e == 0:
                part = route[len(route) * tb // B:len(route) * (tb + 1) // B]
                for x in part:
                    put(*x[0], h=x[1])
            if i + 1 < len(units):
                put("up", ph, *units[i + 1])
            put("down", ph, e, tb)

    self_attention(SELF0)
    cross0()
    ffn(FFN0)
    self_attention(SELF1)
    cross1()
    ffn(FFN1)
    return steps



def build(nc, a):
    steps = plan()

    nth, at, helper_of = {}, {}, {}
    seen = {}
    ring = {"st": 0, "mx": 0, "pt": 0, "pv": 0}
    waiting = []
    pt_reader = {}
    for kind, args, hb in steps:
        key = (kind,) + args
        nth[key] = seen.get(kind, 0)
        seen[kind] = nth[key] + 1
        at[key] = dict(ring)
        helper_of[key] = hb
        if kind in ("sc", "ysc"):
            waiting.append(ring["pt"])
            ring["st"] += 1
            ring["pt"] += 1
        if kind == "up":
            ring["st"] += FT
        if kind in ("max", "ymax", "down"):
            ring["mx"] += 1
        if kind in ("pv", "ypv"):
            n = J if kind == "pv" else 2
            for t in waiting[:n]:
                pt_reader[t] = ring["pv"]
            waiting = waiting[n:]
            ring["pv"] += 1
    norms = [args for kind, args, _ in steps if kind == "ln"]
    projs = [args for kind, args, _ in steps if kind == "proj"]

    with ExitStack() as ctx:
        def sb(name, shape, dt=F32):
            return ctx.enter_context(nc.sbuf_tensor(name, shape, dt))

        def ps(name, shape, dt=F32):
            return ctx.enter_context(nc.psum_tensor(name, shape, dt))

        sems = {}

        def sem(name):
            if name not in sems:
                sems[name] = ctx.enter_context(nc.semaphore(name))
            return sems[name]

        st = ps("st", [P, NST, 512])
        mx = ps("mx", [P, NMX, 512])
        pv = ps("pv", [P, 512])
        mi = ps("mi", [P, NMI, 512])

        x = sb("x", [P, NT, D])
        xn = sb("xn", [P, 2, QT, D])
        xh = sb("xh", [P, B, S], F16)
        xl = sb("xl", [P, B, S], F16)
        const = sb("const", [P, NCONST])
        const16 = sb("const16", [P, NCONST16], F16)
        ones = sb("ones", [P, P])
        minus_half = sb("minus_half", [P, QT])
        wf = sb("wf", [P, max(n for _, n in PO)])
        wh = [sb(f"wh{n}", [P, PO[n][1]], F16) for n in range(3)]
        wl = [sb(f"wl{n}", [P, PO[n][1]], F16) for n in range(3)]
        wo = sb("wo", [P, 3, G, D])
        ywo = sb("ywo", [P, HP, D])
        bo = sb("bo", [P, 2, D])
        smscale = sb("smscale", [P, 1])
        gbias = sb("gbias", [P, E])
        maskT = sb("maskT", [C, S], I32)
        maskb = sb("maskb", [C, S], BF16)
        stats = sb("stats", [P, QT, 6])
        mv = sb("mv", [P, QT, 2])
        veps = sb("veps", [P, QT])
        rstd = sb("rstd", [P, QT])
        ropea = sb("ropea", [P, S])
        ropeb = sb("ropeb", [P, S])
        cf = sb("cf", [P, S])
        ch = sb("ch", [P, 2, S], F16)
        cl = sb("cl", [P, 2, S], F16)
        ks = sb("ks", [P, S], F16)
        kz = sb("kz", [P, NQS, J, S], F16)
        qs = sb("qs", [P, NQS, S], F16)
        mneg = sb("mneg", [P, 2, QT, P], F16)
        mnegb = sb("mnegb", [P, 2, QT, P], BF16)
        mneg1 = sb("mneg1", [P, 2, QT, P], F16)
        mtb = sb("mtb", [P, S], BF16)
        mt1 = sb("mt1", [P, S], F16)
        va = sb("va", [P, 2, QT, H, 32])
        nvx, nkx = B * H * 32, B * G * J * C // 2
        cross = sb("cross", [P, nvx + nkx])
        vx = cross[0:C, 0:nvx].rearrange("p (b h r) -> p b h r", b=B, h=H)
        kx = cross[:, nvx:nvx + nkx].bitcast(F16).rearrange("p (b g j c) -> p b g j c", b=B, g=G, j=J)
        vy = sb("vy", [C, B, H1, DH])
        pt = sb("pt", [P, NPT, S])
        ou = sb("ou", [P, S])
        rc = sb("rc", [P, S])
        on = sb("on", [P, 2, G, S])
        qh2 = va[:].rearrange("p a t h r -> p (a t h r)").bitcast(F16).rearrange("p (a h s) -> p a h s", a=2, h=H1)
        ql2 = cross[:, 0:H1 * S].bitcast(F16).rearrange("p (a h s) -> p a h s", a=2, h=H1)
        kzf = kz[:].rearrange("p a j s -> p (a j s)")
        nk = H1 * B * C
        kA = kzf[:, 0:nk].rearrange("p (h b c) -> p h b c", h=H1, b=B)
        kB = kzf[:, nk:2 * nk].rearrange("p (h b c) -> p h b c", h=H1, b=B)
        w1f = sb("w1f", [P, F])
        w1h = sb("w1h", [P, 2, F], F16)
        w1l = sb("w1l", [P, 2, F], F16)
        w2 = sb("w2", [P, 2, FT, D])
        b1 = sb("b1", [P, 2, E + 1, FT])
        b2 = sb("b2", [P, 2, D])
        hid = pt[:].rearrange("p (a f) s -> p a f s", a=2)
        lg = sb("lg", [P, NT, E])
        sm = sb("sm", [P, NT])
        rs = sb("rs", [P, NT])
        pr = sb("pr", [P, E, NT])
        gate = sb("gate", [P, E, NT])
        t0 = sb("t0", [P, E, NT])
        t1 = sb("t1", [P, E, NT])
        t2 = sb("t2", [P, E, NT])
        cum = sb("cum", [P, E * NT])
        thr = sb("thr", [P, 1], I32)
        cand = sb("cand", [P, 1], I32)
        inc = sb("inc", [P, 1], I32)
        part = sb("part", [P, 1])
        left = sb("left", [P, 1])
        left16 = sb("left16", [P, NT])

        def cst(name):
            p0, n = CO[name]
            return const[:, p0:p0 + n]

        def c16(name):
            p0, n = CH[name]
            return const16[:, p0:p0 + n]

        def sel(name, g):
            p0, _ = CH[name]
            return const16[:, p0 + g * P:p0 + (g + 1) * P]

        where = {name: (n, PO[n][0][name]) for n in range(3) for name, _ in PACKS[n]}

        def w(name, low=False, cut=slice(None)):
            n, (p0, k) = where[name]
            return (wl if low else wh)[n][:, p0:p0 + k][:, cut]

        needs_pack = {SELF0: 1, CROSS0: 2, FFN0: 2, SELF1: 3, CROSS1: 3, FFN1: 3}
        WQ = {SELF0: "wq0", CROSS0: "xwq0", SELF1: "wq1"}
        WK = {SELF0: "wk0", CROSS0: "xwk0", SELF1: "wk1"}
        WV = {SELF0: "wv0", SELF1: "wv1"}
        WO = {SELF0: 0, CROSS0: 1, SELF1: 2}
        SPLIT_AT = {("mT", SELF0, 1): 1, ("mT", SELF0, 5): 2}
        EXPERT = {FFN0: 0, FFN1: E + 1}

        def split_expert_at(kind, args):
            if kind == "logits":
                return EXPERT[args[0]]
            if kind == "up" and args[2] == 1 and args[1] < E:
                return EXPERT[args[0]] + args[1] + 1
            return None

        def done(*key):
            return nth[key] + 1

        def helper_read(eng, hb):
            eng.wait_ge(sem(f"helper_read{hb % NMI}"), hb // NMI + 1)

        def helper_filled(eng, hb):
            eng.wait_ge(sem("helper_filled"), hb + 1)

        def read_sem(hb):
            return sem(f"helper_read{hb % NMI}")

        def tile(t, n=1):
            return slice(t * P, (t + n) * P)

        def summed(eng, ph, b):
            if ph in (CROSS0, SELF1 + 1):
                eng.wait_ge(sem("out_summed"), done("out", ph - 1, b))
            elif ph in (FFN0, FFN1):
                eng.wait_ge(sem("out_summed"), done("out", ph - 1, b))
            elif ph == SELF1:
                eng.wait_ge(sem("down_summed"), done("down", FFN0, E, b))

        downs = [(k,) + ar for k, ar, _ in steps if k == "down"]

        def down_of(k):
            return at[downs[k]]["mx"] + 1

        ons = [(k,) + ar for k, ar, _ in steps if k in ("ou", "ypv")]

        def on_count(key):
            return ons.index(key) + 1

        def ons_before(key):
            reads = [(k, ) + ar for k, ar, _ in steps if k in ("ou", "ypv")]
            if key[0] == "pv":
                mine = ("ou", key[1], key[2])
            else:
                mine = key
            return reads.index(mine)

        block = ctx.enter_context(nc.Block())

        @block.sync
        def _(sp):
            def tokens(t, b):
                return t[b].rearrange("(t p) d -> p t d", p=P)

            sp.dma_start(x[:, 0:QT, :], tokens(a["x"], 0)).then_inc(sem("x_loaded0"), 16)
            sp.dma_start(const[:], a["const"]).then_inc(sem("const_loaded"), 16)
            sp.dma_start(wf[:, 0:PO[0][1]], a["pack0"]).then_inc(sem("pack_loaded"), 16)
            sp.dma_start(const16[:], a["const16"]).then_inc(sem("const16_loaded"), 16)
            for b in range(1, B):
                sp.dma_start(x[:, b * QT:(b + 1) * QT, :], tokens(a["x"], b)).then_inc(sem(f"x_loaded{b}"), 16)
            sp.dma_start(smscale[:], a["smscale"].partition_broadcast(P)).then_inc(sem("small_loaded"), 16)
            sp.dma_start(gbias[:], a["gbias"].partition_broadcast(P)).then_inc(sem("small_loaded"), 16)
            sp.dma_start(b1[:], a["b1"]).then_inc(sem("small_loaded"), 16)
            sp.dma_start(bo[:], a["bo"].partition_broadcast(P)).then_inc(sem("small_loaded"), 16)
            sp.dma_start(maskT[:], a["maskT"]).then_inc(sem("small_loaded"), 16)
            sp.dma_start(wo[:], a["wo"]).then_inc(sem("small_loaded"), 16)
            sp.dma_start(ywo[:], a["ywo"]).then_inc(sem("small_loaded"), 16)
            for n in (1, 2):
                sp.wait_ge(sem("pack_high"), n)
                sp.wait_ge(sem("pack_low"), n)
                sp.dma_start(wf[:, 0:PO[n][1]], a[f"pack{n}"]).then_inc(sem("pack_loaded"), 16)
            for n in range(2 * (E + 1)):
                ly, e = divmod(n, E + 1)
                if n:
                    sp.wait_ge(sem("w1_low"), n)
                sp.dma_start(w1f[:], a["w1"][ly, e]).then_inc(sem("w1_loaded"), 16)
                if n >= 2:
                    sp.wait_ge(sem("down_summed"), B * (n - 1))
                sp.dma_start(w2[:, n % 2], a["w2"][ly, e]).then_inc(sem(f"w2_loaded{n % 2}"), 16)
                sp.dma_start(b2[:, n % 2], a["b2"][ly, e].partition_broadcast(P)).then_inc(sem(f"w2_loaded{n % 2}"), 16)
            for b in range(B):
                sp.wait_ge(sem("down_summed"), done("down", FFN1, E, b))
                sp.dma_start(tokens(a["out"], b), x[:, b * QT:(b + 1) * QT, :]).then_inc(sem("stored"), 16)
            sp.wait_ge(sem("stored"), 16 * B)

        @block.gpsimd
        def _(pool):
            eng = nc.gpsimd

            def split_pack(n):
                pool.wait_ge(sem("pack_loaded"), 16 * (n + 1))
                pool.wait_ge(sem("pack_high"), n + 1)
                m = PO[n][1]
                eng.tensor_tensor(wl[n][:], wf[:, 0:m], wh[n][:], ALU.subtract).then_inc(sem("pack_low"), 1)

            eng.memset(minus_half[:], -0.5).then_inc(sem("half_set"), 1)
            pool.wait_ge(sem("half_set"), 1)
            eng.memset(ones[:], 1.0).then_inc(sem("ones_set"), 1)
            eng.memset(mneg[:], 0.0).then_inc(sem("mneg_cleared"), 1)
            split_pack(0)
            for kind, args, hb in steps:
                if kind == "ln":
                    pool.wait_ge(sem("var_ready"), done(kind, *args))
                    eng.tensor_tensor(rstd[:], veps[:], minus_half[:], ALU.pow).then_inc(sem("rstd_ready"), 1)
                    if args == (SELF0, 0):
                        eng.memset(va[:], 0.0).then_inc(sem("v_cleared"), 1)
                        pool.wait_ge(sem("v_cleared"), 1)
                        eng.memset(va[:, :, :, :, DK:DK + 1].rearrange("p a t h o -> p (a t h) o"), 1.0)\
                           .then_inc(sem("v_ones"), 1)
                    if args == (SELF0, 2):
                        eng.memset(vx[:], 0.0).then_inc(sem("v_cleared"), 1)
                        pool.wait_ge(sem("v_cleared"), 2)
                        eng.memset(vx[:, :, :, DK:DK + 1].rearrange("p b h o -> p (b h) o"), 1.0)\
                           .then_inc(sem("v_ones"), 1)
                        eng.memset(mnegb[:], 0.0).then_inc(sem("mneg_cleared"), 1)
                        eng.memset(mneg1[:], 0.0).then_inc(sem("mneg_cleared"), 1)
                if kind == "proj":
                    ph, b, which = args
                    qk, m = int(which == "k"), B * C if (ph, which) == (CROSS0, "k") else S
                    pool.wait_ge(sem("ch_ready"), done(kind, *args))
                    eng.tensor_tensor(cl[:, qk, 0:m], cf[:, 0:m], ch[:, qk, 0:m], ALU.subtract)\
                       .then_inc(sem("cl_ready"), 1)
                if kind == "ks":
                    ph, n = args
                    helper_read(pool, hb)
                    for j in range(J):
                        eng.tensor_scalar(kz[:, n % NQS, j, :], ks[:], cst("headmask")[:, j:j + 1], 0.0,
                                          ALU.mult, ALU.add).then_inc(sem("kz_ready"), 1)
                if kind == "ks0":
                    g, = args
                    helper_read(pool, hb)
                    for j in range(J):
                        eng.tensor_scalar(kx[:, :, g, j, :], ks[:, 0:B * C].rearrange("p (b c) -> p b c", b=B),
                                          cst("headmask")[:, j:j + 1], 0.0, ALU.mult, ALU.add)\
                           .then_inc(sem("kx_ready"), 1)
                if kind == "sb":
                    ph, n = args
                    helper_read(pool, hb)
                    pool.wait_ge(sem("pv_read"), on_count(("ou",) + args))
                    b, g = divmod(n, G)
                    eng.tensor_tensor(on[:, b % 2, g, :], ou[:], rc[:], ALU.mult).then_inc(sem("on_ready"), 1)
                if (kind,) + args in SPLIT_AT:
                    split_pack(SPLIT_AT[(kind,) + args])
                n = split_expert_at(kind, args)
                if n is not None:
                    pool.wait_ge(sem("w1_loaded"), 16 * (n + 1))
                    if n >= 2:
                        ly, e = divmod(n - 2, E + 1)
                        pool.wait_ge(sem("st_filled"), at[("up", (FFN0, FFN1)[ly], e, B - 1)]["st"] + FT)
                    eng.tensor_copy(w1h[:, n % 2, :], w1f[:]).then_inc(sem("w1_high"), 1)
                    pool.wait_ge(sem("w1_high"), n + 1)
                    eng.tensor_tensor(w1l[:, n % 2, :], w1f[:], w1h[:, n % 2, :], ALU.subtract)\
                       .then_inc(sem("w1_low"), 1)

        @block.scalar
        def _(act):
            eng = nc.scalar

            def copy(out, in_):
                return eng.activation(out, in_, ACT.Copy)

            def split_pack(n):
                act.wait_ge(sem("pack_loaded"), 16 * (n + 1))
                copy(wh[n][:], wf[:, 0:PO[n][1]]).then_inc(sem("pack_high"), 1)

            split_pack(0)
            for kind, args, hb in steps:
                key = (kind,) + args
                if kind == "xT":
                    ph, b = args
                    helper_filled(act, hb)
                    copy(xh[:, b, :], mi[:, hb % NMI, :]).then_inc(sem("xh_ready"), 1)
                elif kind == "proj":
                    ph, b, which = args
                    qk, m = int(which == "k"), B * C if (ph, which) == (CROSS0, "k") else S
                    if ph == SELF0:
                        act.wait_ge(sem("roped"), done(*key))
                    else:
                        helper_filled(act, hb)
                        if nth[key]:
                            act.wait_ge(sem("cl_ready"), nth[key])
                        if (ph, which) == (SELF1, "q"):
                            act.wait_ge(sem("small_loaded"), 16 * 7)
                            eng.activation(cf[:, 0:m], mi[:, hb % NMI, 0:m], ACT.Identity, scale=smscale[:, 0:1])\
                               .then_inc(read_sem(hb), 1)
                        else:
                            copy(cf[:, 0:m], mi[:, hb % NMI, 0:m]).then_inc(read_sem(hb), 1)
                        helper_read(act, hb)
                    copy(ch[:, qk, 0:m], cf[:, 0:m]).then_inc(sem("ch_ready"), 1)
                elif kind == "v":
                    ph, b = args
                    helper_filled(act, hb)
                    act.wait_ge(sem("v_cleared"), 1)
                    copy(va[:, b % 2, :, :, 0:DK].rearrange("p t h d -> p (t h) d"),
                         mi[:, hb % NMI, :].rearrange("p (a d) -> p a d", d=DK)).then_inc(read_sem(hb), 1)
                elif kind == "v0":
                    b, = args
                    helper_filled(act, hb)
                    act.wait_ge(sem("v_cleared"), 2)
                    copy(vx[:, b, :, 0:DK], mi[0:C, hb % NMI, 0:D].rearrange("p (a d) -> p a d", d=DK))\
                        .then_inc(read_sem(hb), 1)
                elif kind == "ks":
                    helper_filled(act, hb)
                    act.wait_ge(sem("const_loaded"), 16)
                    if nth[key]:
                        act.wait_ge(sem("kz_ready"), J * nth[key])
                    eng.activation(ks[:], mi[:, hb % NMI, :], ACT.Identity, bias=cst("onerow")).then_inc(read_sem(hb), 1)
                elif kind == "ks0":
                    g, = args
                    helper_filled(act, hb)
                    if g:
                        act.wait_ge(sem("kx_ready"), J * g)
                    else:
                        act.wait_ge(sem("kz_ready"), J * B * G)
                    copy(ks[:, 0:B * C], mi[:, hb % NMI, 0:B * C]).then_inc(read_sem(hb), 1)
                elif kind == "qs":
                    ph, n = args
                    helper_filled(act, hb)
                    copy(qs[:, n % NQS, :], mi[:, hb % NMI, :]).then_inc(read_sem(hb), 1)
                elif kind == "mT" and args[0] == CROSS0:
                    helper_filled(act, hb)
                    copy(mtb[:], mi[:, hb % NMI, :]).then_inc(read_sem(hb), 1)
                elif kind == "ymT":
                    helper_filled(act, hb)
                    copy(mt1[:], mi[:, hb % NMI, :]).then_inc(read_sem(hb), 1)
                elif kind in ("sc", "ysc"):
                    u, t = at[key]["st"], at[key]["pt"]
                    ph = args[0] if kind == "sc" else CROSS1
                    rows = P if ph in (SELF0, SELF1) else C
                    scale = {SELF0: DK ** -0.5, CROSS0: DK ** -0.5, SELF1: 1.0, CROSS1: DH ** -0.5}[ph]
                    act.wait_ge(sem("st_filled"), u + 1)
                    if t >= NPT:
                        act.wait_ge(sem("pv_done"), pt_reader[t - NPT] + 1)
                    eng.activation(pt[0:rows, t % NPT, :], st[0:rows, u % NST, :], ACT.Exp, scale=scale)\
                       .then_inc(sem("st_read"), 1)
                elif kind == "ou":
                    ph, n = args
                    act.wait_ge(sem("pv_done"), at[key]["pv"])
                    if nth[key]:
                        act.wait_ge(sem("on_ready"), on_count(key) - 1)
                    copy(ou[:], pv[:]).then_inc(sem("pv_read"), 1)
                elif kind == "yk":
                    h, = args
                    helper_filled(act, hb)
                    copy(kA[0:DH, h].rearrange("p b c -> p (b c)"), mi[0:DH, hb % NMI, 0:B * C]).then_inc(sem("kh_ready"), 1)
                    copy(kB[DH:P, h].rearrange("p b c -> p (b c)"), mi[DH:P, hb % NMI, 0:B * C]).then_inc(sem("kh_ready"), 1)
                elif kind == "yv":
                    b, = args
                    helper_filled(act, hb)
                    copy(vy[:, b].rearrange("p h d -> p (h d)"), mi[0:C, hb % NMI, :]).then_inc(read_sem(hb), 1)
                elif kind == "yq":
                    b, h = args
                    helper_filled(act, hb)
                    copy(qh2[:, b % 2, h, :], mi[:, hb % NMI, :]).then_inc(sem("qh_ready"), 1)
                elif kind == "soft":
                    act.wait_ge(sem("logits_shifted"), done(*key))
                    eng.activation(lg[:], lg[:], ACT.Exp).then_inc(sem("logits_exp"), 1)
                elif kind == "up":
                    ph, e, tb = args
                    n = EXPERT[ph] + e
                    act.wait_ge(sem("small_loaded"), 16 * 7)
                    if nth[key] >= 2:
                        act.wait_ge(sem("mx_filled"), down_of(nth[key] - 2))
                    for ft in range(FT):
                        u = at[key]["st"] + ft
                        act.wait_ge(sem("st_filled"), u + 1)
                        eng.activation(hid[:, nth[key] % 2, ft, :], st[:, u % NST, :], ACT.Gelu_apprx_tanh,
                                       bias=b1[:, n // (E + 1), e, ft:ft + 1]).then_inc(sem("st_read"), 1)
                if key in SPLIT_AT:
                    split_pack(SPLIT_AT[key])

        @block.tensor
        def _(pe):
            mm = nc.tensor.matmul
            loaded = set()

            def once(name, value):
                if (name, value) not in loaded:
                    loaded.add((name, value))
                    pe.wait_ge(sem(name), value)

            def helper_free(hb):
                if hb >= NMI:
                    helper_read(pe, hb - NMI)

            def st_free(u):
                if u >= NST:
                    pe.wait_ge(sem("st_read"), u - NST + 1)

            def mx_free(u):
                if u >= NMX:
                    pe.wait_ge(sem("mx_read"), u - NMX + 1)

            def three(out, lh, ll, rh, rl, start=True, stop=True):
                mm(out, lh, rh, start=start, stop=False)
                mm(out, lh, rl, start=False, stop=False)
                return mm(out, ll, rh, start=False, stop=stop)

            once("pack_low", 1)
            once("const16_loaded", 16)
            once("const_loaded", 16)
            for kind, args, hb in steps:
                key = (kind,) + args
                o = mi[:, hb % NMI, :]
                if kind == "xT":
                    ph, b = args
                    pe.wait_ge(sem("xn_ready"), done(*key))
                    helper_free(hb)
                    for t in range(QT):
                        last = nc.tensor.transpose(o[:, tile(t)], xn[:, nth[key] % 2, t, :], cst("ident"))
                    last.then_inc(sem("helper_filled"), 1)
                elif kind == "proj":
                    ph, b, which = args
                    once("pack_low", needs_pack[ph])
                    if (ph, which) == (CROSS0, "k"):
                        helper_free(hb)
                        three(o[:, 0:B * C], w("xwk0"), w("xwk0", 1), w("ctx"), w("ctx", 1)).then_inc(sem("helper_filled"), 1)
                    else:
                        helper_read(pe, helper_of[("xT", ph, b)])
                        name = (WQ if which == "q" else WK)[ph]
                        names = [name, name[:2] + "p0"] if ph == SELF0 else [name]
                        for k, nm in enumerate(names):
                            helper_free(hb + k)
                            three(mi[:, (hb + k) % NMI, :], w(nm), w(nm, 1), xh[:, b], xl[:, b])\
                                .then_inc(sem("helper_filled"), 1)
                elif kind == "v":
                    ph, b = args
                    helper_read(pe, helper_of[("xT", ph, b)])
                    helper_free(hb)
                    for t in range(QT):
                        last = three(o[:, tile(t)], xh[:, b, tile(t)], xl[:, b, tile(t)], w(WV[ph]), w(WV[ph], 1))
                    last.then_inc(sem("helper_filled"), 1)
                elif kind == "v0":
                    b, = args
                    helper_free(hb)
                    cb = slice(b * C, (b + 1) * C)
                    three(o[0:C, 0:D], w("ctx", 0, cb), w("ctx", 1, cb), w("xwv0"), w("xwv0", 1))\
                        .then_inc(sem("helper_filled"), 1)
                elif kind in ("ks", "ks0", "qs"):
                    if kind == "ks0":
                        g, m, proj = args[0], B * C, ("proj", CROSS0, 0, "k")
                    else:
                        b, g = divmod(args[1], G)
                        m, proj = S, ("proj", args[0], b, kind[0])
                    pe.wait_ge(sem("cl_ready"), done(*proj))
                    helper_free(hb)
                    c = kind[0]
                    mm(o[:, 0:m], sel(f"sel{c}h", g), ch[:, int(c == "k"), 0:m], start=True, stop=False)
                    mm(o[:, 0:m], sel(f"sel{c}l", g), cl[:, int(c == "k"), 0:m], start=False, stop=True)\
                        .then_inc(sem("helper_filled"), 1)
                elif kind == "max":
                    ph, n, qt, j = args
                    u = at[key]["mx"]
                    b, g = divmod(n, G)
                    helper_read(pe, helper_of[("qs", ph, n)])
                    lhs = qs[:, n % NQS, tile(qt)]
                    if ph == CROSS0:
                        pe.wait_ge(sem("kx_ready"), J * G)
                        once("mask_ready", 1)
                        mx_free(u)
                        mm(mx[:, u % NMX, 0:J * C], lhs, kx[:, b, g].rearrange("p j c -> p (j c)"), start=True, stop=False)
                        mm(mx[:, u % NMX, 0:J * C], maskb[:, tile(qt)], c16("irep")[0:C, :], start=False, stop=True)\
                            .then_inc(sem("mx_filled"), 1)
                    else:
                        pe.wait_ge(sem("kz_ready"), J * done("ks", ph, n))
                        mx_free(u)
                        mm(mx[:, u % NMX, :], lhs, kz[:, n % NQS, j, :], start=True, stop=True).then_inc(sem("mx_filled"), 1)
                elif kind == "mT":
                    ph, n = args
                    last_max = ("max", ph, n, QT - 1, 0 if ph == CROSS0 else J - 1)
                    pe.wait_ge(sem("mx_read"), at[last_max]["mx"] + 1)
                    helper_free(hb)
                    src = mnegb if ph == CROSS0 else mneg
                    for t in range(QT):
                        last = mm(o[:, tile(t)], src[:, n % 2, t, :], c16("id16"), start=True, stop=True)
                    last.then_inc(sem("helper_filled"), 1)
                elif kind == "sc":
                    ph, n, kt, j = args
                    b, g = divmod(n, G)
                    u = at[key]["st"]
                    helper_read(pe, helper_of[("mT", ph, n)])
                    st_free(u)
                    if ph == CROSS0:
                        out = st[0:C, u % NST, :]
                        mm(out, kx[:, b, g, j, :], qs[:, n % NQS, :], start=True, stop=False)
                        mm(out, c16("id16")[0:C, 0:C], maskb[:], start=False, stop=False)
                        mm(out, c16("selm0")[:, j * C:(j + 1) * C], mtb[:], start=False, stop=True)\
                            .then_inc(sem("st_filled"), 1)
                    else:
                        mm(st[:, u % NST, :], kz[:, n % NQS, j, tile(kt)], qs[:, n % NQS, :], start=True, stop=True)\
                            .then_inc(sem("st_filled"), 1)
                elif kind == "pv":
                    ph, n, kt = args
                    b, g = divmod(n, G)
                    s_last = ("sc", ph, n, kt, J - 1)
                    pe.wait_ge(sem("st_read"), at[s_last]["st"] + 1)
                    once("v_ones", 2 if ph == CROSS0 else 1)
                    if kt == 0:
                        if ph == CROSS0:
                            helper_read(pe, helper_of[("v0", b)])
                        else:
                            helper_read(pe, helper_of[("v", ph, b)])
                        if n or ph != SELF0:
                            pe.wait_ge(sem("pv_read"), ons_before(key))
                    for j in range(J):
                        t = (at[s_last]["pt"] - (J - 1) + j) % NPT
                        out = pv[32 * j:32 * j + 32, :]
                        if ph == CROSS0:
                            last = mm(out, vx[:, b, J * g + j, :], pt[0:C, t, :], start=True, stop=True)
                        else:
                            last = mm(out, va[:, b % 2, kt, J * g + j, :], pt[:, t, :], start=kt == 0, stop=kt == QT - 1)
                    last.then_inc(sem("pv_done"), 1)
                elif kind == "sb":
                    ph, n = args
                    pe.wait_ge(sem("pv_read"), on_count(("ou",) + args))
                    helper_free(hb)
                    mm(o, cst("selb"), ou[:], start=True, stop=True).then_inc(sem("helper_filled"), 1)
                elif kind == "out":
                    ph, b = args
                    last_on = ("ypv", b, HP - 1) if ph == CROSS1 else ("ou", ph, b * G + G - 1)
                    pe.wait_ge(sem("pv_read" if ph == CROSS1 else "on_ready"), on_count(last_on))
                    once("small_loaded", 16 * 7)
                    helper_free(hb)
                    for t in range(QT):
                        for g in range(G):
                            rhs = ywo[:, g, :] if ph == CROSS1 else wo[:, WO[ph], g, :]
                            last = mm(o[:, tile(t)], on[:, b % 2, g, tile(t)], rhs, start=g == 0, stop=g == G - 1)
                    last.then_inc(sem("helper_filled"), 1)
                elif kind == "yk":
                    h, = args
                    once("pack_low", 3)
                    helper_free(hb)
                    cut = slice(h * P, (h + 1) * P)
                    three(o[:, 0:B * C], w("ywk", 0, cut), w("ywk", 1, cut), w("ctx"), w("ctx", 1))\
                        .then_inc(sem("helper_filled"), 1)
                elif kind == "yv":
                    b, = args
                    helper_free(hb)
                    cb = slice(b * C, (b + 1) * C)
                    three(o[0:C, :], w("ctx", 0, cb), w("ctx", 1, cb), w("ywv"), w("ywv", 1)).then_inc(sem("helper_filled"), 1)
                elif kind == "yq":
                    b, h = args
                    helper_read(pe, helper_of[("xT", CROSS1, b)])
                    helper_free(hb)
                    cut = slice(h * P, (h + 1) * P)
                    three(o, w("ywq", 0, cut), w("ywq", 1, cut), xh[:, b], xl[:, b]).then_inc(sem("helper_filled"), 1)
                elif kind == "ymax":
                    b, h = args
                    u = at[key]["mx"]
                    helper_read(pe, helper_of[("yk", h)])
                    helper_read(pe, helper_of[("yq", b, h)])
                    mx_free(u)
                    for t in range(QT):
                        out = mx[:, u % NMX, t * C:(t + 1) * C]
                        mm(out, qh2[:, b % 2, h, tile(t)], kA[:, h, b, :], start=True, stop=False)
                        last = mm(out, ql2[:, b % 2, h, tile(t)], kB[:, h, b, :], start=False, stop=True)
                    last.then_inc(sem("mx_filled"), 1)
                elif kind == "ymT":
                    b, = args
                    pe.wait_ge(sem("mx_read"), at[("ymax", b, H1 - 1)]["mx"] + 1)
                    helper_free(hb)
                    for t in range(QT):
                        last = mm(o[:, tile(t)], mneg1[:, b % 2, t, :], c16("id16"), start=True, stop=True)
                    last.then_inc(sem("helper_filled"), 1)
                elif kind == "ysc":
                    b, h = args
                    u = at[key]["st"]
                    helper_read(pe, helper_of[("ymT", b)])
                    st_free(u)
                    out = st[0:C, u % NST, :]
                    mm(out, kA[:, h, b, :], qh2[:, b % 2, h, :], start=True, stop=False)
                    mm(out, kB[:, h, b, :], ql2[:, b % 2, h, :], start=False, stop=False)
                    mm(out, c16("selm1")[:, h * C:(h + 1) * C], mt1[:], start=False, stop=True).then_inc(sem("st_filled"), 1)
                elif kind == "ypv":
                    b, hp = args
                    s_last = ("ysc", b, 2 * hp + 1)
                    helper_read(pe, helper_of[("yv", b)])
                    pe.wait_ge(sem("st_read"), at[s_last]["st"] + 1)
                    pe.wait_ge(sem("pv_read"), ons_before(key))
                    helper_free(hb)
                    for i2 in range(2):
                        t = (at[s_last]["pt"] - 1 + i2) % NPT
                        r = slice(DH * i2, DH * i2 + DH)
                        mm(pv[r, :], vy[:, b, 2 * hp + i2, :], pt[0:C, t, :], start=True, stop=True)
                    for i2 in range(2):
                        t = (at[s_last]["pt"] - 1 + i2) % NPT
                        r = slice(DH * i2, DH * i2 + DH)
                        last = mm(mi[r, hb % NMI, :], ones[0:C, 0:DH], pt[0:C, t, :], start=True, stop=True)
                        last.then_inc(sem("helper_filled" if i2 else "pv_done"), 1)
                elif kind == "logits":
                    ph, = args
                    helper_free(hb)
                    name = "gate0" if ph == FFN0 else "gate1"
                    for b in range(B):
                        helper_read(pe, helper_of[("xT", ph, b)])
                        for t in range(QT):
                            c = (b * QT + t) * E
                            last = three(o[:, c:c + E], xh[:, b, tile(t)], xl[:, b, tile(t)], w(name), w(name, 1))
                    last.then_inc(sem("helper_filled"), 1)
                elif kind == "bit":
                    k, = args
                    pe.wait_ge(sem("part_ready"), done(*key))
                    helper_free(hb)
                    mm(o[:, 0:1], ones[:], part[:], start=True, stop=True).then_inc(sem("helper_filled"), 1)
                elif kind == "choose":
                    pe.wait_ge(sem("part_ready"), done("bit", 0) + 1)
                    helper_free(hb)
                    flat = t1[:].rearrange("p e t -> p (e t)")
                    mm(o[:, 0:1], ones[:], part[:], start=True, stop=True)
                    mm(o[:, P:2 * P], ones[:], flat, start=True, stop=True)
                    mm(o[:, 2 * P:3 * P], cst("tri"), flat, start=True, stop=True).then_inc(sem("helper_filled"), 1)
                elif kind == "up":
                    ph, e, tb = args
                    n = EXPERT[ph] + e
                    once("w1_low", n + 1)
                    for ft in range(FT):
                        u = at[key]["st"] + ft
                        st_free(u)
                        c = tile(ft)
                        three(st[:, u % NST, :], w1h[:, n % 2, c], w1l[:, n % 2, c], xh[:, tb], xl[:, tb])\
                            .then_inc(sem("st_filled"), 1)
                elif kind == "down":
                    ph, e, tb = args
                    n = EXPERT[ph] + e
                    u = at[key]["mx"]
                    up = ("up",) + args
                    once(f"w2_loaded{n % 2}", 32 * (n // 2 + 1))
                    pe.wait_ge(sem("st_read"), at[up]["st"] + FT)
                    mx_free(u)
                    for t in range(QT):
                        for ft in range(FT):
                            last = mm(mx[:, u % NMX, tile(t)], hid[:, nth[up] % 2, ft, tile(t)], w2[:, n % 2, ft, :],
                                      start=ft == 0, stop=ft == FT - 1)
                    last.then_inc(sem("mx_filled"), 1)

        @block.vector
        def _(dve):
            eng = nc.vector
            chain = [0]

            def link(ins, wait=True):
                chain[0] += 1
                ins.then_inc(sem("dve_chain"), 1)
                if wait:
                    linked()

            def linked():
                dve.wait_ge(sem("dve_chain"), chain[0])

            def bc(ap, shape):
                return ap.to_broadcast(shape)

            def over_tiles(ap):
                return ap.unsqueeze(2).to_broadcast([P, NT, E])

            def te(t):
                return t[:].rearrange("p e t -> p t e")

            def over_batch(ap):
                return ap.unsqueeze(1).to_broadcast([P, QT, D])

            for kind, args, hb in steps:
                key = (kind,) + args
                o = mi[:, hb % NMI, :]
                if kind == "ln":
                    ph, b = args
                    k = nth[key]
                    if ph == SELF0:
                        dve.wait_ge(sem(f"x_loaded{b}"), 16)
                    else:
                        summed(dve, ph, b)
                    if k:
                        dve.wait_ge(sem("xn_ready"), k)
                    for t in range(QT):
                        link(eng.bn_stats(stats[:, t, :], x[:, b * QT + t, :]), t == QT - 1)
                    for t in range(QT):
                        link(eng.bn_aggr(mv[:, t, :], stats[:, t, :]), t == QT - 1)
                    eng.tensor_scalar(veps[:], mv[:, :, 1], EPS, None, ALU.add).then_inc(sem("var_ready"), 1)
                    dve.wait_ge(sem("rstd_ready"), k + 1)
                    if k >= 2:
                        helper_filled(dve, helper_of[("xT",) + norms[k - 2]])
                    for t in range(QT):
                        last = eng.tensor_scalar(xn[:, k % 2, t, :], x[:, b * QT + t, :], mv[:, t, 0:1], rstd[:, t:t + 1],
                                                 ALU.subtract, ALU.mult)
                    last.then_inc(sem("xn_ready"), 1)
                elif kind == "xT":
                    ph, b = args
                    dve.wait_ge(sem("xh_ready"), done(*key))
                    helper_filled(dve, hb)
                    eng.tensor_tensor(xl[:, b, :], o, xh[:, b, :], ALU.subtract).then_inc(read_sem(hb), 1)
                    if ph == FFN1:
                        dve.wait_ge(sem("xn_ready"), done(*key))
                        xb = x[:, b * QT:(b + 1) * QT, :]
                        link(eng.tensor_tensor(xb, xb, xn[:, nth[key] % 2], ALU.add))
                elif kind == "proj" and args[0] == SELF0:
                    ph, b, which = args
                    helper_filled(dve, hb + 1)
                    dve.wait_ge(sem("const_loaded"), 16)
                    if nth[key]:
                        dve.wait_ge(sem("roped"), nth[key])
                    eng.tensor_tensor(ropea[:], o, cst("cos"), ALU.mult).then_inc(read_sem(hb), 1)
                    eng.tensor_tensor(ropeb[:], mi[:, (hb + 1) % NMI, :], cst("sin"), ALU.mult).then_inc(read_sem(hb + 1), 1)
                    helper_read(dve, hb)
                    helper_read(dve, hb + 1)
                    if nth[key]:
                        dve.wait_ge(sem("cl_ready"), nth[key])
                    eng.tensor_tensor(cf[:], ropea[:], ropeb[:], ALU.add).then_inc(sem("roped"), 1)
                elif kind == "max":
                    ph, n, qt, j = args
                    u = at[key]["mx"]
                    dve.wait_ge(sem("mx_filled"), u + 1)
                    dve.wait_ge(sem("mneg_cleared"), 3 if ph == CROSS0 else 1)
                    if ph == CROSS0:
                        eng.tensor_reduce(mnegb[:, n % 2, qt, MROW::32],
                                          mx[:, u % NMX, 0:J * C].rearrange("p (j c) -> p j c", j=J),
                                          AX.X, ALU.max, negate=True).then_inc(sem("mx_read"), 1)
                    else:
                        r = 32 * j + MROW
                        eng.tensor_reduce(mneg[:, n % 2, qt, r:r + 1], mx[:, u % NMX, :], AX.X, ALU.max, negate=True)\
                           .then_inc(sem("mx_read"), 1)
                elif kind == "ymax":
                    b, h = args
                    u = at[key]["mx"]
                    dve.wait_ge(sem("mx_filled"), u + 1)
                    eng.tensor_reduce(mneg1[:, b % 2, :, h], mx[:, u % NMX, 0:QT * C].rearrange("p (t c) -> p t c", t=QT),
                                      AX.X, ALU.max, negate=True).then_inc(sem("mx_read"), 1)
                elif kind == "mT" and args[0] != CROSS0:
                    ph, n = args
                    helper_filled(dve, hb)
                    eng.tensor_tensor(qs[:, n % NQS, :], o, qs[:, n % NQS, :], ALU.add).then_inc(read_sem(hb), 1)
                elif kind == "sb":
                    helper_filled(dve, hb)
                    if on_count(("ou",) + args) > 1:
                        dve.wait_ge(sem("on_ready"), on_count(("ou",) + args) - 1)
                    eng.reciprocal(rc[:], o).then_inc(read_sem(hb), 1)
                elif kind == "ypv":
                    b, hp = args
                    helper_filled(dve, hb)
                    dve.wait_ge(sem("pv_done"), at[key]["pv"] + 1)
                    dve.wait_ge(sem("pv_read"), on_count(key) - 1)
                    dve.wait_ge(sem("on_ready"), on_count(("ou", SELF1, B * G - 1)))
                    eng.reciprocal(rc[:], o).then_inc(read_sem(hb), 1)
                    helper_read(dve, hb)
                    eng.tensor_tensor(on[:, b % 2, hp, :], pv[:], rc[:], ALU.mult).then_inc(sem("pv_read"), 1)
                elif kind == "out":
                    ph, b = args
                    helper_filled(dve, hb)
                    xb = x[:, b * QT:(b + 1) * QT, :]
                    eng.tensor_tensor(xb, o.rearrange("p (t d) -> p t d", t=QT), xb, ALU.add).then_inc(read_sem(hb), 1)
                    helper_read(dve, hb)
                    if ph in (CROSS0, CROSS1):
                        dve.wait_ge(sem("small_loaded"), 16 * 7)
                        eng.tensor_tensor(xb, xb, over_batch(bo[:, int(ph == CROSS1), :]), ALU.add)\
                           .then_inc(sem("out_summed"), 1)
                    else:
                        dve.sem_inc(sem("out_summed"), 1)
                elif kind == "yk":
                    h, = args
                    dve.wait_ge(sem("kh_ready"), 2 * (h + 1))
                    lo, hi = slice(0, DH), slice(DH, P)
                    m = lambda t, r: t[r, h].rearrange("p b c -> p (b c)")
                    link(eng.tensor_tensor(m(kA, hi), mi[hi, hb % NMI, 0:B * C], m(kB, hi), ALU.subtract), False)
                    eng.tensor_tensor(m(kB, lo), mi[lo, hb % NMI, 0:B * C], m(kA, lo), ALU.subtract).then_inc(read_sem(hb), 1)
                elif kind == "yq":
                    b, h = args
                    dve.wait_ge(sem("qh_ready"), done(*key))
                    eng.tensor_tensor(ql2[:, b % 2, h, :], o, qh2[:, b % 2, h, :], ALU.subtract).then_inc(read_sem(hb), 1)
                elif kind == "logits":
                    ph, = args
                    helper_filled(dve, hb)
                    src = o[:, 0:NT * E].rearrange("p (t e) -> p t e", t=NT)
                    if ph == FFN0:
                        eng.tensor_copy(lg[:], src).then_inc(read_sem(hb), 1)
                    else:
                        eng.tensor_tensor(lg[:], src, gbias[:].unsqueeze(1).to_broadcast([P, NT, E]), ALU.add)\
                           .then_inc(read_sem(hb), 1)
                    helper_read(dve, hb)
                elif kind == "soft":
                    ph, = args
                    link(eng.tensor_reduce(sm[:], lg[:], AX.X, ALU.max))
                    eng.tensor_tensor(lg[:], lg[:], over_tiles(sm[:]), ALU.subtract).then_inc(sem("logits_shifted"), 1)
                    dve.wait_ge(sem("logits_exp"), done(*key))
                    link(eng.tensor_reduce(rs[:], lg[:], AX.X, ALU.add))
                    link(eng.reciprocal(rs[:], rs[:]))
                    link(eng.tensor_tensor(te(pr), lg[:], over_tiles(rs[:]), ALU.mult))
                    if ph == FFN0:
                        link(eng.memset(thr[:], 0))
                elif kind == "bit":
                    k, = args
                    link(eng.tensor_scalar(cand[:], thr[:], 1 << k, None, ALU.bitwise_or))
                    eng.tensor_scalar(t0[:], pr[:], cand[:].bitcast(F32), None, ALU.is_ge, ALU.add, accum_out=part[:])\
                       .then_inc(sem("part_ready"), 1)
                    helper_filled(dve, hb)
                    eng.tensor_scalar(inc[:], o[:, 0:1], float(TOPK), float(1 << k), ALU.is_ge, ALU.mult)\
                       .then_inc(read_sem(hb), 1)
                    helper_read(dve, hb)
                    link(eng.tensor_tensor(thr[:], thr[:], inc[:], ALU.bitwise_or))
                elif kind == "choose":
                    tv = thr[:].bitcast(F32)
                    link(eng.tensor_scalar(t1[:], pr[:], tv, None, ALU.is_equal))
                    eng.tensor_scalar(t0[:], pr[:], tv, None, ALU.is_gt, ALU.add, accum_out=part[:])\
                       .then_inc(sem("part_ready"), 1)
                    helper_filled(dve, hb)
                    flat = lambda t: t[:].rearrange("p e t -> p (e t)")
                    link(eng.tensor_scalar(left[:], o[:, 0:1], -1.0, float(TOPK), ALU.mult, ALU.add))
                    link(eng.tensor_tensor_scan(cum[:], ones[:], o[:, P:2 * P], 0.0, ALU.mult, ALU.add))
                    link(eng.tensor_tensor(cum[:], cum[:], o[:, P:2 * P], ALU.subtract))
                    eng.tensor_tensor(cum[:], cum[:], o[:, 2 * P:3 * P], ALU.add).then_inc(read_sem(hb), 1)
                    helper_read(dve, hb)
                    link(eng.scalar_tensor_tensor(flat(t2), cum[:], left[:, 0:1], flat(t1), ALU.is_le, ALU.mult))
                    link(eng.tensor_tensor(t0[:], t0[:], t2[:], ALU.add))
                    link(eng.tensor_tensor(gate[:], t0[:], pr[:], ALU.mult))
                elif kind == "top2":
                    pick = cst("pick").unsqueeze(1).to_broadcast([P, NT, E])

                    def first_max(out, vals, m):
                        link(eng.tensor_reduce(m, te(vals), AX.X, ALU.max))
                        link(eng.tensor_tensor(te(out), te(vals), over_tiles(m), ALU.is_equal))
                        link(eng.tensor_tensor(te(out), te(out), pick, ALU.mult))
                        link(eng.tensor_reduce(rs[:], te(out), AX.X, ALU.max))
                        link(eng.tensor_tensor(te(out), te(out), over_tiles(rs[:]), ALU.is_equal))

                    first_max(t0, pr, sm[:])
                    link(eng.scalar_tensor_tensor(t1[:].rearrange("p e t -> p (e t)"), t0[:].rearrange("p e t -> p (e t)"),
                                                  -2.0, pr[:].rearrange("p e t -> p (e t)"), ALU.mult, ALU.add))
                    first_max(t2, t1, left16[:])
                    link(eng.tensor_tensor(sm[:], sm[:], left16[:], ALU.add))
                    link(eng.tensor_scalar(sm[:], sm[:], 1e-9, None, ALU.add))
                    link(eng.reciprocal(sm[:], sm[:]))
                    link(eng.tensor_tensor(t0[:], t0[:], t2[:], ALU.add))
                    link(eng.tensor_tensor(t0[:], t0[:], pr[:], ALU.mult))
                    link(eng.tensor_tensor(te(gate), te(t0), over_tiles(sm[:]), ALU.mult))
                elif kind == "down":
                    ph, e, tb = args
                    n = EXPERT[ph] + e
                    u = at[key]["mx"]
                    dve.wait_ge(sem("mx_filled"), u + 1)
                    dve.wait_ge(sem(f"w2_loaded{n % 2}"), 32 * (n // 2 + 1))
                    if nth[key] >= 1:
                        dve.wait_ge(sem("down_summed"), nth[key])
                    if e == 0:
                        xb = x[:, tb * QT:(tb + 1) * QT, :]
                        eng.tensor_tensor(xb, mx[:, u % NMX, :].rearrange("p (t d) -> p t d", t=QT), xb, ALU.add)\
                           .then_inc(sem("mx_read"), 1)
                        dve.wait_ge(sem("mx_read"), u + 1)
                        eng.tensor_tensor(xb, xb, over_batch(b2[:, n % 2, :]), ALU.add).then_inc(sem("down_summed"), 1)
                        continue
                    for t in range(QT):
                        tt = tb * QT + t
                        last = eng.scalar_tensor_tensor(x[:, tt, :], mx[:, u % NMX, tile(t)], gate[:, e - 1, tt:tt + 1],
                                                        x[:, tt, :], ALU.mult, ALU.add)
                    last.then_inc(sem("mx_read"), 1)
                    dve.wait_ge(sem("mx_read"), u + 1)
                    for t in range(QT):
                        tt = tb * QT + t
                        last = eng.scalar_tensor_tensor(x[:, tt, :], b2[:, n % 2, :], gate[:, e - 1, tt:tt + 1],
                                                        x[:, tt, :], ALU.mult, ALU.add)
                    last.then_inc(sem("down_summed"), 1)
                if key == ("mT", SELF0, 9):
                    dve.wait_ge(sem("small_loaded"), 16 * 7)
                    eng.tensor_scalar(maskb[:], maskT[:], 0.0, NEG, ALU.is_equal, ALU.mult).then_inc(sem("mask_ready"), 1)


def constants():
    import numpy as np
    c = np.zeros((P, NCONST), np.float32)
    h16 = np.zeros((P, NCONST16), np.float16)

    def put(name, v):
        p0, n = CO[name]
        c[:, p0:p0 + n] = v

    def put16(name, v):
        p0, n = CH[name]
        h16[:v.shape[0], p0:p0 + n] = v.reshape(v.shape[0], n)

    put("ident", np.eye(P))
    put("tri", np.triu(np.ones((P, P))))
    put("pick", E - np.arange(E))
    inv = (1.0 / np.float32(10000.0) ** (np.arange(0, DK, 2, dtype=np.float32) / np.float32(DK))).astype(np.float32)
    freqs = np.arange(S, dtype=np.float32)[:, None] * inv[None, :]
    d = np.arange(P) % DK
    ang = freqs[:, d % (DK // 2)].T
    put("cos", np.cos(ang).astype(np.float32))
    put("sin", np.where(d[:, None] < DK // 2, -1, 1) * np.sin(ang).astype(np.float32))
    row = np.arange(P)
    put("onerow", (row % 32 == MROW)[:, None])
    put("headmask", row[:, None] // 32 == np.arange(J)[None, :])
    selb = np.zeros((P, P))
    for j in range(J):
        selb[32 * j + DK, 32 * j:32 * j + 32] = 1
    put("selb", selb)
    put16("id16", np.eye(P))
    parts = {"selqh": (0, 1), "selql": (2,), "selkh": (0, 2), "selkl": (1,)}
    for name, ts in parts.items():
        s = np.zeros((P, G, P))
        for g in range(G):
            for j in range(J):
                for t in ts:
                    for k in range(DK):
                        s[DK * (J * g + j) + k, g, 32 * j + DK * t + k] = 1
        put16(name, s)
    put16("irep", np.tile(np.eye(C), (1, J)))
    m0 = np.zeros((P, J, C))
    for j in range(J):
        m0[32 * j + MROW, j] = 1
    put16("selm0", m0)
    m1 = np.zeros((P, H1, C))
    for h in range(H1):
        m1[h, h] = 1
    put16("selm1", m1)
    return c, h16


def kernel(**inputs):
    import numpy as np
    import concourse.bacc as _bacc
    from concourse import mybir as _mybir
    from concourse.bass_utils import run_bass_kernel_spmd as _run

    v = {k: np.asarray(a) for k, a in inputs.items()}
    T = lambda name: v[name].T
    arrays = {"x": v["x"], "maskT": v["mask_1x1xSxS2_ik0"][0, 0].T}
    arrays["const"], arrays["const16"] = constants()
    half = DK // 2
    perm = np.array([DK * h + (2 * d + 1 if d < half else 2 * (d - half)) for h in range(H) for d in range(DK)])
    wq, wk = T("L0_attn_Wq"), T("L0_attn_Wk")
    arrays["pack0"] = np.concatenate([wq, wq[:, perm], wk, wk[:, perm], T("L0_attn_Wv")], axis=1)
    ctx = v["ctx_1024"].transpose(2, 0, 1).reshape(D, B * C)
    arrays["pack1"] = np.concatenate([T("L0_xattn_Wq"), T("L0_xattn_Wk"), T("L0_xattn_Wv"), ctx,
                                      T("L0_ffn_gate_weight")], axis=1)

    def twice(wt):
        return np.repeat(wt.reshape(D, H1, 1, DH), 2, axis=2).reshape(D, 2 * H1 * DH)

    arrays["pack2"] = np.concatenate([T("L1_attn_w_q"), np.tile(T("L1_attn_w_k"), (1, H)), np.tile(T("L1_attn_w_v"), (1, H)),
                                      v["L1_ffn_gate_w"], twice(v["L1_xattn_Wq"]), twice(v["L1_xattn_Wk"]),
                                      v["L1_xattn_Wv"]], axis=1)
    wo = np.zeros((3, G, J, 32, D), np.float32)
    for n, name in enumerate(("L0_attn_Wo", "L0_xattn_Wo", "L1_attn_w_out")):
        wo[n, :, :, 0:DK] = T(name).reshape(G, J, DK, D)
    arrays["wo"] = wo.reshape(3, G, P, D).transpose(2, 0, 1, 3)
    arrays["ywo"] = v["L1_xattn_Wo"].reshape(HP, P, D).transpose(1, 0, 2)
    arrays["bo"] = np.stack([v["L0_xattn_bo"], v["L1_xattn_bo"]])
    arrays["smscale"] = v["L1_attn_softmax_scale"]
    arrays["gbias"] = v["L1_ffn_gate_b"]
    w1 = [np.concatenate([v["L0_ffn_Ws1"][None], v["L0_ffn_W1"]]), np.concatenate([v["L1_ffn_sh_w1"][None], v["L1_ffn_ew1"]])]
    w2 = [np.concatenate([v["L0_ffn_Ws2"][None], v["L0_ffn_W2"]]), np.concatenate([v["L1_ffn_sh_w2"][None], v["L1_ffn_ew2"]])]
    b1 = [np.concatenate([v["L0_ffn_bs1"][None], v["L0_ffn_b1"]]), np.concatenate([v["L1_ffn_sh_b1"][None], v["L1_ffn_eb1"]])]
    b2 = [np.concatenate([v["L0_ffn_bs2"][None], v["L0_ffn_b2"]]), np.concatenate([v["L1_ffn_sh_b2"][None], v["L1_ffn_eb2"]])]
    arrays["w1"] = np.stack(w1)
    arrays["w2"] = np.stack(w2).reshape(2, E + 1, FT, P, D).transpose(0, 1, 3, 2, 4)
    arrays["b1"] = np.stack(b1).reshape(2, E + 1, FT, P).transpose(3, 0, 1, 2)
    arrays["b2"] = np.stack(b2)

    nc = _bacc.Bacc("TRN2", target_bir_lowering=False, num_devices=1)
    ins, aps = {}, {}
    for name, arr in arrays.items():
        arr = np.ascontiguousarray(arr)
        ins[f"in_{name}"] = arr
        aps[name] = nc.dram_tensor(f"in_{name}", arr.shape, _mybir.dt.from_np(arr.dtype), kind="ExternalInput").ap()
    aps["out"] = nc.dram_tensor("out_x", (B, S, D), F32, kind="ExternalOutput").ap()
    build(nc, aps)
    r = _run(nc, [ins], core_ids=[0])
    return r.results[0]["out_x"]
```

```python
from contextlib import ExitStack

import concourse.bass as bass
from concourse import mybir

ALU = mybir.AluOpType
ACT = mybir.ActivationFunctionType
AX = mybir.AxisListType
F32 = mybir.dt.float32
F16 = mybir.dt.float16
BF16 = mybir.dt.bfloat16
I32 = mybir.dt.int32

P = 128
B = 4
S = 512
D = 128
QT = S // P
NT = B * QT
H = 16
DK = D // H
G = 4
J = H // G
C = 77
H1 = 8
DH = 64
HP = H1 // 2
E = 8
F = 512
FT = F // P
TOPK = B * S * 2
EPS = 1e-5
NEG = -1e20
MROW = 24

NST, NMX, NMI, NPT, NQS = 3, 2, 2, 8, 3

SELF0, CROSS0, FFN0, SELF1, CROSS1, FFN1 = range(6)

PACKS = [
    [("wq0", D), ("wqp0", D), ("wk0", D), ("wkp0", D), ("wv0", D)],
    [("xwq0", D), ("xwk0", D), ("xwv0", D), ("ctx", B * C), ("gate0", E)],
    [("wq1", D), ("wk1", D), ("wv1", D), ("gate1", E),
     ("ywq", 2 * H1 * DH), ("ywk", 2 * H1 * DH), ("ywv", H1 * DH)],
]
CONSTS = [("ident", P), ("cos", S), ("sin", S), ("onerow", 1), ("headmask", J), ("tri", P), ("pick", E)]
CONSTS16 = [("id16", P), ("selqh", G * P), ("selql", G * P), ("selkh", G * P), ("selkl", G * P),
            ("irep", J * C), ("selm0", J * C), ("selm1", H1 * C)]


def offsets(cols):
    out, at = {}, 0
    for name, n in cols:
        out[name] = (at, n)
        at += n
    return out, at


CO, NCONST = offsets(CONSTS)
CH, NCONST16 = offsets(CONSTS16)
PO = [offsets(p) for p in PACKS]


def plan():
    steps = []
    helper = [0]

    def put(kind, *a, h=0):
        steps.append((kind, a, helper[0]))
        helper[0] += h

    def norm(ph, b):
        return [(("ln", ph, b), 0), (("ln2", ph, b), 0), (("xT", ph, b), 1)]

    def stream(ph, maxs, scores, products, prep, stacks):
        N, U = B * G, len(scores(0))
        lead, lag = U + max(U // 4, 2), 2
        events = []

        def on(pos, *xs):
            for x, h in xs:
                events.append((pos, len(events), x, h))

        for x in prep(0)[0] + prep(0)[1] + stacks(0) + stacks(1):
            put(*x[0], h=x[1])
        for n in range(N):
            b, g = divmod(n, G)
            at0 = n * U
            on(at0 - U + U - 1 - (lead - U) + max(U // 8, 1), (("mT", ph, n), 1))
            for x, used in products(n):
                on(at0 + used - 1 + lag, (x, 0))
            end = at0 + U - 1 + lag
            on(end, (("ou", ph, n), 0))
            on(end + max(U // 6, 1), (("sb", ph, n), 1))
            if g == G - 1:
                on(end + U // 3, (("outT", ph, b), 1))
                on(end + U // 2, (("out", ph, b), 1))
                for i, x in enumerate(norm(ph + 1, b)):
                    on(end + U // 2 + 1 + i * max(U // 8, 1), x)
                if b == B - 1 and ph == SELF0:
                    for i, x in enumerate(cross0_context()):
                        on(at0 + 1 + i, x)
            if n + 2 < N:
                st = stacks(n + 2)
                for i, x in enumerate(st):
                    on(at0 + i * U // 8 + 1, x)
            if b + 1 < B and g in (0, 1):
                part = prep(b + 1)[g]
                for i, x in enumerate(part):
                    on(at0 + U // 4 + 1 + i * (U // 2) // len(part), x)
        events.sort()
        flat_max = [x for n in range(N) for x in maxs(n)]
        flat_sc = [x for n in range(N) for x in scores(n)]
        done_max = 0
        for u in range(-lead, max(N * U, events[-1][0] + 1)):
            if done_max < len(flat_max):
                put(*flat_max[done_max])
                done_max += 1
            if 0 <= u < len(flat_sc):
                put(*flat_sc[u])
            while events and events[0][0] <= u:
                _, _, x, h = events.pop(0)
                put(*x, h=h)

    def cross0_context():
        return ([(("proj", CROSS0, 0, "k"), 1)] + [(("ks0", g), 1) for g in range(G)]
                + [(("v0", b), 1) for b in range(B)])

    def cross1_context():
        return [(("yk", h), 1) for h in range(H1)] + [(("yv", b), 1) for b in range(B)]

    def self_attention(ph):
        def prep(b):
            rope = ph == SELF0
            return norm(ph, b) if ph == SELF0 else [], [(("proj", ph, b, "q"), 1 + rope), (("proj", ph, b, "k"), 1 + rope), (("v", ph, b), 1)]

        stream(ph,
               maxs=lambda n: [("max", ph, n, qt, j) for qt in range(QT) for j in range(J)],
               scores=lambda n: [("sc", ph, n, kt, j) for kt in range(QT) for j in range(J)],
               products=lambda n: [(("pv", ph, n, kt), J * (kt + 1)) for kt in range(QT)],
               prep=prep, stacks=lambda n: [(("ks", ph, n), 1), (("qs", ph, n), 1)])

    def cross0():
        ph = CROSS0
        stream(ph,
               maxs=lambda n: [("max", ph, n, qt, 0) for qt in range(QT)],
               scores=lambda n: [("sc", ph, n, 0, j) for j in range(J)],
               products=lambda n: [(("pv", ph, n, 0), J)],
               prep=lambda b: ([], [(("proj", ph, b, "q"), 1)]), stacks=lambda n: [(("qs", ph, n), 1)])

    def cross1():
        ph = CROSS1
        wait_max, wait_sc = 2, H1 + 3
        for s in range(B * H1 + wait_sc + 3):
            sc = s - wait_sc
            if 0 <= sc < B * H1:
                put("ysc", *divmod(sc, H1))
            if s < B * H1:
                put("yq", *divmod(s, H1), h=1)
            sc -= 1
            if 0 <= sc < B * H1 and sc % 2:
                b, h = divmod(sc, H1)
                put("ypv", b, h // 2, h=1)
            if 0 <= s - wait_max < B * H1:
                put("ymax", *divmod(s - wait_max, H1))
            m = s - wait_max - 1
            if 0 <= m < B * H1 and m % H1 == H1 - 1:
                put("ymT", m // H1, h=1)
            sc -= 1
            if 0 <= sc < B * H1 and sc % 2:
                b, h = divmod(sc, H1)
                put("ybc", b, h // 2, h=1)
            if sc >= H1 and sc % H1 == 0:
                b = sc // H1 - 1
                put("out", ph, b, h=1)
                for x in norm(FFN1, b):
                    put(*x[0], h=x[1])

    def ffn(ph):
        put("logits", ph, h=1)
        put("soft", ph)
        route = [(("bit", 28 - 2 * i), 1) for i in range(15)] + [(("choose",), 1)] if ph == FFN0 else [(("top2",), 0)]
        context = cross1_context()
        units = [(e, tb) for e in range(E + 1) for tb in range(B)]
        put("up", ph, 0, 0)
        for i, (e, tb) in enumerate(units):
            if e == 0:
                part = route[len(route) * tb // B:len(route) * (tb + 1) // B]
                for x in part:
                    put(*x[0], h=x[1])
            if i + 1 < len(units):
                put("up", ph, *units[i + 1])
            put("down", ph, e, tb)
            if ph == FFN0:
                if e == E:
                    for x in norm(SELF1, tb):
                        put(*x[0], h=x[1])
                elif e and i % 2:
                    for x in context[:1]:
                        put(*x[0], h=x[1])
                    context = context[1:]

    self_attention(SELF0)
    cross0()
    ffn(FFN0)
    self_attention(SELF1)
    cross1()
    ffn(FFN1)
    return steps



def build(nc, a):
    steps = plan()

    nth, at, helper_of = {}, {}, {}
    seen = {}
    ring = {"st": 0, "mx": 0, "pt": 0, "pv": 0}
    waiting = []
    pt_reader = {}
    for kind, args, hb in steps:
        key = (kind,) + args
        nth[key] = seen.get(kind, 0)
        seen[kind] = nth[key] + 1
        at[key] = dict(ring)
        helper_of[key] = hb
        if kind in ("sc", "ysc"):
            waiting.append(ring["pt"])
            ring["st"] += 1
            ring["pt"] += 1
        if kind == "up":
            ring["st"] += FT
        if kind in ("max", "ymax", "down"):
            ring["mx"] += 1
        if kind in ("pv", "ypv"):
            n = J if kind == "pv" else 2
            for t in waiting[:n]:
                pt_reader[t] = (ring["pv"], key)
            waiting = waiting[n:]
            ring["pv"] += 1
    norms = [args for kind, args, _ in steps if kind == "ln"]
    projs = [args for kind, args, _ in steps if kind == "proj"]

    with ExitStack() as ctx:
        def sb(name, shape, dt=F32):
            return ctx.enter_context(nc.sbuf_tensor(name, shape, dt))

        def ps(name, shape, dt=F32):
            return ctx.enter_context(nc.psum_tensor(name, shape, dt))

        sems = {}

        def sem(name):
            if name not in sems:
                sems[name] = ctx.enter_context(nc.semaphore(name))
            return sems[name]

        st = ps("st", [P, NST, 512])
        mx = ps("mx", [P, NMX, 512])
        pv = ps("pv", [P, 512])
        mi = ps("mi", [P, NMI, 512])

        x = sb("x", [P, NT, D])
        xn = sb("xn", [P, 2, QT, D])
        xh = sb("xh", [P, B, S], F16)
        xl = sb("xl", [P, B, S], F16)
        const = sb("const", [P, NCONST])
        const16 = sb("const16", [P, NCONST16], F16)
        ones = sb("ones", [P, P])
        minus_half = sb("minus_half", [P, QT])
        wf = sb("wf", [P, max(n for _, n in PO)])
        wh = [sb(f"wh{n}", [P, PO[n][1]], F16) for n in range(3)]
        wl = [sb(f"wl{n}", [P, PO[n][1]], F16) for n in range(3)]
        wo = sb("wo", [P, 3, D])
        ywo = sb("ywo", [P, HP, D])
        bo = sb("bo", [P, 2, D])
        smscale = sb("smscale", [P, 1])
        gbias = sb("gbias", [P, E])
        maskT = sb("maskT", [C, S], I32)
        maskb = sb("maskb", [C, S], BF16)
        stats = sb("stats", [P, QT, 6])
        mv = sb("mv", [P, QT, 2])
        veps = sb("veps", [P, QT])
        rstd = sb("rstd", [P, QT])
        rope = sb("rope", [P, 2, S])
        cf = sb("cf", [P, S])
        ch = sb("ch", [P, 2, S], F16)
        cl = sb("cl", [P, 2, S], F16)
        ks = sb("ks", [P, S], F16)
        kz = sb("kz", [P, NQS, J, S], F16)
        qs = sb("qs", [P, NQS, S], F16)
        mneg = sb("mneg", [P, 2, QT, P], F16)
        mnegb = sb("mnegb", [P, 2, QT, P], BF16)
        mneg1 = sb("mneg1", [P, 2, QT, P], F16)
        mtb = sb("mtb", [P, 2, S], BF16)
        mt1 = sb("mt1", [P, S], F16)
        va = sb("va", [P, 2, QT, H, 32])
        nvx, nkx = B * H * 32, B * G * J * C // 2
        cross = sb("cross", [P, nvx + nkx])
        vx = cross[0:C, 0:nvx].rearrange("p (b h r) -> p b h r", b=B, h=H)
        kx = cross[:, nvx:nvx + nkx].bitcast(F16).rearrange("p (b g j c) -> p b g j c", b=B, g=G, j=J)
        vy = sb("vy", [C, B, H1, DH])
        pt = sb("pt", [P, NPT, S])
        ou = sb("ou", [P, S])
        ou1 = sb("ou1", [P, 2, S])
        rc = sb("rc", [P, 2, QT * J])
        rce = rope
        ont = sb("ont", [P, 2, QT, D])
        onT = sb("onT", [P, S])
        on = sb("on", [P, 2, G, S])
        qh2 = va[:].rearrange("p a t h r -> p (a t h r)").bitcast(F16).rearrange("p (a h s) -> p a h s", a=2, h=H1)
        ql2 = cross[:, 0:H1 * S].bitcast(F16).rearrange("p (a h s) -> p a h s", a=2, h=H1)
        kzf = wf[:].bitcast(F16)
        nk = H1 * B * C
        kA = kzf[:, 0:nk].rearrange("p (h b c) -> p h b c", h=H1, b=B)
        kB = kzf[:, nk:2 * nk].rearrange("p (h b c) -> p h b c", h=H1, b=B)
        w1f = sb("w1f", [P, F])
        w1h = sb("w1h", [P, 2, F], F16)
        w1l = sb("w1l", [P, 2, F], F16)
        w2 = sb("w2", [P, 2, FT, D])
        b1 = sb("b1", [P, 2, E + 1, FT])
        b2 = sb("b2", [P, 2, D])
        hid = pt[:].rearrange("p (a f) s -> p a f s", a=2)
        lg = sb("lg", [P, NT, E])
        sm = sb("sm", [P, NT])
        rs = sb("rs", [P, NT])
        pr = sb("pr", [P, E, NT])
        gate = sb("gate", [P, E, NT])
        t0 = sb("t0", [P, E, NT])
        t1 = sb("t1", [P, E, NT])
        t2 = sb("t2", [P, E, NT])
        cum = sb("cum", [P, E * NT])
        thr = sb("thr", [P, 1], I32)
        cand = sb("cand", [P, 3], I32)
        inc = sb("inc", [P, 1], I32)
        part = sb("part", [P, 3])
        left = sb("left", [P, 1])
        passed = sb("passed", [P, 3])
        left16 = sb("left16", [P, NT])

        def cst(name):
            p0, n = CO[name]
            return const[:, p0:p0 + n]

        def c16(name):
            p0, n = CH[name]
            return const16[:, p0:p0 + n]

        def sel(name, g):
            p0, _ = CH[name]
            return const16[:, p0 + g * P:p0 + (g + 1) * P]

        where = {name: (n, PO[n][0][name]) for n in range(3) for name, _ in PACKS[n]}

        def w(name, low=False, cut=slice(None)):
            n, (p0, k) = where[name]
            return (wl if low else wh)[n][:, p0:p0 + k][:, cut]

        needs_pack = {SELF0: 1, CROSS0: 2, FFN0: 2, SELF1: 3, CROSS1: 3, FFN1: 3}
        WQ = {SELF0: "wq0", CROSS0: "xwq0", SELF1: "wq1"}
        WK = {SELF0: "wk0", CROSS0: "xwk0", SELF1: "wk1"}
        WV = {SELF0: "wv0", SELF1: "wv1"}
        WO = {SELF0: 0, CROSS0: 1, SELF1: 2}
        SPLIT_AT = {("mT", SELF0, 1): 1, ("mT", SELF0, 5): 2}
        EXPERT = {FFN0: 0, FFN1: E + 1}

        def split_expert_at(kind, args):
            if kind == "logits":
                return EXPERT[args[0]]
            if kind == "up" and args[2] == 1 and args[1] < E:
                return EXPERT[args[0]] + args[1] + 1
            return None

        def done(*key):
            return nth[key] + 1

        def helper_read(eng, hb):
            eng.wait_ge(sem(f"helper_read{hb % NMI}"), hb // NMI + 1)

        def helper_filled(eng, hb):
            eng.wait_ge(sem("helper_filled"), hb + 1)

        def read_sem(hb):
            return sem(f"helper_read{hb % NMI}")

        def tile(t, n=1):
            return slice(t * P, (t + n) * P)

        def summed(eng, ph, b):
            if ph in (CROSS0, SELF1 + 1):
                eng.wait_ge(sem("out_summed"), done("out", ph - 1, b))
            elif ph in (FFN0, FFN1):
                eng.wait_ge(sem("out_summed"), done("out", ph - 1, b))
            elif ph == SELF1:
                eng.wait_ge(sem("down_summed"), done("down", FFN0, E, b))

        downs = [(k,) + ar for k, ar, _ in steps if k == "down"]

        def down_of(k):
            return at[downs[k]]["mx"] + 1

        ons = [(k,) + ar for k, ar, _ in steps if k in ("ou", "ypv")]

        def on_count(key):
            return ons.index(key) + 1

        ybcs = [(k,) + ar for k, ar, _ in steps if k == "ybc"]

        def ons_before(key):
            reads = [(k, ) + ar for k, ar, _ in steps if k in ("ou", "ypv")]
            if key[0] == "pv":
                mine = ("ou", key[1], key[2])
            else:
                mine = key
            return reads.index(mine)

        block = ctx.enter_context(nc.Block())

        @block.sync
        def _(sp):
            def tokens(t, b):
                return t[b].rearrange("(t p) d -> p t d", p=P)

            sp.dma_start(x[:, 0:QT, :], tokens(a["x"], 0)).then_inc(sem("x_loaded0"), 16)
            sp.dma_start(const[:], a["const"]).then_inc(sem("const_loaded"), 16)
            sp.dma_start(wf[:, 0:PO[0][1]], a["pack0"]).then_inc(sem("pack_loaded"), 16)
            sp.dma_start(const16[:], a["const16"]).then_inc(sem("const16_loaded"), 16)
            for b in range(1, B):
                sp.dma_start(x[:, b * QT:(b + 1) * QT, :], tokens(a["x"], b)).then_inc(sem(f"x_loaded{b}"), 16)
            sp.dma_start(smscale[:], a["smscale"].partition_broadcast(P)).then_inc(sem("small_loaded"), 16)
            sp.dma_start(gbias[:], a["gbias"].partition_broadcast(P)).then_inc(sem("small_loaded"), 16)
            sp.dma_start(b1[:], a["b1"]).then_inc(sem("small_loaded"), 16)
            sp.dma_start(bo[:], a["bo"].partition_broadcast(P)).then_inc(sem("small_loaded"), 16)
            sp.dma_start(maskT[:], a["maskT"]).then_inc(sem("small_loaded"), 16)
            sp.dma_start(wo[:], a["wo"]).then_inc(sem("small_loaded"), 16)
            sp.dma_start(ywo[:], a["ywo"]).then_inc(sem("small_loaded"), 16)
            for n in (1, 2):
                sp.wait_ge(sem("pack_high"), n)
                sp.wait_ge(sem("pack_low"), n)
                sp.dma_start(wf[:, 0:PO[n][1]], a[f"pack{n}"]).then_inc(sem("pack_loaded"), 16)
            for n in range(2 * (E + 1)):
                ly, e = divmod(n, E + 1)
                if n:
                    sp.wait_ge(sem("w1_low"), n)
                sp.dma_start(w1f[:], a["w1"][ly, e]).then_inc(sem("w1_loaded"), 16)
                if n >= 2:
                    sp.wait_ge(sem("down_summed"), B * (n - 1))
                sp.dma_start(w2[:, n % 2], a["w2"][ly, e]).then_inc(sem(f"w2_loaded{n % 2}"), 16)
                sp.dma_start(b2[:, n % 2], a["b2"][ly, e].partition_broadcast(P)).then_inc(sem(f"w2_loaded{n % 2}"), 16)
            for b in range(B):
                sp.wait_ge(sem("down_summed"), done("down", FFN1, E, b))
                sp.dma_start(tokens(a["out"], b), x[:, b * QT:(b + 1) * QT, :]).then_inc(sem("stored"), 16)
            sp.wait_ge(sem("stored"), 16 * B)

        @block.gpsimd
        def _(pool):
            eng = nc.gpsimd

            def split_pack(n):
                pool.wait_ge(sem("pack_loaded"), 16 * (n + 1))
                pool.wait_ge(sem("pack_high"), n + 1)
                m = PO[n][1]
                eng.tensor_tensor(wl[n][:], wf[:, 0:m], wh[n][:], ALU.subtract).then_inc(sem("pack_low"), 1)

            eng.memset(minus_half[:], -0.5).then_inc(sem("half_set"), 1)
            pool.wait_ge(sem("half_set"), 1)
            eng.memset(ones[:], 1.0).then_inc(sem("ones_set"), 1)
            eng.memset(mneg[:], 0.0).then_inc(sem("mneg_cleared"), 1)
            split_pack(0)
            for kind, args, hb in steps:
                if kind == "ln":
                    pool.wait_ge(sem("var_ready"), done(kind, *args))
                    eng.tensor_tensor(rstd[:], veps[:], minus_half[:], ALU.pow).then_inc(sem("rstd_ready"), 1)
                    if args == (SELF0, 0):
                        eng.memset(va[:], 0.0).then_inc(sem("v_cleared"), 1)
                        pool.wait_ge(sem("v_cleared"), 1)
                        eng.memset(va[:, :, :, :, DK:DK + 1].rearrange("p a t h o -> p (a t h) o"), 1.0)\
                           .then_inc(sem("v_ones"), 1)
                    if args == (SELF0, 2):
                        eng.memset(vx[:], 0.0).then_inc(sem("v_cleared"), 1)
                        pool.wait_ge(sem("v_cleared"), 2)
                        eng.memset(vx[:, :, :, DK:DK + 1].rearrange("p b h o -> p (b h) o"), 1.0)\
                           .then_inc(sem("v_ones"), 1)
                        eng.memset(mnegb[:], 0.0).then_inc(sem("mneg_cleared"), 1)
                        eng.memset(mneg1[:], 0.0).then_inc(sem("mneg_cleared"), 1)
                if kind == "proj":
                    ph, b, which = args
                    qk, m = int(which == "k"), B * C if (ph, which) == (CROSS0, "k") else S
                    pool.wait_ge(sem("ch_ready"), done(kind, *args))
                    eng.tensor_tensor(cl[:, qk, 0:m], cf[:, 0:m], ch[:, qk, 0:m], ALU.subtract)\
                       .then_inc(sem("cl_ready"), 1)
                if kind == "ks":
                    ph, n = args
                    helper_read(pool, hb)
                    for j in range(J):
                        eng.tensor_scalar(kz[:, n % NQS, j, :], ks[:], cst("headmask")[:, j:j + 1], 0.0,
                                          ALU.mult, ALU.add).then_inc(sem("kz_ready"), 1)
                if kind == "ks0":
                    g, = args
                    helper_read(pool, hb)
                    for j in range(J):
                        eng.tensor_scalar(kx[:, :, g, j, :], ks[:, 0:B * C].rearrange("p (b c) -> p b c", b=B),
                                          cst("headmask")[:, j:j + 1], 0.0, ALU.mult, ALU.add)\
                           .then_inc(sem("kx_ready"), 1)
                if (kind,) + args in SPLIT_AT:
                    split_pack(SPLIT_AT[(kind,) + args])
                n = split_expert_at(kind, args)
                if n is not None:
                    pool.wait_ge(sem("w1_loaded"), 16 * (n + 1))
                    if n >= 2:
                        ly, e = divmod(n - 2, E + 1)
                        pool.wait_ge(sem("st_filled"), at[("up", (FFN0, FFN1)[ly], e, B - 1)]["st"] + FT)
                    eng.tensor_copy(w1h[:, n % 2, :], w1f[:]).then_inc(sem("w1_high"), 1)
                    pool.wait_ge(sem("w1_high"), n + 1)
                    eng.tensor_tensor(w1l[:, n % 2, :], w1f[:], w1h[:, n % 2, :], ALU.subtract)\
                       .then_inc(sem("w1_low"), 1)

        @block.scalar
        def _(act):
            eng = nc.scalar

            def copy(out, in_):
                return eng.activation(out, in_, ACT.Copy)

            def split_pack(n):
                act.wait_ge(sem("pack_loaded"), 16 * (n + 1))
                copy(wh[n][:], wf[:, 0:PO[n][1]]).then_inc(sem("pack_high"), 1)

            split_pack(0)
            for kind, args, hb in steps:
                key = (kind,) + args
                if kind == "xT":
                    ph, b = args
                    helper_filled(act, hb)
                    copy(xh[:, b, :], mi[:, hb % NMI, :]).then_inc(sem("xh_ready"), 1)
                elif kind == "proj":
                    ph, b, which = args
                    qk, m = int(which == "k"), B * C if (ph, which) == (CROSS0, "k") else S
                    if ph == SELF0:
                        act.wait_ge(sem("roped"), done(*key))
                    else:
                        helper_filled(act, hb)
                        if nth[key]:
                            act.wait_ge(sem("cl_ready"), nth[key])
                        if (ph, which) == (SELF1, "q"):
                            act.wait_ge(sem("small_loaded"), 16 * 7)
                            eng.activation(cf[:, 0:m], mi[:, hb % NMI, 0:m], ACT.Identity, scale=smscale[:, 0:1])\
                               .then_inc(read_sem(hb), 1)
                        else:
                            copy(cf[:, 0:m], mi[:, hb % NMI, 0:m]).then_inc(read_sem(hb), 1)
                        helper_read(act, hb)
                    copy(ch[:, qk, 0:m], cf[:, 0:m]).then_inc(sem("ch_ready"), 1)
                elif kind == "v":
                    ph, b = args
                    helper_filled(act, hb)
                    act.wait_ge(sem("v_cleared"), 1)
                    copy(va[:, b % 2, :, :, 0:DK].rearrange("p t h d -> p (t h) d"),
                         mi[:, hb % NMI, :].rearrange("p (a d) -> p a d", d=DK)).then_inc(read_sem(hb), 1)
                elif kind == "v0":
                    b, = args
                    helper_filled(act, hb)
                    act.wait_ge(sem("v_cleared"), 2)
                    copy(vx[:, b, :, 0:DK], mi[0:C, hb % NMI, 0:D].rearrange("p (a d) -> p a d", d=DK))\
                        .then_inc(read_sem(hb), 1)
                elif kind == "ks":
                    helper_filled(act, hb)
                    act.wait_ge(sem("const_loaded"), 16)
                    if nth[key]:
                        act.wait_ge(sem("kz_ready"), J * nth[key])
                    eng.activation(ks[:], mi[:, hb % NMI, :], ACT.Identity, bias=cst("onerow")).then_inc(read_sem(hb), 1)
                elif kind == "ks0":
                    g, = args
                    helper_filled(act, hb)
                    if g:
                        act.wait_ge(sem("kx_ready"), J * g)
                    else:
                        act.wait_ge(sem("kz_ready"), J * B * G)
                    copy(ks[:, 0:B * C], mi[:, hb % NMI, 0:B * C]).then_inc(read_sem(hb), 1)
                elif kind == "qs":
                    ph, n = args
                    helper_filled(act, hb)
                    copy(qs[:, n % NQS, :], mi[:, hb % NMI, :]).then_inc(read_sem(hb), 1)
                elif kind == "mT" and args[0] == CROSS0:
                    helper_filled(act, hb)
                    copy(mtb[:, args[1] % 2, :], mi[:, hb % NMI, :]).then_inc(read_sem(hb), 1)
                elif kind == "ymT":
                    helper_filled(act, hb)
                    copy(mt1[:], mi[:, hb % NMI, :]).then_inc(read_sem(hb), 1)
                elif kind in ("sc", "ysc"):
                    u, t = at[key]["st"], at[key]["pt"]
                    ph = args[0] if kind == "sc" else CROSS1
                    rows = P if ph in (SELF0, SELF1) else C
                    scale = {SELF0: DK ** -0.5, CROSS0: DK ** -0.5, SELF1: 1.0, CROSS1: DH ** -0.5}[ph]
                    act.wait_ge(sem("st_filled"), u + 1)
                    if t >= NPT:
                        product, reader = pt_reader[t - NPT]
                        if reader[0] == "ypv":
                            helper_filled(act, helper_of[reader])
                        else:
                            act.wait_ge(sem("pv_done"), product + 1)
                    eng.activation(pt[0:rows, t % NPT, :], st[0:rows, u % NST, :], ACT.Exp, scale=scale)\
                       .then_inc(sem("st_read"), 1)
                elif kind == "ou":
                    ph, n = args
                    act.wait_ge(sem("pv_done"), at[key]["pv"])
                    copy(ou[:], pv[:]).then_inc(sem("pv_read"), 1)
                elif kind == "outT":
                    helper_filled(act, hb)
                    copy(onT[:], mi[:, hb % NMI, :]).then_inc(read_sem(hb), 1)
                elif kind == "ypv":
                    b, hp = args
                    act.wait_ge(sem("pv_done"), at[key]["pv"] + 1)
                    if nth[key] >= 2:
                        helper_read(act, helper_of[ybcs[nth[key] - 2]])
                    copy(ou1[:, hp % 2, :], pv[:]).then_inc(sem("pv_read"), 1)
                elif kind == "yk":
                    h, = args
                    helper_filled(act, hb)
                    copy(kA[0:DH, h].rearrange("p b c -> p (b c)"), mi[0:DH, hb % NMI, 0:B * C]).then_inc(sem("kh_ready"), 1)
                    copy(kB[DH:P, h].rearrange("p b c -> p (b c)"), mi[DH:P, hb % NMI, 0:B * C]).then_inc(sem("kh_ready"), 1)
                elif kind == "yv":
                    b, = args
                    helper_filled(act, hb)
                    copy(vy[:, b].rearrange("p h d -> p (h d)"), mi[0:C, hb % NMI, :]).then_inc(read_sem(hb), 1)
                elif kind == "yq":
                    b, h = args
                    helper_filled(act, hb)
                    copy(qh2[:, b % 2, h, :], mi[:, hb % NMI, :]).then_inc(sem("qh_ready"), 1)
                elif kind == "soft":
                    act.wait_ge(sem("logits_shifted"), done(*key))
                    eng.activation(lg[:], lg[:], ACT.Exp).then_inc(sem("logits_exp"), 1)
                elif kind == "up":
                    ph, e, tb = args
                    n = EXPERT[ph] + e
                    act.wait_ge(sem("small_loaded"), 16 * 7)
                    if nth[key] >= 2:
                        act.wait_ge(sem("mx_filled"), down_of(nth[key] - 2))
                    for ft in range(FT):
                        u = at[key]["st"] + ft
                        act.wait_ge(sem("st_filled"), u + 1)
                        eng.activation(hid[:, nth[key] % 2, ft, :], st[:, u % NST, :], ACT.Gelu_apprx_tanh,
                                       bias=b1[:, n // (E + 1), e, ft:ft + 1]).then_inc(sem("st_read"), 1)
                if key in SPLIT_AT:
                    split_pack(SPLIT_AT[key])

        @block.tensor
        def _(pe):
            mm = nc.tensor.matmul
            loaded = set()

            def once(name, value):
                if (name, value) not in loaded:
                    loaded.add((name, value))
                    pe.wait_ge(sem(name), value)

            def helper_free(hb):
                if hb >= NMI:
                    helper_read(pe, hb - NMI)

            def st_free(u):
                if u >= NST:
                    pe.wait_ge(sem("st_read"), u - NST + 1)

            def mx_free(u):
                if u >= NMX:
                    pe.wait_ge(sem("mx_read"), u - NMX + 1)

            def three(out, lh, ll, rh, rl, start=True, stop=True):
                mm(out, lh, rh, start=start, stop=False)
                mm(out, lh, rl, start=False, stop=False)
                return mm(out, ll, rh, start=False, stop=stop)

            once("pack_low", 1)
            once("const16_loaded", 16)
            once("const_loaded", 16)
            for kind, args, hb in steps:
                key = (kind,) + args
                o = mi[:, hb % NMI, :]
                if kind == "xT":
                    ph, b = args
                    pe.wait_ge(sem("xn_ready"), done(*key))
                    helper_free(hb)
                    for t in range(QT):
                        last = nc.tensor.transpose(o[:, tile(t)], xn[:, nth[key] % 2, t, :], cst("ident"))
                    last.then_inc(sem("helper_filled"), 1)
                elif kind == "proj":
                    ph, b, which = args
                    once("pack_low", needs_pack[ph])
                    if (ph, which) == (CROSS0, "k"):
                        helper_free(hb)
                        three(o[:, 0:B * C], w("xwk0"), w("xwk0", 1), w("ctx"), w("ctx", 1)).then_inc(sem("helper_filled"), 1)
                    else:
                        helper_read(pe, helper_of[("xT", ph, b)])
                        name = (WQ if which == "q" else WK)[ph]
                        names = [name, name[:2] + "p0"] if ph == SELF0 else [name]
                        for k, nm in enumerate(names):
                            helper_free(hb + k)
                            three(mi[:, (hb + k) % NMI, :], w(nm), w(nm, 1), xh[:, b], xl[:, b])\
                                .then_inc(sem("helper_filled"), 1)
                elif kind == "v":
                    ph, b = args
                    helper_read(pe, helper_of[("xT", ph, b)])
                    helper_free(hb)
                    for t in range(QT):
                        last = three(o[:, tile(t)], xh[:, b, tile(t)], xl[:, b, tile(t)], w(WV[ph]), w(WV[ph], 1))
                    last.then_inc(sem("helper_filled"), 1)
                elif kind == "v0":
                    b, = args
                    helper_free(hb)
                    cb = slice(b * C, (b + 1) * C)
                    three(o[0:C, 0:D], w("ctx", 0, cb), w("ctx", 1, cb), w("xwv0"), w("xwv0", 1))\
                        .then_inc(sem("helper_filled"), 1)
                elif kind in ("ks", "ks0", "qs"):
                    if kind == "ks0":
                        g, m, proj = args[0], B * C, ("proj", CROSS0, 0, "k")
                    else:
                        b, g = divmod(args[1], G)
                        m, proj = S, ("proj", args[0], b, kind[0])
                    pe.wait_ge(sem("cl_ready"), done(*proj))
                    helper_free(hb)
                    c = kind[0]
                    mm(o[:, 0:m], sel(f"sel{c}h", g), ch[:, int(c == "k"), 0:m], start=True, stop=False)
                    mm(o[:, 0:m], sel(f"sel{c}l", g), cl[:, int(c == "k"), 0:m], start=False, stop=True)\
                        .then_inc(sem("helper_filled"), 1)
                elif kind == "max":
                    ph, n, qt, j = args
                    u = at[key]["mx"]
                    b, g = divmod(n, G)
                    helper_read(pe, helper_of[("qs", ph, n)])
                    lhs = qs[:, n % NQS, tile(qt)]
                    if ph == CROSS0:
                        pe.wait_ge(sem("kx_ready"), J * G)
                        once("mask_ready", 1)
                        mx_free(u)
                        mm(mx[:, u % NMX, 0:J * C], lhs, kx[:, b, g].rearrange("p j c -> p (j c)"), start=True, stop=False)
                        mm(mx[:, u % NMX, 0:J * C], maskb[:, tile(qt)], c16("irep")[0:C, :], start=False, stop=True)\
                            .then_inc(sem("mx_filled"), 1)
                    else:
                        pe.wait_ge(sem("kz_ready"), J * done("ks", ph, n))
                        mx_free(u)
                        mm(mx[:, u % NMX, :], lhs, kz[:, n % NQS, j, :], start=True, stop=True).then_inc(sem("mx_filled"), 1)
                elif kind == "mT":
                    ph, n = args
                    last_max = ("max", ph, n, QT - 1, 0 if ph == CROSS0 else J - 1)
                    pe.wait_ge(sem("mx_read"), at[last_max]["mx"] + 1)
                    helper_free(hb)
                    src = mnegb if ph == CROSS0 else mneg
                    for t in range(QT):
                        last = mm(o[:, tile(t)], src[:, n % 2, t, :], c16("id16"), start=True, stop=True)
                    last.then_inc(sem("helper_filled"), 1)
                elif kind == "sc":
                    ph, n, kt, j = args
                    b, g = divmod(n, G)
                    u = at[key]["st"]
                    helper_read(pe, helper_of[("mT", ph, n)])
                    st_free(u)
                    if ph == CROSS0:
                        out = st[0:C, u % NST, :]
                        mm(out, kx[:, b, g, j, :], qs[:, n % NQS, :], start=True, stop=False)
                        mm(out, c16("id16")[0:C, 0:C], maskb[:], start=False, stop=False)
                        mm(out, c16("selm0")[:, j * C:(j + 1) * C], mtb[:, n % 2, :], start=False, stop=True)\
                            .then_inc(sem("st_filled"), 1)
                    else:
                        mm(st[:, u % NST, :], kz[:, n % NQS, j, tile(kt)], qs[:, n % NQS, :], start=True, stop=True)\
                            .then_inc(sem("st_filled"), 1)
                elif kind == "pv":
                    ph, n, kt = args
                    b, g = divmod(n, G)
                    s_last = ("sc", ph, n, kt, J - 1)
                    pe.wait_ge(sem("st_read"), at[s_last]["st"] + 1)
                    once("v_ones", 2 if ph == CROSS0 else 1)
                    if kt == 0:
                        if ph == CROSS0:
                            helper_read(pe, helper_of[("v0", b)])
                        else:
                            helper_read(pe, helper_of[("v", ph, b)])
                        if n or ph != SELF0:
                            pe.wait_ge(sem("pv_read"), ons_before(key))
                    for j in range(J):
                        t = (at[s_last]["pt"] - (J - 1) + j) % NPT
                        out = pv[32 * j:32 * j + 32, :]
                        if ph == CROSS0:
                            last = mm(out, vx[:, b, J * g + j, :], pt[0:C, t, :], start=True, stop=True)
                        else:
                            last = mm(out, va[:, b % 2, kt, J * g + j, :], pt[:, t, :], start=kt == 0, stop=kt == QT - 1)
                    last.then_inc(sem("pv_done"), 1)
                elif kind == "sb":
                    ph, n = args
                    pe.wait_ge(sem("pv_read"), on_count(("ou",) + args))
                    helper_free(hb)
                    for t in range(QT):
                        last = nc.tensor.transpose(o[:, tile(t)], ou[:, tile(t)], cst("ident"))
                    last.then_inc(sem("helper_filled"), 1)
                elif kind == "outT":
                    ph, b = args
                    helper_read(pe, helper_of[("sb", ph, b * G + G - 1)])
                    helper_free(hb)
                    for t in range(QT):
                        last = nc.tensor.transpose(o[:, tile(t)], ont[:, b % 2, t, :], cst("ident"))
                    last.then_inc(sem("helper_filled"), 1)
                elif kind == "ybc":
                    b, hp = args
                    pe.wait_ge(sem("rce_ready"), done(*key))
                    helper_free(hb)
                    for t in range(QT):
                        last = nc.tensor.transpose(o[:, tile(t)], rce[:, hp % 2, tile(t)], cst("ident"))
                    last.then_inc(sem("helper_filled"), 1)
                elif kind == "out":
                    ph, b = args
                    helper_read(pe, helper_of[("ybc", b, HP - 1) if ph == CROSS1 else ("outT", ph, b)])
                    once("small_loaded", 16 * 7)
                    helper_free(hb)
                    for t in range(QT):
                        if ph != CROSS1:
                            last = mm(o[:, tile(t)], onT[:, tile(t)], wo[:, WO[ph], :], start=True, stop=True)
                            continue
                        for hp in range(HP):
                            last = mm(o[:, tile(t)], on[:, b % 2, hp, tile(t)], ywo[:, hp, :],
                                      start=hp == 0, stop=hp == HP - 1)
                    last.then_inc(sem("helper_filled"), 1)
                elif kind == "yk":
                    h, = args
                    once("pack_low", 3)
                    helper_free(hb)
                    cut = slice(h * P, (h + 1) * P)
                    three(o[:, 0:B * C], w("ywk", 0, cut), w("ywk", 1, cut), w("ctx"), w("ctx", 1))\
                        .then_inc(sem("helper_filled"), 1)
                elif kind == "yv":
                    b, = args
                    helper_free(hb)
                    cb = slice(b * C, (b + 1) * C)
                    three(o[0:C, :], w("ctx", 0, cb), w("ctx", 1, cb), w("ywv"), w("ywv", 1)).then_inc(sem("helper_filled"), 1)
                elif kind == "yq":
                    b, h = args
                    helper_read(pe, helper_of[("xT", CROSS1, b)])
                    helper_free(hb)
                    cut = slice(h * P, (h + 1) * P)
                    three(o, w("ywq", 0, cut), w("ywq", 1, cut), xh[:, b], xl[:, b]).then_inc(sem("helper_filled"), 1)
                elif kind == "ymax":
                    b, h = args
                    u = at[key]["mx"]
                    helper_read(pe, helper_of[("yk", h)])
                    helper_read(pe, helper_of[("yq", b, h)])
                    mx_free(u)
                    for t in range(QT):
                        out = mx[:, u % NMX, t * C:(t + 1) * C]
                        mm(out, qh2[:, b % 2, h, tile(t)], kA[:, h, b, :], start=True, stop=False)
                        last = mm(out, ql2[:, b % 2, h, tile(t)], kB[:, h, b, :], start=False, stop=True)
                    last.then_inc(sem("mx_filled"), 1)
                elif kind == "ymT":
                    b, = args
                    pe.wait_ge(sem("mx_read"), at[("ymax", b, H1 - 1)]["mx"] + 1)
                    helper_free(hb)
                    for t in range(QT):
                        last = mm(o[:, tile(t)], mneg1[:, b % 2, t, :], c16("id16"), start=True, stop=True)
                    last.then_inc(sem("helper_filled"), 1)
                elif kind == "ysc":
                    b, h = args
                    u = at[key]["st"]
                    helper_read(pe, helper_of[("ymT", b)])
                    st_free(u)
                    out = st[0:C, u % NST, :]
                    mm(out, kA[:, h, b, :], qh2[:, b % 2, h, :], start=True, stop=False)
                    mm(out, kB[:, h, b, :], ql2[:, b % 2, h, :], start=False, stop=False)
                    mm(out, c16("selm1")[:, h * C:(h + 1) * C], mt1[:], start=False, stop=True).then_inc(sem("st_filled"), 1)
                elif kind == "ypv":
                    b, hp = args
                    s_last = ("ysc", b, 2 * hp + 1)
                    helper_read(pe, helper_of[("yv", b)])
                    pe.wait_ge(sem("st_read"), at[s_last]["st"] + 1)
                    pe.wait_ge(sem("pv_read"), ons_before(key))
                    helper_free(hb)
                    for i2 in range(2):
                        t = (at[s_last]["pt"] - 1 + i2) % NPT
                        r = slice(DH * i2, DH * i2 + DH)
                        last = mm(pv[r, :], vy[:, b, 2 * hp + i2, :], pt[0:C, t, :], start=True, stop=True)
                    last.then_inc(sem("pv_done"), 1)
                    for i2 in range(2):
                        t = (at[s_last]["pt"] - 1 + i2) % NPT
                        for q in range(QT):
                            c = 2 * q + i2
                            last = mm(o[:, c:c + 1], pt[0:C, t, tile(q)], ones[0:C, 0:1], start=True, stop=True)
                    last.then_inc(sem("helper_filled"), 1)
                elif kind == "logits":
                    ph, = args
                    helper_free(hb)
                    name = "gate0" if ph == FFN0 else "gate1"
                    for b in range(B):
                        helper_read(pe, helper_of[("xT", ph, b)])
                        for t in range(QT):
                            c = (b * QT + t) * E
                            last = three(o[:, c:c + E], xh[:, b, tile(t)], xl[:, b, tile(t)], w(name), w(name, 1))
                    last.then_inc(sem("helper_filled"), 1)
                elif kind == "bit":
                    k, = args
                    pe.wait_ge(sem("part_ready"), done(*key))
                    helper_free(hb)
                    mm(o[:, 0:3], ones[:], part[:], start=True, stop=True).then_inc(sem("helper_filled"), 1)
                elif kind == "choose":
                    pe.wait_ge(sem("part_ready"), done("bit", 0) + 1)
                    helper_free(hb)
                    flat = t1[:].rearrange("p e t -> p (e t)")
                    mm(o[:, 0:1], ones[:], part[:, 0:1], start=True, stop=True)
                    mm(o[:, P:2 * P], ones[:], flat, start=True, stop=True)
                    mm(o[:, 2 * P:3 * P], cst("tri"), flat, start=True, stop=True).then_inc(sem("helper_filled"), 1)
                elif kind == "up":
                    ph, e, tb = args
                    n = EXPERT[ph] + e
                    once("w1_low", n + 1)
                    for ft in range(FT):
                        u = at[key]["st"] + ft
                        st_free(u)
                        c = tile(ft)
                        three(st[:, u % NST, :], w1h[:, n % 2, c], w1l[:, n % 2, c], xh[:, tb], xl[:, tb])\
                            .then_inc(sem("st_filled"), 1)
                elif kind == "down":
                    ph, e, tb = args
                    n = EXPERT[ph] + e
                    u = at[key]["mx"]
                    up = ("up",) + args
                    once(f"w2_loaded{n % 2}", 32 * (n // 2 + 1))
                    pe.wait_ge(sem("st_read"), at[up]["st"] + FT)
                    mx_free(u)
                    for t in range(QT):
                        for ft in range(FT):
                            last = mm(mx[:, u % NMX, tile(t)], hid[:, nth[up] % 2, ft, tile(t)], w2[:, n % 2, ft, :],
                                      start=ft == 0, stop=ft == FT - 1)
                    last.then_inc(sem("mx_filled"), 1)

        @block.vector
        def _(dve):
            eng = nc.vector
            chain = [0]

            def link(ins, wait=True):
                chain[0] += 1
                ins.then_inc(sem("dve_chain"), 1)
                if wait:
                    linked()

            def linked():
                dve.wait_ge(sem("dve_chain"), chain[0])

            def bc(ap, shape):
                return ap.to_broadcast(shape)

            def over_tiles(ap):
                return ap.unsqueeze(2).to_broadcast([P, NT, E])

            def te(t):
                return t[:].rearrange("p e t -> p t e")

            def over_batch(ap):
                return ap.unsqueeze(1).to_broadcast([P, QT, D])

            for kind, args, hb in steps:
                key = (kind,) + args
                o = mi[:, hb % NMI, :]
                if kind == "ln":
                    ph, b = args
                    k = nth[key]
                    if ph == SELF0:
                        dve.wait_ge(sem(f"x_loaded{b}"), 16)
                    else:
                        summed(dve, ph, b)
                    if k:
                        dve.wait_ge(sem("xn_ready"), k)
                    for t in range(QT):
                        link(eng.bn_stats(stats[:, t, :], x[:, b * QT + t, :]), t == QT - 1)
                    for t in range(QT):
                        link(eng.bn_aggr(mv[:, t, :], stats[:, t, :]), t == QT - 1)
                    eng.tensor_scalar(veps[:], mv[:, :, 1], EPS, None, ALU.add).then_inc(sem("var_ready"), 1)
                elif kind == "ln2":
                    ph, b = args
                    k = nth[key]
                    dve.wait_ge(sem("rstd_ready"), k + 1)
                    if k >= 2:
                        helper_filled(dve, helper_of[("xT",) + norms[k - 2]])
                    for t in range(QT):
                        last = eng.tensor_scalar(xn[:, k % 2, t, :], x[:, b * QT + t, :], mv[:, t, 0:1], rstd[:, t:t + 1],
                                                 ALU.subtract, ALU.mult)
                    last.then_inc(sem("xn_ready"), 1)
                elif kind == "xT":
                    ph, b = args
                    dve.wait_ge(sem("xh_ready"), done(*key))
                    helper_filled(dve, hb)
                    eng.tensor_tensor(xl[:, b, :], o, xh[:, b, :], ALU.subtract).then_inc(read_sem(hb), 1)
                    if ph == FFN1:
                        dve.wait_ge(sem("xn_ready"), done(*key))
                        xb = x[:, b * QT:(b + 1) * QT, :]
                        link(eng.tensor_tensor(xb, xb, xn[:, nth[key] % 2], ALU.add))
                elif kind == "proj" and args[0] == SELF0:
                    ph, b, which = args
                    helper_filled(dve, hb + 1)
                    dve.wait_ge(sem("const_loaded"), 16)
                    if nth[key]:
                        dve.wait_ge(sem("roped"), nth[key])
                    eng.tensor_tensor(rope[:, 0], o, cst("cos"), ALU.mult).then_inc(read_sem(hb), 1)
                    eng.tensor_tensor(rope[:, 1], mi[:, (hb + 1) % NMI, :], cst("sin"), ALU.mult).then_inc(read_sem(hb + 1), 1)
                    helper_read(dve, hb)
                    helper_read(dve, hb + 1)
                    if nth[key]:
                        dve.wait_ge(sem("cl_ready"), nth[key])
                    eng.tensor_tensor(cf[:], rope[:, 0], rope[:, 1], ALU.add).then_inc(sem("roped"), 1)
                elif kind == "max":
                    ph, n, qt, j = args
                    u = at[key]["mx"]
                    dve.wait_ge(sem("mx_filled"), u + 1)
                    dve.wait_ge(sem("mneg_cleared"), 3 if ph == CROSS0 else 1)
                    if ph == CROSS0:
                        eng.tensor_reduce(mnegb[:, n % 2, qt, MROW::32],
                                          mx[:, u % NMX, 0:J * C].rearrange("p (j c) -> p j c", j=J),
                                          AX.X, ALU.max, negate=True).then_inc(sem("mx_read"), 1)
                    else:
                        r = 32 * j + MROW
                        eng.tensor_reduce(mneg[:, n % 2, qt, r:r + 1], mx[:, u % NMX, :], AX.X, ALU.max, negate=True)\
                           .then_inc(sem("mx_read"), 1)
                elif kind == "ymax":
                    b, h = args
                    u = at[key]["mx"]
                    dve.wait_ge(sem("mx_filled"), u + 1)
                    eng.tensor_reduce(mneg1[:, b % 2, :, h], mx[:, u % NMX, 0:QT * C].rearrange("p (t c) -> p t c", t=QT),
                                      AX.X, ALU.max, negate=True).then_inc(sem("mx_read"), 1)
                elif kind == "mT" and args[0] != CROSS0:
                    ph, n = args
                    helper_filled(dve, hb)
                    eng.tensor_tensor(qs[:, n % NQS, :], o, qs[:, n % NQS, :], ALU.add).then_inc(read_sem(hb), 1)
                elif kind == "sb":
                    ph, n = args
                    b, g = divmod(n, G)
                    helper_filled(dve, hb)
                    heads = o.rearrange("p (t j r) -> p t j r", t=QT, j=J)
                    r4 = rc[:, n % 2, :].rearrange("p (t j) -> p t j", t=QT)
                    link(eng.reciprocal(r4, heads[:, :, :, DK]))
                    eng.tensor_tensor(ont[:, b % 2, :, g * 32:(g + 1) * 32].rearrange("p t (j d) -> p t j d", j=J),
                                      heads[:, :, :, 0:DK], r4.unsqueeze(3).to_broadcast([P, QT, J, DK]), ALU.mult)\
                       .then_inc(read_sem(hb), 1)
                elif kind == "ypv":
                    b, hp = args
                    helper_filled(dve, hb)
                    if nth[key]:
                        dve.wait_ge(sem("rce_ready"), nth[key])
                    eng.reciprocal(rc[:, hp % 2, 0:2 * QT], o[:, 0:2 * QT]).then_inc(read_sem(hb), 1)
                    helper_read(dve, hb)
                    if nth[key] >= 2:
                        helper_filled(dve, helper_of[ybcs[nth[key] - 2]])
                    eng.tensor_copy(rce[:, hp % 2, :].rearrange("p (c k) -> p c k", c=2 * QT),
                                    rc[:, hp % 2, 0:2 * QT].unsqueeze(2).to_broadcast([P, 2 * QT, DH]))\
                       .then_inc(sem("rce_ready"), 1)
                elif kind == "ybc":
                    b, hp = args
                    helper_filled(dve, hb)
                    dve.wait_ge(sem("pv_read"), on_count(("ypv", b, hp)))
                    eng.tensor_tensor(on[:, b % 2, hp, :], o, ou1[:, hp % 2, :], ALU.mult).then_inc(read_sem(hb), 1)
                elif kind == "out":
                    ph, b = args
                    helper_filled(dve, hb)
                    xb = x[:, b * QT:(b + 1) * QT, :]
                    eng.tensor_tensor(xb, o.rearrange("p (t d) -> p t d", t=QT), xb, ALU.add).then_inc(read_sem(hb), 1)
                    helper_read(dve, hb)
                    if ph in (CROSS0, CROSS1):
                        dve.wait_ge(sem("small_loaded"), 16 * 7)
                        eng.tensor_tensor(xb, xb, over_batch(bo[:, int(ph == CROSS1), :]), ALU.add)\
                           .then_inc(sem("out_summed"), 1)
                    else:
                        dve.sem_inc(sem("out_summed"), 1)
                elif kind == "yk":
                    h, = args
                    dve.wait_ge(sem("kh_ready"), 2 * (h + 1))
                    lo, hi = slice(0, DH), slice(DH, P)
                    m = lambda t, r: t[r, h].rearrange("p b c -> p (b c)")
                    link(eng.tensor_tensor(m(kA, hi), mi[hi, hb % NMI, 0:B * C], m(kB, hi), ALU.subtract), False)
                    eng.tensor_tensor(m(kB, lo), mi[lo, hb % NMI, 0:B * C], m(kA, lo), ALU.subtract).then_inc(read_sem(hb), 1)
                elif kind == "yq":
                    b, h = args
                    dve.wait_ge(sem("qh_ready"), done(*key))
                    eng.tensor_tensor(ql2[:, b % 2, h, :], o, qh2[:, b % 2, h, :], ALU.subtract).then_inc(read_sem(hb), 1)
                elif kind == "logits":
                    ph, = args
                    helper_filled(dve, hb)
                    src = o[:, 0:NT * E].rearrange("p (t e) -> p t e", t=NT)
                    if ph == FFN0:
                        eng.tensor_copy(lg[:], src).then_inc(read_sem(hb), 1)
                    else:
                        eng.tensor_tensor(lg[:], src, gbias[:].unsqueeze(1).to_broadcast([P, NT, E]), ALU.add)\
                           .then_inc(read_sem(hb), 1)
                    helper_read(dve, hb)
                elif kind == "soft":
                    ph, = args
                    link(eng.tensor_reduce(sm[:], lg[:], AX.X, ALU.max))
                    eng.tensor_tensor(lg[:], lg[:], over_tiles(sm[:]), ALU.subtract).then_inc(sem("logits_shifted"), 1)
                    dve.wait_ge(sem("logits_exp"), done(*key))
                    link(eng.tensor_reduce(rs[:], lg[:], AX.X, ALU.add))
                    link(eng.reciprocal(rs[:], rs[:]))
                    link(eng.tensor_tensor(te(pr), lg[:], over_tiles(rs[:]), ALU.mult))
                    if ph == FFN0:
                        link(eng.memset(thr[:], 0))
                elif kind == "bit":
                    k, = args
                    for v in range(3):
                        link(eng.tensor_scalar(cand[:, v:v + 1], thr[:], (v + 1) << k, None, ALU.bitwise_or), v == 2)
                    for v in range(3):
                        last = eng.tensor_scalar((t0, t1, t2)[v][:], pr[:], cand[:, v:v + 1].bitcast(F32), None,
                                                 ALU.is_ge, ALU.add, accum_out=part[:, v:v + 1])
                    last.then_inc(sem("part_ready"), 1)
                    helper_filled(dve, hb)
                    eng.tensor_scalar(passed[:], o[:, 0:3], float(TOPK), None, ALU.is_ge, ALU.add, accum_out=left[:])\
                       .then_inc(read_sem(hb), 1)
                    helper_read(dve, hb)
                    link(eng.tensor_scalar(inc[:], left[:], float(1 << k), None, ALU.mult))
                    link(eng.tensor_tensor(thr[:], thr[:], inc[:], ALU.bitwise_or))
                elif kind == "choose":
                    tv = thr[:].bitcast(F32)
                    link(eng.tensor_scalar(t1[:], pr[:], tv, None, ALU.is_equal))
                    eng.tensor_scalar(t0[:], pr[:], tv, None, ALU.is_gt, ALU.add, accum_out=part[:, 0:1])\
                       .then_inc(sem("part_ready"), 1)
                    helper_filled(dve, hb)
                    flat = lambda t: t[:].rearrange("p e t -> p (e t)")
                    link(eng.tensor_scalar(left[:], o[:, 0:1], -1.0, float(TOPK), ALU.mult, ALU.add))
                    link(eng.tensor_tensor_scan(cum[:], ones[:], o[:, P:2 * P], 0.0, ALU.mult, ALU.add))
                    link(eng.tensor_tensor(cum[:], cum[:], o[:, P:2 * P], ALU.subtract))
                    eng.tensor_tensor(cum[:], cum[:], o[:, 2 * P:3 * P], ALU.add).then_inc(read_sem(hb), 1)
                    helper_read(dve, hb)
                    link(eng.scalar_tensor_tensor(flat(t2), cum[:], left[:, 0:1], flat(t1), ALU.is_le, ALU.mult))
                    link(eng.tensor_tensor(t0[:], t0[:], t2[:], ALU.add))
                    link(eng.tensor_tensor(gate[:], t0[:], pr[:], ALU.mult))
                elif kind == "top2":
                    pick = cst("pick").unsqueeze(1).to_broadcast([P, NT, E])

                    def first_max(out, vals, m):
                        link(eng.tensor_reduce(m, te(vals), AX.X, ALU.max))
                        link(eng.tensor_tensor(te(out), te(vals), over_tiles(m), ALU.is_equal))
                        link(eng.tensor_tensor(te(out), te(out), pick, ALU.mult))
                        link(eng.tensor_reduce(rs[:], te(out), AX.X, ALU.max))
                        link(eng.tensor_tensor(te(out), te(out), over_tiles(rs[:]), ALU.is_equal))

                    first_max(t0, pr, sm[:])
                    link(eng.scalar_tensor_tensor(t1[:].rearrange("p e t -> p (e t)"), t0[:].rearrange("p e t -> p (e t)"),
                                                  -2.0, pr[:].rearrange("p e t -> p (e t)"), ALU.mult, ALU.add))
                    first_max(t2, t1, left16[:])
                    link(eng.tensor_tensor(sm[:], sm[:], left16[:], ALU.add))
                    link(eng.tensor_scalar(sm[:], sm[:], 1e-9, None, ALU.add))
                    link(eng.reciprocal(sm[:], sm[:]))
                    link(eng.tensor_tensor(t0[:], t0[:], t2[:], ALU.add))
                    link(eng.tensor_tensor(t0[:], t0[:], pr[:], ALU.mult))
                    link(eng.tensor_tensor(te(gate), te(t0), over_tiles(sm[:]), ALU.mult))
                elif kind == "down":
                    ph, e, tb = args
                    n = EXPERT[ph] + e
                    u = at[key]["mx"]
                    dve.wait_ge(sem("mx_filled"), u + 1)
                    dve.wait_ge(sem(f"w2_loaded{n % 2}"), 32 * (n // 2 + 1))
                    if nth[key] >= 1:
                        dve.wait_ge(sem("down_summed"), nth[key])
                    if e == 0:
                        xb = x[:, tb * QT:(tb + 1) * QT, :]
                        eng.tensor_tensor(xb, mx[:, u % NMX, :].rearrange("p (t d) -> p t d", t=QT), xb, ALU.add)\
                           .then_inc(sem("mx_read"), 1)
                        dve.wait_ge(sem("mx_read"), u + 1)
                        eng.tensor_tensor(xb, xb, over_batch(b2[:, n % 2, :]), ALU.add).then_inc(sem("down_summed"), 1)
                        continue
                    for t in range(QT):
                        tt = tb * QT + t
                        last = eng.scalar_tensor_tensor(x[:, tt, :], mx[:, u % NMX, tile(t)], gate[:, e - 1, tt:tt + 1],
                                                        x[:, tt, :], ALU.mult, ALU.add)
                    last.then_inc(sem("mx_read"), 1)
                    dve.wait_ge(sem("mx_read"), u + 1)
                    for t in range(QT):
                        tt = tb * QT + t
                        last = eng.scalar_tensor_tensor(x[:, tt, :], b2[:, n % 2, :], gate[:, e - 1, tt:tt + 1],
                                                        x[:, tt, :], ALU.mult, ALU.add)
                    last.then_inc(sem("down_summed"), 1)
                if key == ("mT", SELF0, 9):
                    dve.wait_ge(sem("small_loaded"), 16 * 7)
                    eng.tensor_scalar(maskb[:], maskT[:], 0.0, NEG, ALU.is_equal, ALU.mult).then_inc(sem("mask_ready"), 1)


def constants():
    import numpy as np
    c = np.zeros((P, NCONST), np.float32)
    h16 = np.zeros((P, NCONST16), np.float16)

    def put(name, v):
        p0, n = CO[name]
        c[:, p0:p0 + n] = v

    def put16(name, v):
        p0, n = CH[name]
        h16[:v.shape[0], p0:p0 + n] = v.reshape(v.shape[0], n)

    put("ident", np.eye(P))
    put("tri", np.triu(np.ones((P, P))))
    put("pick", E - np.arange(E))
    inv = (1.0 / np.float32(10000.0) ** (np.arange(0, DK, 2, dtype=np.float32) / np.float32(DK))).astype(np.float32)
    freqs = np.arange(S, dtype=np.float32)[:, None] * inv[None, :]
    d = np.arange(P) % DK
    ang = freqs[:, d % (DK // 2)].T
    put("cos", np.cos(ang).astype(np.float32))
    put("sin", np.where(d[:, None] < DK // 2, -1, 1) * np.sin(ang).astype(np.float32))
    row = np.arange(P)
    put("onerow", (row % 32 == MROW)[:, None])
    put("headmask", row[:, None] // 32 == np.arange(J)[None, :])
    put16("id16", np.eye(P))
    parts = {"selqh": (0, 1), "selql": (2,), "selkh": (0, 2), "selkl": (1,)}
    for name, ts in parts.items():
        s = np.zeros((P, G, P))
        for g in range(G):
            for j in range(J):
                for t in ts:
                    for k in range(DK):
                        s[DK * (J * g + j) + k, g, 32 * j + DK * t + k] = 1
        put16(name, s)
    put16("irep", np.tile(np.eye(C), (1, J)))
    m0 = np.zeros((P, J, C))
    for j in range(J):
        m0[32 * j + MROW, j] = 1
    put16("selm0", m0)
    m1 = np.zeros((P, H1, C))
    for h in range(H1):
        m1[h, h] = 1
    put16("selm1", m1)
    return c, h16


def kernel(**inputs):
    import numpy as np
    import concourse.bacc as _bacc
    from concourse import mybir as _mybir
    from concourse.bass_utils import run_bass_kernel_spmd as _run

    v = {k: np.asarray(a) for k, a in inputs.items()}
    T = lambda name: v[name].T
    arrays = {"x": v["x"], "maskT": v["mask_1x1xSxS2_ik0"][0, 0].T}
    arrays["const"], arrays["const16"] = constants()
    half = DK // 2
    perm = np.array([DK * h + (2 * d + 1 if d < half else 2 * (d - half)) for h in range(H) for d in range(DK)])
    wq, wk = T("L0_attn_Wq"), T("L0_attn_Wk")
    arrays["pack0"] = np.concatenate([wq, wq[:, perm], wk, wk[:, perm], T("L0_attn_Wv")], axis=1)
    ctx = v["ctx_1024"].transpose(2, 0, 1).reshape(D, B * C)
    arrays["pack1"] = np.concatenate([T("L0_xattn_Wq"), T("L0_xattn_Wk"), T("L0_xattn_Wv"), ctx,
                                      T("L0_ffn_gate_weight")], axis=1)

    def twice(wt):
        return np.repeat(wt.reshape(D, H1, 1, DH), 2, axis=2).reshape(D, 2 * H1 * DH)

    arrays["pack2"] = np.concatenate([T("L1_attn_w_q"), np.tile(T("L1_attn_w_k"), (1, H)), np.tile(T("L1_attn_w_v"), (1, H)),
                                      v["L1_ffn_gate_w"], twice(v["L1_xattn_Wq"]), twice(v["L1_xattn_Wk"]),
                                      v["L1_xattn_Wv"]], axis=1)
    arrays["wo"] = np.stack([T("L0_attn_Wo"), T("L0_xattn_Wo"), T("L1_attn_w_out")], axis=1)
    arrays["ywo"] = v["L1_xattn_Wo"].reshape(HP, P, D).transpose(1, 0, 2)
    arrays["bo"] = np.stack([v["L0_xattn_bo"], v["L1_xattn_bo"]])
    arrays["smscale"] = v["L1_attn_softmax_scale"]
    arrays["gbias"] = v["L1_ffn_gate_b"]
    w1 = [np.concatenate([v["L0_ffn_Ws1"][None], v["L0_ffn_W1"]]), np.concatenate([v["L1_ffn_sh_w1"][None], v["L1_ffn_ew1"]])]
    w2 = [np.concatenate([v["L0_ffn_Ws2"][None], v["L0_ffn_W2"]]), np.concatenate([v["L1_ffn_sh_w2"][None], v["L1_ffn_ew2"]])]
    b1 = [np.concatenate([v["L0_ffn_bs1"][None], v["L0_ffn_b1"]]), np.concatenate([v["L1_ffn_sh_b1"][None], v["L1_ffn_eb1"]])]
    b2 = [np.concatenate([v["L0_ffn_bs2"][None], v["L0_ffn_b2"]]), np.concatenate([v["L1_ffn_sh_b2"][None], v["L1_ffn_eb2"]])]
    arrays["w1"] = np.stack(w1)
    arrays["w2"] = np.stack(w2).reshape(2, E + 1, FT, P, D).transpose(0, 1, 3, 2, 4)
    arrays["b1"] = np.stack(b1).reshape(2, E + 1, FT, P).transpose(3, 0, 1, 2)
    arrays["b2"] = np.stack(b2)

    nc = _bacc.Bacc("TRN2", target_bir_lowering=False, num_devices=1)
    ins, aps = {}, {}
    for name, arr in arrays.items():
        arr = np.ascontiguousarray(arr)
        ins[f"in_{name}"] = arr
        aps[name] = nc.dram_tensor(f"in_{name}", arr.shape, _mybir.dt.from_np(arr.dtype), kind="ExternalInput").ap()
    aps["out"] = nc.dram_tensor("out_x", (B, S, D), F32, kind="ExternalOutput").ap()
    build(nc, aps)
    r = _run(nc, [ins], core_ids=[0])
    return r.results[0]["out_x"]
```

```python
from contextlib import ExitStack

import concourse.bass as bass
from concourse import mybir

ALU = mybir.AluOpType
ACT = mybir.ActivationFunctionType
AX = mybir.AxisListType
F32 = mybir.dt.float32
F16 = mybir.dt.float16
BF16 = mybir.dt.bfloat16
I32 = mybir.dt.int32

P = 128
B = 4
S = 512
D = 128
QT = S // P
NT = B * QT
H = 16
DK = D // H
G = 4
J = H // G
C = 77
H1 = 8
DH = 64
HP = H1 // 2
E = 8
F = 512
FT = F // P
TOPK = B * S * 2
EPS = 1e-5
NEG = -1e20
NB2 = 4
BITS = [28 - 2 * i for i in range(15)]
MROW = 24

NST, NMX, NMI, NPT, NQS = 2, 3, 2, 8, 3

SELF0, CROSS0, FFN0, SELF1, CROSS1, FFN1 = range(6)

PACKS = [
    [("wq0", D), ("wqp0", D), ("wk0", D), ("wkp0", D), ("wv0", D)],
    [("xwq0", D), ("xwk0", D), ("xwv0", D), ("ctx", B * C), ("gate0", E)],
    [("wq1", D), ("wk1", D), ("wv1", D), ("gate1", E),
     ("ywq", 2 * H1 * DH), ("ywk", 2 * H1 * DH), ("ywv", H1 * DH)],
]
CONSTS = ([("ident", P), ("cos", S), ("sin", S), ("onerow", 1), ("headmask", J), ("tri", P), ("pick", E)]
          + [(f"or{k}", 3) for k in BITS])
CONSTS16 = [("id16", P), ("selqh", G * P), ("selql", G * P), ("selkh", G * P), ("selkl", G * P),
            ("irep", J * C), ("selm0", J * C), ("selm1", H1 * C)]


def offsets(cols):
    out, at = {}, 0
    for name, n in cols:
        out[name] = (at, n)
        at += n
    return out, at


CO, NCONST = offsets(CONSTS)
CH, NCONST16 = offsets(CONSTS16)
PO = [offsets(p) for p in PACKS]


def plan():
    steps = []
    helper = [0]

    def put(kind, *a, h=0):
        steps.append((kind, a, helper[0]))
        helper[0] += h

    def norm(ph, b):
        return [(("ln", ph, b), 0), (("ln2", ph, b), 0), (("xT", ph, b), 1)]

    def stream(ph, maxs, scores, products, prep, stacks, following=()):
        N, U = B * G, len(scores(0))
        lead, lag = U + max(U // 4, 2), 2
        events = []

        def on(pos, *xs):
            for x, h in xs:
                events.append((pos, len(events), x, h))

        for n in range(N):
            b, g = divmod(n, G)
            at0 = n * U
            on(at0 - U + U - 1 - (lead - U) + max(U // 8, 1), (("mT", ph, n), 1))
            for x, used in products(n):
                on(at0 + used - 1 + lag, (x, 0))
            end = at0 + U - 1 + lag
            on(end, (("ou", ph, n), 0))
            on(end + max(U // 6, 1), (("sb", ph, n), 1))
            if g == G - 1:
                on(end + U // 3, (("outT", ph, b), 1))
                on(end + U // 2, (("out", ph, b), 1))
                for i, x in enumerate(norm(ph + 1, b)):
                    on(end + U // 2 + 1 + i * max(U // 5, 2), x)
                if b == B - 1:
                    for i, x in enumerate(following):
                        on(at0 - U - U // 2 + 1 + i * (U + U // 2) // (len(following) - 1), x)
            if n + 2 < N:
                st = stacks(n + 2)
                for i, x in enumerate(st):
                    on(at0 - 1 + i * U // 4, x)
            if b + 1 < B and g in (0, 1):
                part = prep(b + 1)[g]
                for i, x in enumerate(part):
                    on(at0 + U // 4 + 1 + i * (U // 2) // len(part), x)
        events.sort()
        flat_max = [x for n in range(N) for x in maxs(n)]
        flat_sc = [x for n in range(N) for x in scores(n)]
        done_max = 0
        out, tail, first_score = [], [], None
        for u in range(-lead, max(N * U, events[-1][0] + 1)):
            if u == N * U + lag:
                tail = [(x, h) for _, _, x, h in events]
                break
            if u == 0:
                first_score = len(out)
            if done_max < len(flat_max):
                out.append((flat_max[done_max], 0))
                done_max += 1
            if 0 <= u < len(flat_sc):
                out.append((flat_sc[u], 0))
            while events and events[0][0] <= u:
                _, _, x, h = events.pop(0)
                out.append((x, h))
        return out[:first_score], out[first_score:], tail

    def cross0_context():
        return ([(("proj", CROSS0, 0, "k"), 1)] + [(("ks0", g), 1) for g in range(G)]
                + [(("v0", b), 1) for b in range(B)])

    def cross1_context():
        return [(("yk", h), 1) for h in range(H1)] + [(("yv", b), 1) for b in range(B)]

    def self_project(ph, b):
        rope = ph == SELF0
        return [(("proj", ph, b, "q"), 1 + rope), (("proj", ph, b, "k"), 1 + rope), (("v", ph, b), 1)]

    def self_head(ph):
        return self_project(ph, 0) + [((k, ph, n), 1) for n in range(2) for k in ("ks", "qs")]

    def self_attention(ph, following=()):
        def prep(b):
            return norm(ph, b) if ph == SELF0 else [], self_project(ph, b)

        return stream(ph,
               maxs=lambda n: [("max", ph, n, qt, j) for qt in range(QT) for j in range(J)],
               scores=lambda n: [("sc", ph, n, kt, j) for kt in range(QT) for j in range(J)],
               products=lambda n: [(("pv", ph, n, kt), J * (kt + 1)) for kt in range(QT)],
               prep=prep, stacks=lambda n: [(("ks", ph, n), 1), (("qs", ph, n), 1)], following=following)

    def cross0():
        ph = CROSS0
        return stream(ph,
               maxs=lambda n: [("max", ph, n, qt, 0) for qt in range(QT)],
               scores=lambda n: [("sc", ph, n, 0, j) for j in range(J)],
               products=lambda n: [(("pv", ph, n, 0), J)],
               prep=lambda b: ([], [(("proj", ph, b, "q"), 1)]), stacks=lambda n: [(("qs", ph, n), 1)])

    def cross0_head():
        return [(("proj", CROSS0, 0, "q"), 1), (("qs", CROSS0, 0), 1), (("qs", CROSS0, 1), 1)]

    def cross1():
        ph = CROSS1
        wait_max, wait_sc = 2, H1 + 3
        out, tail, later = [], [], []

        def put(*x, h=0):
            out.append((x, h))

        for s in range(B * H1 + wait_sc + 3):
            if later:
                put(*later[0][0], h=later[0][1])
                later = later[1:]
            sc = s - wait_sc
            if 0 <= sc < B * H1:
                put("ysc", *divmod(sc, H1))
            if s < B * H1:
                put("yq", *divmod(s, H1), h=1)
            sc -= 1
            if 0 <= sc < B * H1 and sc % 2:
                b, h = divmod(sc, H1)
                put("ypv", b, h // 2)
            if 0 <= s - wait_max < B * H1:
                put("ymax", *divmod(s - wait_max, H1))
            m = s - wait_max - 1
            if 0 <= m < B * H1 and m % H1 == H1 - 1:
                put("ymT", m // H1, h=1)
            sc -= 1
            if 0 <= sc < B * H1 and sc % 2:
                b, h = divmod(sc, H1)
                put("ybc", b, h // 2, h=1)
            if sc >= H1 and sc % H1 == 0:
                b = sc // H1 - 1
                last = [(("out", ph, b), 1)] + norm(FFN1, b)
                if b == B - 1:
                    tail = last
                else:
                    put(*last[0][0], h=last[0][1])
                    later = last[1:]
        return out, tail

    def merge(main, side, every):
        out, side = [], list(side)
        for i, x in enumerate(main):
            out.append(x)
            if i % every == every - 1 and side:
                out.append(side.pop(0))
        return out + side

    def ffn(ph, before, after=()):
        after = list(after)
        routed = [[(("logits", ph), 1), (("soft", ph), 0)]]
        if ph == FFN0:
            for k in BITS:
                routed += [[(("bit", k), 0)], [(("bsum", k), 1)], [(("passed", k), 0)]]
            routed += [[(("choose",), 1)]]
        else:
            routed += [[(("top2",), 0)]]
        context = cross1_context()
        units = ([(e, tb) for e in range(E - 1) for tb in range(B)]
                 + [(e, tb) for tb in range(B) for e in (E - 1, E)])
        pieces = [("up", ph) + units[i] + (ft,) for i in range(2) for ft in range(FT)]
        for i, (e, tb) in enumerate(units):
            for t in range(QT):
                if i + 2 < len(units):
                    pieces.append(("up", ph) + units[i + 2] + (t,))
                pieces.append(("down", ph, e, tb, t))
        before_to = 4 * FT
        routes_from, routes_to = before_to, 2 * FT + 2 * FT * B * (2 if ph == FFN0 else 1) + 1
        pending, norm0_done = {}, None
        for i, x in enumerate(pieces):
            if x[0:3] == ("down", FFN0, 2) and x[4] == 0:
                put("defer", x[3])
            put(*x)
            m, n = len(before) - 1, before_to - 4
            for y in before[m * i // n:m * (i + 1) // n] if i < n else before[-1:] if i == before_to - 1 else ():
                put(*y[0], h=y[1])
            k = i - routes_from
            n = routes_to - routes_from
            if 0 <= k < n:
                for y in routed[len(routed) * k // n:len(routed) * (k + 1) // n]:
                    for z in y:
                        put(*z[0], h=z[1])
            if ph == FFN0:
                _, _, e, tb, t = x if x[0] == "down" else (None, None, None, None, None)
                if e and e < E and t == QT - 1 and tb % 2:
                    for y in context[:1]:
                        put(*y[0], h=y[1])
                    context = context[1:]
                if e == E and t == QT - 1:
                    norms_at = {i + 1: norm(SELF1, tb)[:1], i + 3: norm(SELF1, tb)[1:2], i + 7: norm(SELF1, tb)[2:]}
                    if tb == 0:
                        norm0_done = i + 7
                    pending.update({k: pending.get(k, []) + v for k, v in norms_at.items()})
                for y in pending.pop(i, []):
                    put(*y[0], h=y[1])
                if norm0_done is not None and i > norm0_done:
                    m = len(pieces) - norm0_done - 1
                    j = i - norm0_done - 1
                    for y in after[len(after) * j // m:len(after) * (j + 1) // m]:
                        put(*y[0], h=y[1])
        if ph == FFN0:
            assert not context
        return [y for k in sorted(pending) for y in pending[k]]

    def run(xs):
        for x in xs:
            put(*x[0], h=x[1])

    self0_lead, self0, self0_tail = self_attention(SELF0, cross0_context() + cross0_head())
    cross0_lead, cross0_rest, cross0_tail = cross0()
    self1_lead, self1, self1_tail = self_attention(SELF1)
    cross1_steps, cross1_tail = cross1()
    run(norm(SELF0, 0) + self_head(SELF0) + self0_lead)
    run(self0)
    run(merge(cross0_lead + cross0_rest, self0_tail, 4))
    left = ffn(FFN0, cross0_tail, self_head(SELF1) + self1_lead)
    run(merge(self1, left, 4))
    run(merge(cross1_steps, self1_tail, 4))
    ffn(FFN1, cross1_tail)
    return steps



def build(nc, a):
    steps = plan()

    nth, at, helper_of = {}, {}, {}
    seen = {}
    ring = {"st": 0, "mx": 0, "pt": 0, "pv": 0}
    waiting = []
    pt_reader = {}
    for kind, args, hb in steps:
        key = (kind,) + args
        nth[key] = seen.get(kind, 0)
        seen[kind] = nth[key] + 1
        at[key] = dict(ring)
        helper_of[key] = hb
        if kind in ("sc", "ysc"):
            waiting.append(ring["pt"])
            ring["st"] += 1
            ring["pt"] += 1
        if kind == "up":
            ring["st"] += 1
        if kind in ("max", "ymax", "ypv", "down"):
            ring["mx"] += 1
        if kind in ("pv", "ypv"):
            n = J if kind == "pv" else 2
            for t in waiting[:n]:
                pt_reader[t] = (ring["pv"], key)
            waiting = waiting[n:]
            ring["pv"] += 1
    norms = [args for kind, args, _ in steps if kind == "ln"]
    projs = [args for kind, args, _ in steps if kind == "proj"]

    with ExitStack() as ctx:
        def sb(name, shape, dt=F32):
            return ctx.enter_context(nc.sbuf_tensor(name, shape, dt))

        def ps(name, shape, dt=F32):
            return ctx.enter_context(nc.psum_tensor(name, shape, dt))

        sems = {}

        def sem(name):
            if name not in sems:
                sems[name] = ctx.enter_context(nc.semaphore(name))
            return sems[name]

        st = ps("st", [P, NST, 512])
        mx = ps("mx", [P, NMX, 512])
        pv = ps("pv", [P, 512])
        mi = ps("mi", [P, NMI, 512])

        x = sb("x", [P, NT, D])
        xn = sb("xn", [P, 2, QT, D])
        xh = sb("xh", [P, B, S], F16)
        xl = sb("xl", [P, B, S], F16)
        const = sb("const", [P, NCONST])
        const16 = sb("const16", [P, NCONST16], F16)
        ones = sb("ones", [P, P])
        minus_half = sb("minus_half", [P, QT])
        wf = sb("wf", [P, max(n for _, n in PO)])
        wh = [sb(f"wh{n}", [P, PO[n][1]], F16) for n in range(3)]
        wl = [sb(f"wl{n}", [P, PO[n][1]], F16) for n in range(3)]
        wo = sb("wo", [P, 3, D])
        ywo = sb("ywo", [P, HP, D])
        bo = sb("bo", [P, 2, D])
        smscale = sb("smscale", [P, 1])
        gbias = sb("gbias", [P, E])
        maskT = sb("maskT", [C, S], I32)
        maskb = sb("maskb", [C, S], BF16)
        stats = sb("stats", [P, QT, 6])
        mv = sb("mv", [P, QT, 2])
        veps = sb("veps", [P, QT])
        rstd = sb("rstd", [P, QT])
        rope = sb("rope", [P, 2, S])
        cf = sb("cf", [P, S])
        ch = sb("ch", [P, 2, S], F16)
        cl = sb("cl", [P, 2, S], F16)
        ks = sb("ks", [P, S], F16)
        kz = sb("kz", [P, NQS, J, S], F16)
        qs = sb("qs", [P, NQS, S], F16)
        mneg = sb("mneg", [P, 2, QT, P], F16)
        mnegb = sb("mnegb", [P, 2, QT, P], BF16)
        mneg1 = sb("mneg1", [P, 2, QT, P], F16)
        mtb = sb("mtb", [P, 2, S], BF16)
        mt1 = sb("mt1", [P, S], F16)
        va = sb("va", [P, 2, QT, H, 32])
        nvx, nkx = B * H * 32, B * G * J * C // 2
        cross = sb("cross", [P, nvx + nkx])
        vx = cross[0:C, 0:nvx].rearrange("p (b h r) -> p b h r", b=B, h=H)
        kx = cross[:, nvx:nvx + nkx].bitcast(F16).rearrange("p (b g j c) -> p b g j c", b=B, g=G, j=J)
        vy = sb("vy", [C, B, H1, DH + 1])
        pt = sb("pt", [P, NPT, S])
        ou = sb("ou", [P, S])
        rc = sb("rc", [P, 2, QT * J])
        ont = sb("ont", [P, 2, QT, D])
        onT = sb("onT", [P, S])
        on = sb("on", [P, 2, G, S])
        qh2 = va[:].rearrange("p a t h r -> p (a t h r)").bitcast(F16).rearrange("p (a h s) -> p a h s", a=2, h=H1)
        ql2 = cross[:, 0:H1 * S].bitcast(F16).rearrange("p (a h s) -> p a h s", a=2, h=H1)
        kzf = wf[:].bitcast(F16)
        nk = H1 * B * C
        kA = kzf[:, 0:nk].rearrange("p (h b c) -> p h b c", h=H1, b=B)
        kB = kzf[:, nk:2 * nk].rearrange("p (h b c) -> p h b c", h=H1, b=B)
        w1f = sb("w1f", [P, F])
        w1h = sb("w1h", [P, 2, F], F16)
        w1l = sb("w1l", [P, 2, F], F16)
        w2f = sb("w2f", [P, FT * D])
        w2h = sb("w2h", [P, 2, FT * D], F16)
        w2l = sb("w2l", [P, 2, FT * D], F16)
        b1 = sb("b1", [P, 2, E + 1, FT])
        b2 = sb("b2", [P, NB2, D])
        y1 = kz[:].rearrange("p a j s -> p (a j s)").bitcast(F32)[:, 0:NT * D].rearrange("p (t d) -> p t d", d=D)
        hid = pt[:].rearrange("p (a f) s -> p a f s", a=2)
        on_words = on[:].rearrange("p a g s -> p (a g s)")

        def hidden_part(unit, low):
            words = (cross, cross, on_words)[unit % 3]
            at_word = (unit % 3 % 2 * 2 + low) * FT * S // 2
            return words[:, at_word:at_word + FT * S // 2].bitcast(F16).rearrange("p (f s) -> p f s", f=FT)

        def hidh(unit):
            return hidden_part(unit, 0)

        def hidl(unit):
            return hidden_part(unit, 1)

        lg = sb("lg", [P, NT, E])
        sm = sb("sm", [P, NT])
        rs = sb("rs", [P, NT])
        pr = sb("pr", [P, E, NT])
        gate = sb("gate", [P, E, NT])
        t0 = sb("t0", [P, E, NT])
        t1 = sb("t1", [P, E, NT])
        t2 = sb("t2", [P, E, NT])
        cum = sb("cum", [P, E * NT])
        thr = sb("thr", [P, 1], I32)
        cand = sb("cand", [P, 3], I32)
        inc = sb("inc", [P, 1], I32)
        part = sb("part", [P, 3])
        left = sb("left", [P, 1])
        passed = sb("passed", [P, 3])
        left16 = sb("left16", [P, NT])

        def cst(name):
            p0, n = CO[name]
            return const[:, p0:p0 + n]

        def c16(name):
            p0, n = CH[name]
            return const16[:, p0:p0 + n]

        def sel(name, g):
            p0, _ = CH[name]
            return const16[:, p0 + g * P:p0 + (g + 1) * P]

        where = {name: (n, PO[n][0][name]) for n in range(3) for name, _ in PACKS[n]}

        def w(name, low=False, cut=slice(None)):
            n, (p0, k) = where[name]
            return (wl if low else wh)[n][:, p0:p0 + k][:, cut]

        needs_pack = {SELF0: 1, CROSS0: 2, FFN0: 2, SELF1: 3, CROSS1: 3, FFN1: 3}
        slot_of = {(ph, n): (B * G * i + n) % NQS for i, ph in enumerate((SELF0, CROSS0, SELF1)) for n in range(B * G)}
        WQ = {SELF0: "wq0", CROSS0: "xwq0", SELF1: "wq1"}
        WK = {SELF0: "wk0", CROSS0: "xwk0", SELF1: "wk1"}
        WV = {SELF0: "wv0", SELF1: "wv1"}
        WO = {SELF0: 0, CROSS0: 1, SELF1: 2}
        SPLIT_AT = {("mT", SELF0, 1): 1, ("mT", SELF0, 5): 2}
        EXPERT = {FFN0: 0, FFN1: E + 1}

        def split_expert_at(kind, args):
            if (kind,) + args == ("mT", SELF0, 9):
                return 0
            if (kind,) + args == ("mT", SELF1, 1):
                return E + 1
            if kind == "up" and args[1] < E and args[2:] == (0 if args[1] == E - 1 else 1, 0):
                return EXPERT[args[0]] + args[1] + 1
            return None

        def split_second_at(kind, args):
            if (kind,) + args == ("mT", SELF0, 9):
                return 0
            if (kind,) + args == ("mT", SELF1, 1):
                return E + 1
            if kind == "up" and args[1] < E and args[2:] == (1 if args[1] == E - 1 else 2, 0):
                return EXPERT[args[0]] + args[1] + 1
            return None

        def done(*key):
            return nth[key] + 1

        def helper_read(eng, hb):
            eng.wait_ge(sem(f"helper_read{hb % NMI}"), hb // NMI + 1)

        def helper_filled(eng, hb):
            eng.wait_ge(sem("helper_filled"), hb + 1)

        def read_sem(hb):
            return sem(f"helper_read{hb % NMI}")

        def tile(t, n=1):
            return slice(t * P, (t + n) * P)

        def down_summed(eng, ph, e, b):
            eng.wait_ge(sem("mx_read"), at[("down", ph, e, b, QT - 1)]["mx"] + 1)

        def summed(eng, ph, b):
            if ph == SELF1:
                down_summed(eng, FFN0, E, b)
            else:
                eng.wait_ge(sem("out_summed"), done("out", ph - 1, b))

        downs = [(k,) + ar for k, ar, _ in steps if k == "down"]

        def down_of(k):
            return at[downs[QT * k + QT - 1]]["mx"] + 1

        def parts_of(key, behind):
            i, per_phase = nth[key], FT * B * (E + 1)
            first = i // per_phase * per_phase
            last = i if i == first + per_phase - 1 else i - behind
            return range(max(i - behind, first), last + 1)

        def dve_lows(unit):
            return 1 if unit < 2 * B else FT // 2

        def lows_made(eng, unit):
            n = sum(dve_lows(i) for i in range(unit + 1))
            eng.wait_ge(sem("hidden_low_dve"), n)
            eng.wait_ge(sem("hidden_low_pool"), FT * (unit + 1) - n)

        def hidden_low(engine, eng, tile_no, made):
            unit, ft = divmod(tile_no, FT)
            engine.wait_ge(sem("hidden_high"), tile_no + 1)
            eng.tensor_tensor(hidl(unit)[:, ft, :], hid[:, unit % 2, ft, :], hidh(unit)[:, ft, :], ALU.subtract)\
               .then_inc(sem(made), 1)

        ons = [(k,) + ar for k, ar, _ in steps if k in ("ou", "ypv")]

        def on_count(key):
            return ons.index(key) + 1

        ybcs = [(k,) + ar for k, ar, _ in steps if k == "ybc"]

        def ons_before(key):
            reads = [(k, ) + ar for k, ar, _ in steps if k in ("ou", "ypv")]
            if key[0] == "pv":
                mine = ("ou", key[1], key[2])
            else:
                mine = key
            return reads.index(mine)

        block = ctx.enter_context(nc.Block())

        @block.sync
        def _(sp):
            def tokens(t, b):
                return t[b].rearrange("(t p) d -> p t d", p=P)

            sp.dma_start(x[:, 0:QT, :], tokens(a["x"], 0)).then_inc(sem("x_loaded0"), 16)
            sp.dma_start(const[:], a["const"]).then_inc(sem("const_loaded"), 16)
            sp.dma_start(wf[:, 0:PO[0][1]], a["pack0"]).then_inc(sem("pack_loaded"), 16)
            sp.dma_start(const16[:], a["const16"]).then_inc(sem("const16_loaded"), 16)
            for b in range(1, B):
                sp.dma_start(x[:, b * QT:(b + 1) * QT, :], tokens(a["x"], b)).then_inc(sem(f"x_loaded{b}"), 16)
            sp.dma_start(smscale[:], a["smscale"].partition_broadcast(P)).then_inc(sem("small_loaded"), 16)
            sp.dma_start(gbias[:], a["gbias"].partition_broadcast(P)).then_inc(sem("small_loaded"), 16)
            sp.dma_start(b1[:], a["b1"]).then_inc(sem("small_loaded"), 16)
            sp.dma_start(bo[:], a["bo"].partition_broadcast(P)).then_inc(sem("small_loaded"), 16)
            sp.dma_start(maskT[:], a["maskT"]).then_inc(sem("small_loaded"), 16)
            sp.dma_start(wo[:], a["wo"]).then_inc(sem("small_loaded"), 16)
            sp.dma_start(ywo[:], a["ywo"]).then_inc(sem("small_loaded"), 16)
            for n in (1, 2):
                sp.wait_ge(sem("pack_high"), n)
                sp.wait_ge(sem("pack_low"), n)
                sp.dma_start(wf[:, 0:PO[n][1]], a[f"pack{n}"]).then_inc(sem("pack_loaded"), 16)
            for n in range(2 * (E + 1)):
                ly, e = divmod(n, E + 1)
                if n:
                    sp.wait_ge(sem("w1_low"), n)
                sp.dma_start(w1f[:], a["w1"][ly, e]).then_inc(sem("w1_loaded"), 16)
                if n:
                    sp.wait_ge(sem("w2_low"), n)
                sp.dma_start(w2f[:], a["w2"][ly, e]).then_inc(sem("w2_loaded"), 16)
                if n >= NB2:
                    ly2, e2 = divmod(n - NB2, E + 1)
                    down_summed(sp, (FFN0, FFN1)[ly2], e2, B - 1)
                    if n - NB2 == 1:
                        sp.wait_ge(sem("deferred"), B)
                sp.dma_start(b2[:, n % NB2], a["b2"][ly, e].partition_broadcast(P))\
                  .then_inc(sem(f"b2_loaded{n % NB2}"), 16)
            for b in range(B):
                down_summed(sp, FFN1, E, b)
                sp.dma_start(tokens(a["out"], b), x[:, b * QT:(b + 1) * QT, :]).then_inc(sem("stored"), 16)
            sp.wait_ge(sem("stored"), 16 * B)

        @block.gpsimd
        def _(pool):
            eng = nc.gpsimd

            def split_pack(n):
                pool.wait_ge(sem("pack_loaded"), 16 * (n + 1))
                pool.wait_ge(sem("pack_high"), n + 1)
                m = PO[n][1]
                eng.tensor_tensor(wl[n][:], wf[:, 0:m], wh[n][:], ALU.subtract).then_inc(sem("pack_low"), 1)

            eng.memset(minus_half[:], -0.5).then_inc(sem("half_set"), 1)
            pool.wait_ge(sem("half_set"), 1)
            eng.memset(ones[:], 1.0).then_inc(sem("ones_set"), 1)
            eng.memset(mneg[:], 0.0).then_inc(sem("mneg_cleared"), 1)
            for kind, args, hb in steps:
                key = (kind,) + args
                if kind == "ln":
                    pool.wait_ge(sem("var_ready"), done(kind, *args))
                    eng.tensor_tensor(rstd[:], veps[:], minus_half[:], ALU.pow).then_inc(sem("rstd_ready"), 1)
                    if args == (SELF0, 0):
                        split_pack(0)
                        eng.memset(va[:], 0.0).then_inc(sem("v_cleared"), 1)
                        pool.wait_ge(sem("v_cleared"), 1)
                        eng.memset(va[:, :, :, :, DK:DK + 1].rearrange("p a t h o -> p (a t h) o"), 1.0)\
                           .then_inc(sem("v_ones"), 1)
                    if args == (SELF0, 2):
                        eng.memset(vx[:], 0.0).then_inc(sem("v_cleared"), 1)
                        pool.wait_ge(sem("v_cleared"), 2)
                        eng.memset(vx[:, :, :, DK:DK + 1].rearrange("p b h o -> p (b h) o"), 1.0)\
                           .then_inc(sem("v_ones"), 1)
                        eng.memset(vy[:, :, :, DH:DH + 1].rearrange("p b h o -> p (b h) o"), 1.0)\
                           .then_inc(sem("v_ones"), 1)
                        eng.memset(mnegb[:], 0.0).then_inc(sem("mneg_cleared"), 1)
                        eng.memset(mneg1[:], 0.0).then_inc(sem("mneg_cleared"), 1)
                if kind == "proj":
                    ph, b, which = args
                    qk, m = int(which == "k"), B * C if (ph, which) == (CROSS0, "k") else S
                    pool.wait_ge(sem("ch_ready"), done(kind, *args))
                    eng.tensor_tensor(cl[:, qk, 0:m], cf[:, 0:m], ch[:, qk, 0:m], ALU.subtract)\
                       .then_inc(sem("cl_ready"), 1)
                if kind == "ks":
                    ph, n = args
                    helper_read(pool, hb)
                    for j in range(J):
                        eng.tensor_scalar(kz[:, slot_of[ph, n], j, :], ks[:], cst("headmask")[:, j:j + 1], 0.0,
                                          ALU.mult, ALU.add).then_inc(sem("kz_ready"), 1)
                if kind == "ks0":
                    g, = args
                    helper_read(pool, hb)
                    for j in range(J):
                        eng.tensor_scalar(kx[:, :, g, j, :], ks[:, 0:B * C].rearrange("p (b c) -> p b c", b=B),
                                          cst("headmask")[:, j:j + 1], 0.0, ALU.mult, ALU.add)\
                           .then_inc(sem("kx_ready"), 1)
                if (kind,) + args in SPLIT_AT:
                    split_pack(SPLIT_AT[(kind,) + args])
                n = split_expert_at(kind, args)
                if n is not None:
                    pool.wait_ge(sem("w1_loaded"), 16 * (n + 1))
                    if n >= 2:
                        ly, e = divmod(n - 2, E + 1)
                        pool.wait_ge(sem("st_filled"), at[("up", (FFN0, FFN1)[ly], e, B - 1, FT - 1)]["st"] + 1)
                    eng.tensor_copy(w1h[:, n % 2, :], w1f[:]).then_inc(sem("w1_high"), 1)
                    pool.wait_ge(sem("w1_high"), n + 1)
                    eng.tensor_tensor(w1l[:, n % 2, :], w1f[:], w1h[:, n % 2, :], ALU.subtract)\
                       .then_inc(sem("w1_low"), 1)
                n = split_second_at(kind, args)
                if n is not None:
                    pool.wait_ge(sem("w2_loaded"), 16 * (n + 1))
                    if n >= 2:
                        ly, e = divmod(n - 2, E + 1)
                        pool.wait_ge(sem("mx_filled"), at[("down", (FFN0, FFN1)[ly], e, B - 1, QT - 1)]["mx"] + 1)
                    eng.tensor_copy(w2h[:, n % 2, :], w2f[:]).then_inc(sem("w2_high"), 1)
                    pool.wait_ge(sem("w2_high"), n + 1)
                    eng.tensor_tensor(w2l[:, n % 2, :], w2f[:], w2h[:, n % 2, :], ALU.subtract)\
                       .then_inc(sem("w2_low"), 1)
                if kind == "up":
                    for k in parts_of(key, 2):
                        if k % FT >= dve_lows(k // FT):
                            hidden_low(pool, eng, k, "hidden_low_pool")

        @block.scalar
        def _(act):
            eng = nc.scalar

            def copy(out, in_):
                return eng.activation(out, in_, ACT.Copy)

            def split_pack(n):
                act.wait_ge(sem("pack_loaded"), 16 * (n + 1))
                copy(wh[n][:], wf[:, 0:PO[n][1]]).then_inc(sem("pack_high"), 1)

            split_pack(0)
            for kind, args, hb in steps:
                key = (kind,) + args
                if kind == "xT":
                    ph, b = args
                    helper_filled(act, hb)
                    copy(xh[:, b, :], mi[:, hb % NMI, :]).then_inc(sem("xh_ready"), 1)
                elif kind == "proj":
                    ph, b, which = args
                    qk, m = int(which == "k"), B * C if (ph, which) == (CROSS0, "k") else S
                    if ph == SELF0:
                        act.wait_ge(sem("roped"), done(*key))
                    else:
                        helper_filled(act, hb)
                        if nth[key]:
                            act.wait_ge(sem("cl_ready"), nth[key])
                        if (ph, which) == (SELF1, "q"):
                            act.wait_ge(sem("small_loaded"), 16 * 7)
                            eng.activation(cf[:, 0:m], mi[:, hb % NMI, 0:m], ACT.Identity, scale=smscale[:, 0:1])\
                               .then_inc(read_sem(hb), 1)
                        else:
                            copy(cf[:, 0:m], mi[:, hb % NMI, 0:m]).then_inc(read_sem(hb), 1)
                        helper_read(act, hb)
                    copy(ch[:, qk, 0:m], cf[:, 0:m]).then_inc(sem("ch_ready"), 1)
                elif kind == "v":
                    ph, b = args
                    helper_filled(act, hb)
                    act.wait_ge(sem("v_cleared"), 1)
                    copy(va[:, b % 2, :, :, 0:DK].rearrange("p t h d -> p (t h) d"),
                         mi[:, hb % NMI, :].rearrange("p (a d) -> p a d", d=DK)).then_inc(read_sem(hb), 1)
                elif kind == "v0":
                    b, = args
                    helper_filled(act, hb)
                    act.wait_ge(sem("v_cleared"), 2)
                    copy(vx[:, b, :, 0:DK], mi[0:C, hb % NMI, 0:D].rearrange("p (a d) -> p a d", d=DK))\
                        .then_inc(read_sem(hb), 1)
                elif kind == "ks":
                    helper_filled(act, hb)
                    act.wait_ge(sem("const_loaded"), 16)
                    if nth[key]:
                        act.wait_ge(sem("kz_ready"), J * nth[key])
                    eng.activation(ks[:], mi[:, hb % NMI, :], ACT.Identity, bias=cst("onerow")).then_inc(read_sem(hb), 1)
                elif kind == "ks0":
                    g, = args
                    helper_filled(act, hb)
                    if g:
                        act.wait_ge(sem("kx_ready"), J * g)
                    else:
                        act.wait_ge(sem("kz_ready"), J * B * G)
                    copy(ks[:, 0:B * C], mi[:, hb % NMI, 0:B * C]).then_inc(read_sem(hb), 1)
                elif kind == "qs":
                    ph, n = args
                    helper_filled(act, hb)
                    copy(qs[:, slot_of[ph, n], :], mi[:, hb % NMI, :]).then_inc(read_sem(hb), 1)
                elif kind == "mT" and args[0] == CROSS0:
                    helper_filled(act, hb)
                    copy(mtb[:, args[1] % 2, :], mi[:, hb % NMI, :]).then_inc(read_sem(hb), 1)
                elif kind == "ymT":
                    helper_filled(act, hb)
                    copy(mt1[:], mi[:, hb % NMI, :]).then_inc(read_sem(hb), 1)
                elif kind in ("sc", "ysc"):
                    u, t = at[key]["st"], at[key]["pt"]
                    ph = args[0] if kind == "sc" else CROSS1
                    rows = P if ph in (SELF0, SELF1) else C
                    scale = {SELF0: DK ** -0.5, CROSS0: DK ** -0.5, SELF1: 1.0, CROSS1: DH ** -0.5}[ph]
                    act.wait_ge(sem("st_filled"), u + 1)
                    if t >= NPT:
                        product, reader = pt_reader[t - NPT]
                        if reader[0] == "ypv":
                            act.wait_ge(sem("mx_filled"), at[reader]["mx"] + 1)
                        else:
                            act.wait_ge(sem("pv_done"), product + 1)
                    eng.activation(pt[0:rows, t % NPT, :], st[0:rows, u % NST, :], ACT.Exp, scale=scale)\
                       .then_inc(sem("st_read"), 1)
                elif kind == "ou":
                    ph, n = args
                    act.wait_ge(sem("pv_done"), at[key]["pv"])
                    copy(ou[:], pv[:]).then_inc(sem("pv_read"), 1)
                elif kind == "outT":
                    helper_filled(act, hb)
                    copy(onT[:], mi[:, hb % NMI, :]).then_inc(read_sem(hb), 1)
                elif kind == "ybc":
                    b, hp = args
                    helper_filled(act, hb)
                    copy(on[:, b % 2, hp, :], mi[:, hb % NMI, :]).then_inc(read_sem(hb), 1)
                elif kind == "yk":
                    h, = args
                    helper_filled(act, hb)
                    copy(kA[0:DH, h].rearrange("p b c -> p (b c)"), mi[0:DH, hb % NMI, 0:B * C]).then_inc(sem("kh_ready"), 1)
                    copy(kB[DH:P, h].rearrange("p b c -> p (b c)"), mi[DH:P, hb % NMI, 0:B * C]).then_inc(sem("kh_ready"), 1)
                elif kind == "yv":
                    b, = args
                    helper_filled(act, hb)
                    copy(vy[:, b, :, 0:DH], mi[0:C, hb % NMI, :].rearrange("p (h d) -> p h d", h=H1))\
                        .then_inc(read_sem(hb), 1)
                elif kind == "yq":
                    b, h = args
                    helper_filled(act, hb)
                    copy(qh2[:, b % 2, h, :], mi[:, hb % NMI, :]).then_inc(sem("qh_ready"), 1)
                elif kind == "soft":
                    act.wait_ge(sem("logits_shifted"), done(*key))
                    eng.activation(lg[:], lg[:], ACT.Exp).then_inc(sem("logits_exp"), 1)
                elif kind == "up":
                    ph, e, tb, ft = args
                    unit, u = nth[key] // FT, at[key]["st"]
                    if nth[key] == 0:
                        act.wait_ge(sem("small_loaded"), 16 * 7)
                    if unit >= 3 and ft == 0:
                        act.wait_ge(sem("mx_filled"), down_of(unit - 3))
                    if unit >= 2 and ft == 0:
                        lows_made(act, unit - 2)
                    act.wait_ge(sem("st_filled"), u + 1)
                    eng.activation(hid[:, unit % 2, ft, :], st[:, u % NST, :], ACT.Gelu_apprx_tanh,
                                   bias=b1[:, int(ph == FFN1), e, ft:ft + 1]).then_inc(sem("st_read"), 1)
                    for k in parts_of(key, 1):
                        u2, ft2 = divmod(k, FT)
                        act.wait_ge(sem("st_read"), u - nth[key] + k + 1)
                        copy(hidh(u2)[:, ft2, :], hid[:, u2 % 2, ft2, :]).then_inc(sem("hidden_high"), 1)
                elif kind == "down" and args[0:2] == (FFN0, 1):
                    _, _, tb, t = args
                    u = at[key]["mx"]
                    if u:
                        act.wait_ge(sem("mx_read"), u)
                    act.wait_ge(sem("mx_filled"), u + 1)
                    copy(y1[:, tb * QT + t, :], mx[:, u % NMX, 0:D]).then_inc(sem("mx_read"), 1)
                if key in SPLIT_AT:
                    split_pack(SPLIT_AT[key])

        @block.tensor
        def _(pe):
            mm = nc.tensor.matmul
            loaded = set()

            def once(name, value):
                if (name, value) not in loaded:
                    loaded.add((name, value))
                    pe.wait_ge(sem(name), value)

            def helper_free(hb):
                if hb >= NMI:
                    helper_read(pe, hb - NMI)

            def st_free(u):
                if u >= NST:
                    pe.wait_ge(sem("st_read"), u - NST + 1)

            def mx_free(u):
                if u >= NMX:
                    pe.wait_ge(sem("mx_read"), u - NMX + 1)

            def three(out, lh, ll, rh, rl, start=True, stop=True):
                mm(out, lh, rh, start=start, stop=False)
                mm(out, lh, rl, start=False, stop=False)
                return mm(out, ll, rh, start=False, stop=stop)

            once("const_loaded", 16)
            for kind, args, hb in steps:
                key = (kind,) + args
                o = mi[:, hb % NMI, :]
                if kind == "xT":
                    ph, b = args
                    pe.wait_ge(sem("xn_ready"), done(*key))
                    helper_free(hb)
                    for t in range(QT):
                        last = nc.tensor.transpose(o[:, tile(t)], xn[:, nth[key] % 2, t, :], cst("ident"))
                    last.then_inc(sem("helper_filled"), 1)
                elif kind == "proj":
                    ph, b, which = args
                    once("pack_low", needs_pack[ph])
                    if (ph, which) == (CROSS0, "k"):
                        helper_free(hb)
                        three(o[:, 0:B * C], w("xwk0"), w("xwk0", 1), w("ctx"), w("ctx", 1)).then_inc(sem("helper_filled"), 1)
                    else:
                        helper_read(pe, helper_of[("xT", ph, b)])
                        name = (WQ if which == "q" else WK)[ph]
                        names = [name, name[:2] + "p0"] if ph == SELF0 else [name]
                        for k, nm in enumerate(names):
                            helper_free(hb + k)
                            three(mi[:, (hb + k) % NMI, :], w(nm), w(nm, 1), xh[:, b], xl[:, b])\
                                .then_inc(sem("helper_filled"), 1)
                elif kind == "v":
                    ph, b = args
                    helper_read(pe, helper_of[("xT", ph, b)])
                    helper_free(hb)
                    for t in range(QT):
                        last = three(o[:, tile(t)], xh[:, b, tile(t)], xl[:, b, tile(t)], w(WV[ph]), w(WV[ph], 1))
                    last.then_inc(sem("helper_filled"), 1)
                elif kind == "v0":
                    b, = args
                    helper_free(hb)
                    cb = slice(b * C, (b + 1) * C)
                    three(o[0:C, 0:D], w("ctx", 0, cb), w("ctx", 1, cb), w("xwv0"), w("xwv0", 1))\
                        .then_inc(sem("helper_filled"), 1)
                elif kind in ("ks", "ks0", "qs"):
                    once("const16_loaded", 16)
                    if kind == "ks0":
                        g, m, proj = args[0], B * C, ("proj", CROSS0, 0, "k")
                    else:
                        b, g = divmod(args[1], G)
                        m, proj = S, ("proj", args[0], b, kind[0])
                    pe.wait_ge(sem("cl_ready"), done(*proj))
                    helper_free(hb)
                    c = kind[0]
                    mm(o[:, 0:m], sel(f"sel{c}h", g), ch[:, int(c == "k"), 0:m], start=True, stop=False)
                    mm(o[:, 0:m], sel(f"sel{c}l", g), cl[:, int(c == "k"), 0:m], start=False, stop=True)\
                        .then_inc(sem("helper_filled"), 1)
                elif kind == "max":
                    ph, n, qt, j = args
                    u = at[key]["mx"]
                    b, g = divmod(n, G)
                    helper_read(pe, helper_of[("qs", ph, n)])
                    lhs = qs[:, slot_of[ph, n], tile(qt)]
                    if ph == CROSS0:
                        pe.wait_ge(sem("kx_ready"), J * G)
                        once("mask_ready", 1)
                        mx_free(u)
                        mm(mx[:, u % NMX, 0:J * C], lhs, kx[:, b, g].rearrange("p j c -> p (j c)"), start=True, stop=False)
                        mm(mx[:, u % NMX, 0:J * C], maskb[:, tile(qt)], c16("irep")[0:C, :], start=False, stop=True)\
                            .then_inc(sem("mx_filled"), 1)
                    else:
                        pe.wait_ge(sem("kz_ready"), J * done("ks", ph, n))
                        mx_free(u)
                        mm(mx[:, u % NMX, :], lhs, kz[:, slot_of[ph, n], j, :], start=True, stop=True).then_inc(sem("mx_filled"), 1)
                elif kind == "mT":
                    ph, n = args
                    last_max = ("max", ph, n, QT - 1, 0 if ph == CROSS0 else J - 1)
                    pe.wait_ge(sem("mx_read"), at[last_max]["mx"] + 1)
                    helper_free(hb)
                    src = mnegb if ph == CROSS0 else mneg
                    for t in range(QT):
                        last = mm(o[:, tile(t)], src[:, n % 2, t, :], c16("id16"), start=True, stop=True)
                    last.then_inc(sem("helper_filled"), 1)
                elif kind == "sc":
                    ph, n, kt, j = args
                    b, g = divmod(n, G)
                    u = at[key]["st"]
                    helper_read(pe, helper_of[("mT", ph, n)])
                    st_free(u)
                    if ph == CROSS0:
                        out = st[0:C, u % NST, :]
                        mm(out, kx[:, b, g, j, :], qs[:, slot_of[ph, n], :], start=True, stop=False)
                        mm(out, c16("id16")[0:C, 0:C], maskb[:], start=False, stop=False)
                        mm(out, c16("selm0")[:, j * C:(j + 1) * C], mtb[:, n % 2, :], start=False, stop=True)\
                            .then_inc(sem("st_filled"), 1)
                    else:
                        mm(st[:, u % NST, :], kz[:, slot_of[ph, n], j, tile(kt)], qs[:, slot_of[ph, n], :], start=True, stop=True)\
                            .then_inc(sem("st_filled"), 1)
                elif kind == "pv":
                    ph, n, kt = args
                    b, g = divmod(n, G)
                    s_last = ("sc", ph, n, kt, J - 1)
                    pe.wait_ge(sem("st_read"), at[s_last]["st"] + 1)
                    once("v_ones", 2 if ph == CROSS0 else 1)
                    if kt == 0:
                        if ph == CROSS0:
                            helper_read(pe, helper_of[("v0", b)])
                        else:
                            helper_read(pe, helper_of[("v", ph, b)])
                        if n or ph != SELF0:
                            pe.wait_ge(sem("pv_read"), ons_before(key))
                    for j in range(J):
                        t = (at[s_last]["pt"] - (J - 1) + j) % NPT
                        out = pv[32 * j:32 * j + 32, :]
                        if ph == CROSS0:
                            last = mm(out, vx[:, b, J * g + j, :], pt[0:C, t, :], start=True, stop=True)
                        else:
                            last = mm(out, va[:, b % 2, kt, J * g + j, :], pt[:, t, :], start=kt == 0, stop=kt == QT - 1)
                    last.then_inc(sem("pv_done"), 1)
                elif kind == "sb":
                    ph, n = args
                    pe.wait_ge(sem("pv_read"), on_count(("ou",) + args))
                    helper_free(hb)
                    for t in range(QT):
                        last = nc.tensor.transpose(o[:, tile(t)], ou[:, tile(t)], cst("ident"))
                    last.then_inc(sem("helper_filled"), 1)
                elif kind == "outT":
                    ph, b = args
                    helper_read(pe, helper_of[("sb", ph, b * G + G - 1)])
                    helper_free(hb)
                    for t in range(QT):
                        last = nc.tensor.transpose(o[:, tile(t)], ont[:, b % 2, t, :], cst("ident"))
                    last.then_inc(sem("helper_filled"), 1)
                elif kind == "ybc":
                    b, hp = args
                    pe.wait_ge(sem("pv_read"), on_count(("ypv", b, hp)))
                    pe.wait_ge(sem("mx_read"), at["ypv", b, hp]["mx"] + 1)
                    helper_free(hb)
                    for t in range(QT):
                        last = nc.tensor.transpose(o[:, tile(t)], ont[:, hp % 2, t, :], cst("ident"))
                    last.then_inc(sem("helper_filled"), 1)
                elif kind == "out":
                    ph, b = args
                    helper_read(pe, helper_of[("ybc", b, HP - 1) if ph == CROSS1 else ("outT", ph, b)])
                    once("small_loaded", 16 * 7)
                    helper_free(hb)
                    for t in range(QT):
                        if ph != CROSS1:
                            last = mm(o[:, tile(t)], onT[:, tile(t)], wo[:, WO[ph], :], start=True, stop=True)
                            continue
                        for hp in range(HP):
                            last = mm(o[:, tile(t)], on[:, b % 2, hp, tile(t)], ywo[:, hp, :],
                                      start=hp == 0, stop=hp == HP - 1)
                    last.then_inc(sem("helper_filled"), 1)
                elif kind == "yk":
                    h, = args
                    once("pack_low", 3)
                    helper_free(hb)
                    cut = slice(h * P, (h + 1) * P)
                    three(o[:, 0:B * C], w("ywk", 0, cut), w("ywk", 1, cut), w("ctx"), w("ctx", 1))\
                        .then_inc(sem("helper_filled"), 1)
                elif kind == "yv":
                    b, = args
                    helper_free(hb)
                    cb = slice(b * C, (b + 1) * C)
                    three(o[0:C, :], w("ctx", 0, cb), w("ctx", 1, cb), w("ywv"), w("ywv", 1)).then_inc(sem("helper_filled"), 1)
                elif kind == "yq":
                    b, h = args
                    helper_read(pe, helper_of[("xT", CROSS1, b)])
                    helper_free(hb)
                    cut = slice(h * P, (h + 1) * P)
                    three(o, w("ywq", 0, cut), w("ywq", 1, cut), xh[:, b], xl[:, b]).then_inc(sem("helper_filled"), 1)
                elif kind == "ymax":
                    b, h = args
                    u = at[key]["mx"]
                    helper_read(pe, helper_of[("yk", h)])
                    helper_read(pe, helper_of[("yq", b, h)])
                    mx_free(u)
                    for t in range(QT):
                        out = mx[:, u % NMX, t * C:(t + 1) * C]
                        mm(out, qh2[:, b % 2, h, tile(t)], kA[:, h, b, :], start=True, stop=False)
                        last = mm(out, ql2[:, b % 2, h, tile(t)], kB[:, h, b, :], start=False, stop=True)
                    last.then_inc(sem("mx_filled"), 1)
                elif kind == "ymT":
                    b, = args
                    pe.wait_ge(sem("mx_read"), at[("ymax", b, H1 - 1)]["mx"] + 1)
                    helper_free(hb)
                    for t in range(QT):
                        last = mm(o[:, tile(t)], mneg1[:, b % 2, t, :], c16("id16"), start=True, stop=True)
                    last.then_inc(sem("helper_filled"), 1)
                elif kind == "ysc":
                    b, h = args
                    u = at[key]["st"]
                    helper_read(pe, helper_of[("ymT", b)])
                    st_free(u)
                    out = st[0:C, u % NST, :]
                    mm(out, kA[:, h, b, :], qh2[:, b % 2, h, :], start=True, stop=False)
                    mm(out, kB[:, h, b, :], ql2[:, b % 2, h, :], start=False, stop=False)
                    mm(out, c16("selm1")[:, h * C:(h + 1) * C], mt1[:], start=False, stop=True).then_inc(sem("st_filled"), 1)
                elif kind == "ypv":
                    b, hp = args
                    s_last = ("ysc", b, 2 * hp + 1)
                    helper_read(pe, helper_of[("yv", b)])
                    pe.wait_ge(sem("st_read"), at[s_last]["st"] + 1)
                    pe.wait_ge(sem("pv_read"), ons_before(key))
                    once("v_ones", 3)
                    mx_free(at[key]["mx"])
                    for i2, (bank, filled) in enumerate(((pv[:], "pv_done"), (mx[:, at[key]["mx"] % NMX, :], "mx_filled"))):
                        t = (at[s_last]["pt"] - 1 + i2) % NPT
                        for q in range(QT):
                            last = mm(bank[:, q * (DH + 1):(q + 1) * (DH + 1)], pt[0:C, t, tile(q)],
                                      vy[:, b, 2 * hp + i2, :], start=True, stop=True)
                        last.then_inc(sem(filled), 1)
                elif kind == "logits":
                    ph, = args
                    helper_free(hb)
                    name = "gate0" if ph == FFN0 else "gate1"
                    for b in range(B):
                        helper_read(pe, helper_of[("xT", ph, b)])
                        for t in range(QT):
                            c = (b * QT + t) * E
                            last = three(o[:, c:c + E], xh[:, b, tile(t)], xl[:, b, tile(t)], w(name), w(name, 1))
                    last.then_inc(sem("helper_filled"), 1)
                elif kind == "bsum":
                    k, = args
                    pe.wait_ge(sem("part_ready"), done(*key))
                    helper_free(hb)
                    mm(o[:, 0:3], ones[:], part[:], start=True, stop=True).then_inc(sem("helper_filled"), 1)
                elif kind == "choose":
                    pe.wait_ge(sem("part_ready"), done("bit", 0) + 1)
                    helper_free(hb)
                    flat = t1[:].rearrange("p e t -> p (e t)")
                    mm(o[:, 0:1], ones[:], part[:, 0:1], start=True, stop=True)
                    mm(o[:, P:2 * P], ones[:], flat, start=True, stop=True)
                    mm(o[:, 2 * P:3 * P], cst("tri"), flat, start=True, stop=True).then_inc(sem("helper_filled"), 1)
                elif kind == "up":
                    ph, e, tb, ft = args
                    n, u, c = EXPERT[ph] + e, at[key]["st"], tile(ft)
                    once("w1_low", n + 1)
                    if e == 0 and ft == 0:
                        helper_read(pe, helper_of[("xT", ph, tb)])
                    st_free(u)
                    three(st[:, u % NST, :], w1h[:, n % 2, c], w1l[:, n % 2, c], xh[:, tb], xl[:, tb])\
                        .then_inc(sem("st_filled"), 1)
                elif kind == "down":
                    ph, e, tb, t = args
                    n, u, unit = EXPERT[ph] + e, at[key]["mx"], nth[key] // QT
                    once("w2_low", n + 1)
                    if t == 0:
                        lows_made(pe, unit)
                    mx_free(u)
                    for ft in range(FT):
                        last = three(mx[:, u % NMX, 0:D], hidh(unit)[:, ft, tile(t)], hidl(unit)[:, ft, tile(t)],
                                     w2h[:, n % 2, tile(ft)], w2l[:, n % 2, tile(ft)], start=ft == 0, stop=ft == FT - 1)
                    last.then_inc(sem("mx_filled"), 1)

        @block.vector
        def _(dve):
            eng = nc.vector
            chain = [0]

            def link(ins, wait=True):
                chain[0] += 1
                ins.then_inc(sem("dve_chain"), 1)
                if wait:
                    linked()

            def linked():
                dve.wait_ge(sem("dve_chain"), chain[0])

            def bc(ap, shape):
                return ap.to_broadcast(shape)

            def over_tiles(ap):
                return ap.unsqueeze(2).to_broadcast([P, NT, E])

            def te(t):
                return t[:].rearrange("p e t -> p t e")

            def over_batch(ap):
                return ap.unsqueeze(1).to_broadcast([P, QT, D])

            for kind, args, hb in steps:
                key = (kind,) + args
                o = mi[:, hb % NMI, :]
                if kind == "ln":
                    ph, b = args
                    k = nth[key]
                    if ph == SELF0:
                        dve.wait_ge(sem(f"x_loaded{b}"), 16)
                    else:
                        summed(dve, ph, b)
                    if k:
                        dve.wait_ge(sem("xn_ready"), k)
                    for t in range(QT):
                        link(eng.bn_stats(stats[:, t, :], x[:, b * QT + t, :]), t == QT - 1)
                    for t in range(QT):
                        link(eng.bn_aggr(mv[:, t, :], stats[:, t, :]), t == QT - 1)
                    eng.tensor_scalar(veps[:], mv[:, :, 1], EPS, None, ALU.add).then_inc(sem("var_ready"), 1)
                elif kind == "ln2":
                    ph, b = args
                    k = nth[key]
                    dve.wait_ge(sem("rstd_ready"), k + 1)
                    if k >= 2:
                        helper_filled(dve, helper_of[("xT",) + norms[k - 2]])
                    for t in range(QT):
                        last = eng.tensor_scalar(xn[:, k % 2, t, :], x[:, b * QT + t, :], mv[:, t, 0:1], rstd[:, t:t + 1],
                                                 ALU.subtract, ALU.mult)
                    last.then_inc(sem("xn_ready"), 1)
                elif kind == "xT":
                    ph, b = args
                    dve.wait_ge(sem("xh_ready"), done(*key))
                    helper_filled(dve, hb)
                    eng.tensor_tensor(xl[:, b, :], o, xh[:, b, :], ALU.subtract).then_inc(read_sem(hb), 1)
                    if ph == FFN1:
                        dve.wait_ge(sem("xn_ready"), done(*key))
                        xb = x[:, b * QT:(b + 1) * QT, :]
                        link(eng.tensor_tensor(xb, xb, xn[:, nth[key] % 2], ALU.add))
                elif kind == "proj" and args[0] == SELF0:
                    ph, b, which = args
                    helper_filled(dve, hb + 1)
                    dve.wait_ge(sem("const_loaded"), 16)
                    if nth[key]:
                        dve.wait_ge(sem("roped"), nth[key])
                    eng.tensor_tensor(rope[:, 0], o, cst("cos"), ALU.mult).then_inc(read_sem(hb), 1)
                    eng.tensor_tensor(rope[:, 1], mi[:, (hb + 1) % NMI, :], cst("sin"), ALU.mult).then_inc(read_sem(hb + 1), 1)
                    helper_read(dve, hb)
                    helper_read(dve, hb + 1)
                    if nth[key]:
                        dve.wait_ge(sem("cl_ready"), nth[key])
                    eng.tensor_tensor(cf[:], rope[:, 0], rope[:, 1], ALU.add).then_inc(sem("roped"), 1)
                elif kind == "max":
                    ph, n, qt, j = args
                    u = at[key]["mx"]
                    dve.wait_ge(sem("mx_filled"), u + 1)
                    dve.wait_ge(sem("mneg_cleared"), 3 if ph == CROSS0 else 1)
                    if ph == CROSS0:
                        eng.tensor_reduce(mnegb[:, n % 2, qt, MROW::32],
                                          mx[:, u % NMX, 0:J * C].rearrange("p (j c) -> p j c", j=J),
                                          AX.X, ALU.max, negate=True).then_inc(sem("mx_read"), 1)
                    else:
                        r = 32 * j + MROW
                        eng.tensor_reduce(mneg[:, n % 2, qt, r:r + 1], mx[:, u % NMX, :], AX.X, ALU.max, negate=True)\
                           .then_inc(sem("mx_read"), 1)
                elif kind == "ymax":
                    b, h = args
                    u = at[key]["mx"]
                    dve.wait_ge(sem("mx_filled"), u + 1)
                    eng.tensor_reduce(mneg1[:, b % 2, :, h], mx[:, u % NMX, 0:QT * C].rearrange("p (t c) -> p t c", t=QT),
                                      AX.X, ALU.max, negate=True).then_inc(sem("mx_read"), 1)
                elif kind == "mT" and args[0] != CROSS0:
                    ph, n = args
                    helper_filled(dve, hb)
                    eng.tensor_tensor(qs[:, slot_of[ph, n], :], o, qs[:, slot_of[ph, n], :], ALU.add).then_inc(read_sem(hb), 1)
                elif kind == "sb":
                    ph, n = args
                    b, g = divmod(n, G)
                    helper_filled(dve, hb)
                    heads = o.rearrange("p (t j r) -> p t j r", t=QT, j=J)
                    r4 = rc[:, n % 2, :].rearrange("p (t j) -> p t j", t=QT)
                    link(eng.reciprocal(r4, heads[:, :, :, DK]))
                    eng.tensor_tensor(ont[:, b % 2, :, g * 32:(g + 1) * 32].rearrange("p t (j d) -> p t j d", j=J),
                                      heads[:, :, :, 0:DK], r4.unsqueeze(3).to_broadcast([P, QT, J, DK]), ALU.mult)\
                       .then_inc(read_sem(hb), 1)
                elif kind == "ypv":
                    b, hp = args
                    u = at[key]["mx"]
                    if nth[key] >= 2:
                        helper_filled(dve, helper_of[ybcs[nth[key] - 2]])
                    for i2, bank in enumerate((pv[:], mx[:, u % NMX, :])):
                        dve.wait_ge(sem("mx_filled" if i2 else "pv_done"), u + 1 if i2 else at[key]["pv"] + 1)
                        heads = bank[:, 0:QT * (DH + 1)].rearrange("p (t r) -> p t r", t=QT)
                        r1 = rc[:, i2, 0:QT]
                        link(eng.reciprocal(r1, heads[:, :, DH]))
                        eng.tensor_tensor(ont[:, hp % 2, :, DH * i2:DH * (i2 + 1)], heads[:, :, 0:DH],
                                          r1.unsqueeze(2).to_broadcast([P, QT, DH]), ALU.mult)\
                           .then_inc(sem("mx_read" if i2 else "pv_read"), 1)
                elif kind == "out":
                    ph, b = args
                    helper_filled(dve, hb)
                    xb = x[:, b * QT:(b + 1) * QT, :]
                    eng.tensor_tensor(xb, o.rearrange("p (t d) -> p t d", t=QT), xb, ALU.add).then_inc(read_sem(hb), 1)
                    helper_read(dve, hb)
                    if ph in (CROSS0, CROSS1):
                        dve.wait_ge(sem("small_loaded"), 16 * 7)
                        eng.tensor_tensor(xb, xb, over_batch(bo[:, int(ph == CROSS1), :]), ALU.add)\
                           .then_inc(sem("out_summed"), 1)
                    else:
                        dve.sem_inc(sem("out_summed"), 1)
                elif kind == "yk":
                    h, = args
                    dve.wait_ge(sem("kh_ready"), 2 * (h + 1))
                    lo, hi = slice(0, DH), slice(DH, P)
                    m = lambda t, r: t[r, h].rearrange("p b c -> p (b c)")
                    link(eng.tensor_tensor(m(kA, hi), mi[hi, hb % NMI, 0:B * C], m(kB, hi), ALU.subtract), False)
                    eng.tensor_tensor(m(kB, lo), mi[lo, hb % NMI, 0:B * C], m(kA, lo), ALU.subtract).then_inc(read_sem(hb), 1)
                elif kind == "yq":
                    b, h = args
                    dve.wait_ge(sem("qh_ready"), done(*key))
                    eng.tensor_tensor(ql2[:, b % 2, h, :], o, qh2[:, b % 2, h, :], ALU.subtract).then_inc(read_sem(hb), 1)
                elif kind == "logits":
                    ph, = args
                    helper_filled(dve, hb)
                    src = o[:, 0:NT * E].rearrange("p (t e) -> p t e", t=NT)
                    if ph == FFN0:
                        eng.tensor_copy(lg[:], src).then_inc(read_sem(hb), 1)
                    else:
                        eng.tensor_tensor(lg[:], src, gbias[:].unsqueeze(1).to_broadcast([P, NT, E]), ALU.add)\
                           .then_inc(read_sem(hb), 1)
                    helper_read(dve, hb)
                elif kind == "soft":
                    ph, = args
                    link(eng.tensor_reduce(sm[:], lg[:], AX.X, ALU.max))
                    eng.tensor_tensor(lg[:], lg[:], over_tiles(sm[:]), ALU.subtract).then_inc(sem("logits_shifted"), 1)
                    dve.wait_ge(sem("logits_exp"), done(*key))
                    link(eng.tensor_reduce(rs[:], lg[:], AX.X, ALU.add))
                    link(eng.reciprocal(rs[:], rs[:]))
                    link(eng.tensor_tensor(te(pr), lg[:], over_tiles(rs[:]), ALU.mult))
                    if ph == FFN0:
                        link(eng.memset(thr[:], 0))
                elif kind == "bit":
                    k, = args
                    link(eng.tensor_tensor(cand[:], cst(f"or{k}").bitcast(I32), thr[:].to_broadcast([P, 3]), ALU.bitwise_or))
                    for v in range(3):
                        last = eng.tensor_scalar((t0, t1, t2)[v][:], pr[:], cand[:, v:v + 1].bitcast(F32), None,
                                                 ALU.is_ge, ALU.add, accum_out=part[:, v:v + 1])
                    last.then_inc(sem("part_ready"), 1)
                elif kind == "passed":
                    k, = args
                    hb = helper_of[("bsum", k)]
                    o = mi[:, hb % NMI, :]
                    helper_filled(dve, hb)
                    eng.tensor_scalar(passed[:], o[:, 0:3], float(TOPK), None, ALU.is_ge, ALU.add, accum_out=left[:])\
                       .then_inc(read_sem(hb), 1)
                    helper_read(dve, hb)
                    link(eng.tensor_scalar(inc[:], left[:], float(1 << k), None, ALU.mult))
                    link(eng.tensor_tensor(thr[:], thr[:], inc[:], ALU.bitwise_or))
                elif kind == "choose":
                    tv = thr[:].bitcast(F32)
                    link(eng.tensor_scalar(t1[:], pr[:], tv, None, ALU.is_equal))
                    eng.tensor_scalar(t0[:], pr[:], tv, None, ALU.is_gt, ALU.add, accum_out=part[:, 0:1])\
                       .then_inc(sem("part_ready"), 1)
                    helper_filled(dve, hb)
                    flat = lambda t: t[:].rearrange("p e t -> p (e t)")
                    link(eng.tensor_scalar(left[:], o[:, 0:1], -1.0, float(TOPK), ALU.mult, ALU.add))
                    link(eng.tensor_tensor_scan(cum[:], ones[:], o[:, P:2 * P], 0.0, ALU.mult, ALU.add))
                    link(eng.tensor_tensor(cum[:], cum[:], o[:, P:2 * P], ALU.subtract))
                    eng.tensor_tensor(cum[:], cum[:], o[:, 2 * P:3 * P], ALU.add).then_inc(read_sem(hb), 1)
                    helper_read(dve, hb)
                    link(eng.scalar_tensor_tensor(flat(t2), cum[:], left[:, 0:1], flat(t1), ALU.is_le, ALU.mult))
                    link(eng.tensor_tensor(t0[:], t0[:], t2[:], ALU.add))
                    link(eng.tensor_tensor(gate[:], t0[:], pr[:], ALU.mult))
                elif kind == "top2":
                    pick = cst("pick").unsqueeze(1).to_broadcast([P, NT, E])

                    def first_max(out, vals, m):
                        link(eng.tensor_reduce(m, te(vals), AX.X, ALU.max))
                        link(eng.tensor_tensor(te(out), te(vals), over_tiles(m), ALU.is_equal))
                        link(eng.tensor_tensor(te(out), te(out), pick, ALU.mult))
                        link(eng.tensor_reduce(rs[:], te(out), AX.X, ALU.max))
                        link(eng.tensor_tensor(te(out), te(out), over_tiles(rs[:]), ALU.is_equal))

                    first_max(t0, pr, sm[:])
                    link(eng.scalar_tensor_tensor(t1[:].rearrange("p e t -> p (e t)"), t0[:].rearrange("p e t -> p (e t)"),
                                                  -2.0, pr[:].rearrange("p e t -> p (e t)"), ALU.mult, ALU.add))
                    first_max(t2, t1, left16[:])
                    link(eng.tensor_tensor(sm[:], sm[:], left16[:], ALU.add))
                    link(eng.tensor_scalar(sm[:], sm[:], 1e-9, None, ALU.add))
                    link(eng.reciprocal(sm[:], sm[:]))
                    link(eng.tensor_tensor(t0[:], t0[:], t2[:], ALU.add))
                    link(eng.tensor_tensor(t0[:], t0[:], pr[:], ALU.mult))
                    link(eng.tensor_tensor(te(gate), te(t0), over_tiles(sm[:]), ALU.mult))
                elif kind == "up":
                    for k in parts_of(key, 2):
                        if k % FT < dve_lows(k // FT):
                            hidden_low(dve, eng, k, "hidden_low_dve")
                elif kind == "defer":
                    tb, = args
                    dve.wait_ge(sem("b2_loaded1"), 16)
                    dve.wait_ge(sem("mx_read"), at[("down", FFN0, 1, tb, QT - 1)]["mx"] + 1)
                    for src in (lambda tt: b2[:, 1, :], lambda tt: y1[:, tt, :]):
                        for t in range(QT):
                            tt = tb * QT + t
                            link(eng.scalar_tensor_tensor(x[:, tt, :], src(tt), gate[:, 0, tt:tt + 1], x[:, tt, :],
                                                          ALU.mult, ALU.add), t == QT - 1)
                    dve.sem_inc(sem("deferred"), 1)
                elif kind == "down":
                    ph, e, tb, t = args
                    n, u, tt = EXPERT[ph] + e, at[key]["mx"], tb * QT + t
                    xt = x[:, tt, :]
                    if (ph, e) == (FFN0, 1):
                        continue
                    if tb == 0 and t == 0:
                        dve.wait_ge(sem(f"b2_loaded{n % NB2}"), 16 * (n // NB2 + 1))
                    if e:
                        dve.wait_ge(sem("mx_read"), at[("down", ph, e - 1, tb, t)]["mx"] + 1)
                        g1 = gate[:, e - 1, tt:tt + 1]
                        eng.scalar_tensor_tensor(xt, b2[:, n % NB2, :], g1, xt, ALU.mult, ALU.add).then_inc(sem("b2_added"), 1)
                    else:
                        eng.tensor_tensor(xt, xt, b2[:, n % NB2, :], ALU.add).then_inc(sem("b2_added"), 1)
                    dve.wait_ge(sem("b2_added"), nth[key] + 1 - (NT if (ph, e) > (FFN0, 1) else 0))
                    dve.wait_ge(sem("mx_filled"), u + 1)
                    y = mx[:, u % NMX, 0:D]
                    if e:
                        eng.scalar_tensor_tensor(xt, y, g1, xt, ALU.mult, ALU.add).then_inc(sem("mx_read"), 1)
                    else:
                        eng.tensor_tensor(xt, y, xt, ALU.add).then_inc(sem("mx_read"), 1)
                if key == ("mT", SELF0, 9):
                    dve.wait_ge(sem("small_loaded"), 16 * 7)
                    eng.tensor_scalar(maskb[:], maskT[:], 0.0, NEG, ALU.is_equal, ALU.mult).then_inc(sem("mask_ready"), 1)


def constants():
    import numpy as np
    c = np.zeros((P, NCONST), np.float32)
    h16 = np.zeros((P, NCONST16), np.float16)

    def put(name, v):
        p0, n = CO[name]
        c[:, p0:p0 + n] = v

    def put16(name, v):
        p0, n = CH[name]
        h16[:v.shape[0], p0:p0 + n] = v.reshape(v.shape[0], n)

    put("ident", np.eye(P))
    put("tri", np.triu(np.ones((P, P))))
    put("pick", E - np.arange(E))
    for k in BITS:
        put(f"or{k}", (np.arange(1, 4, dtype=np.int32) << k).view(np.float32))
    inv = (1.0 / np.float32(10000.0) ** (np.arange(0, DK, 2, dtype=np.float32) / np.float32(DK))).astype(np.float32)
    freqs = np.arange(S, dtype=np.float32)[:, None] * inv[None, :]
    d = np.arange(P) % DK
    ang = freqs[:, d % (DK // 2)].T
    put("cos", np.cos(ang).astype(np.float32))
    put("sin", np.where(d[:, None] < DK // 2, -1, 1) * np.sin(ang).astype(np.float32))
    row = np.arange(P)
    put("onerow", (row % 32 == MROW)[:, None])
    put("headmask", row[:, None] // 32 == np.arange(J)[None, :])
    put16("id16", np.eye(P))
    parts = {"selqh": (0, 1), "selql": (2,), "selkh": (0, 2), "selkl": (1,)}
    for name, ts in parts.items():
        s = np.zeros((P, G, P))
        for g in range(G):
            for j in range(J):
                for t in ts:
                    for k in range(DK):
                        s[DK * (J * g + j) + k, g, 32 * j + DK * t + k] = 1
        put16(name, s)
    put16("irep", np.tile(np.eye(C), (1, J)))
    m0 = np.zeros((P, J, C))
    for j in range(J):
        m0[32 * j + MROW, j] = 1
    put16("selm0", m0)
    m1 = np.zeros((P, H1, C))
    for h in range(H1):
        m1[h, h] = 1
    put16("selm1", m1)
    return c, h16


def kernel(**inputs):
    import numpy as np
    import concourse.bacc as _bacc
    from concourse import mybir as _mybir
    from concourse.bass_utils import run_bass_kernel_spmd as _run

    v = {k: np.asarray(a) for k, a in inputs.items()}
    T = lambda name: v[name].T
    arrays = {"x": v["x"], "maskT": v["mask_1x1xSxS2_ik0"][0, 0].T}
    arrays["const"], arrays["const16"] = constants()
    half = DK // 2
    perm = np.array([DK * h + (2 * d + 1 if d < half else 2 * (d - half)) for h in range(H) for d in range(DK)])
    wq, wk = T("L0_attn_Wq"), T("L0_attn_Wk")
    arrays["pack0"] = np.concatenate([wq, wq[:, perm], wk, wk[:, perm], T("L0_attn_Wv")], axis=1)
    ctx = v["ctx_1024"].transpose(2, 0, 1).reshape(D, B * C)
    arrays["pack1"] = np.concatenate([T("L0_xattn_Wq"), T("L0_xattn_Wk"), T("L0_xattn_Wv"), ctx,
                                      T("L0_ffn_gate_weight")], axis=1)

    def twice(wt):
        return np.repeat(wt.reshape(D, H1, 1, DH), 2, axis=2).reshape(D, 2 * H1 * DH)

    arrays["pack2"] = np.concatenate([T("L1_attn_w_q"), np.tile(T("L1_attn_w_k"), (1, H)), np.tile(T("L1_attn_w_v"), (1, H)),
                                      v["L1_ffn_gate_w"], twice(v["L1_xattn_Wq"]), twice(v["L1_xattn_Wk"]),
                                      v["L1_xattn_Wv"]], axis=1)
    arrays["wo"] = np.stack([T("L0_attn_Wo"), T("L0_xattn_Wo"), T("L1_attn_w_out")], axis=1)
    arrays["ywo"] = v["L1_xattn_Wo"].reshape(HP, P, D).transpose(1, 0, 2)
    arrays["bo"] = np.stack([v["L0_xattn_bo"], v["L1_xattn_bo"]])
    arrays["smscale"] = v["L1_attn_softmax_scale"]
    arrays["gbias"] = v["L1_ffn_gate_b"]
    w1 = [np.concatenate([v["L0_ffn_Ws1"][None], v["L0_ffn_W1"]]), np.concatenate([v["L1_ffn_sh_w1"][None], v["L1_ffn_ew1"]])]
    w2 = [np.concatenate([v["L0_ffn_Ws2"][None], v["L0_ffn_W2"]]), np.concatenate([v["L1_ffn_sh_w2"][None], v["L1_ffn_ew2"]])]
    b1 = [np.concatenate([v["L0_ffn_bs1"][None], v["L0_ffn_b1"]]), np.concatenate([v["L1_ffn_sh_b1"][None], v["L1_ffn_eb1"]])]
    b2 = [np.concatenate([v["L0_ffn_bs2"][None], v["L0_ffn_b2"]]), np.concatenate([v["L1_ffn_sh_b2"][None], v["L1_ffn_eb2"]])]
    arrays["w1"] = np.stack(w1)
    arrays["w2"] = np.stack(w2).reshape(2, E + 1, FT, P, D).transpose(0, 1, 3, 2, 4)
    arrays["b1"] = np.stack(b1).reshape(2, E + 1, FT, P).transpose(3, 0, 1, 2)
    arrays["b2"] = np.stack(b2)

    nc = _bacc.Bacc("TRN2", target_bir_lowering=False, num_devices=1)
    ins, aps = {}, {}
    for name, arr in arrays.items():
        arr = np.ascontiguousarray(arr)
        ins[f"in_{name}"] = arr
        aps[name] = nc.dram_tensor(f"in_{name}", arr.shape, _mybir.dt.from_np(arr.dtype), kind="ExternalInput").ap()
    aps["out"] = nc.dram_tensor("out_x", (B, S, D), F32, kind="ExternalOutput").ap()
    build(nc, aps)
    r = _run(nc, [ins], core_ids=[0])
    return r.results[0]["out_x"]
```
